# Optimizing a Trainium2 kernel written in Bass

```python
import numpy as np
import jax
import jax.numpy as jnp

def _softmax(x, axis=-1):
    return jax.nn.softmax(x, axis=axis)

def _gelu(x):
    return jax.nn.gelu(x, approximate=True)

def _silu(x):
    return jax.nn.silu(x)

def _sigmoid(x):
    return jax.nn.sigmoid(x)

def _layernorm(x, axis=-1, eps=1e-05):
    m = jnp.mean(x, axis=axis, keepdims=True)
    v = jnp.var(x, axis=axis, keepdims=True)
    return (x - m) / jnp.sqrt(v + eps)

def _scatter_add(tgt, idx, src, axis=0):
    return tgt.at[idx].add(src)

def _segment_sum(src, seg, n):
    return jax.ops.segment_sum(src, seg, n)
kernel_name = 'mk_decoder_postln_d2_seqx_r8_53fdbd'

def setup_inputs(seed: int=0):
    np.random.seed(seed)
    _w = jnp.asarray

    def _rec_inputs():
        import jax
        import jax.numpy as jnp
        _rk = jax.random.key(seed)
        x = -7.109e-05 + 0.9999 * jax.random.normal(jax.random.fold_in(_rk, 1), (4, 256, 256), jnp.float32)
        _lenS = 256 - jax.random.randint(jax.random.fold_in(_rk, 7), (4,), 0, max(1, 256 // 4) + 1, jnp.int32)
        _lenS2 = 256 - jax.random.randint(jax.random.fold_in(_rk, 8), (4,), 0, max(1, 256 // 4) + 1, jnp.int32)
        _ctx_512P = jax.random.normal(jax.random.fold_in(_rk, 11), (4, 16, 64), jnp.float32)
        _ctx_512c = jax.random.dirichlet(jax.random.fold_in(_rk, 511), 0.3 * jnp.ones((16,), jnp.float32), (4, 256))
        _ctx_512t = jnp.einsum('bsk,bkd->bsd', _ctx_512c, _ctx_512P)
        _ctx_512t = _ctx_512t * jax.lax.rsqrt(jnp.mean(jnp.square(_ctx_512t)) + 1e-12) * 0.953939
        ctx_512 = 2.81802e-05 + 1.00001 * (_ctx_512t + 0.3 * jax.random.normal(jax.random.fold_in(_rk, 611), (4, 256, 64), jnp.float32))
        return (x, ctx_512)
    x, ctx_512 = _rec_inputs()

    def _L0_attn_setup():
        import jax, jax.numpy as jnp
        import numpy as np
        N_HEADS = 16
        N_KV_HEADS = 4
        HEAD_DIM = 128
        ROPE_THETA = 10000.0
        WINDOW = 128
        SOFTCAP = 50.0
        B, T, C = (2, 256, 256)
        G = N_HEADS // N_KV_HEADS

        def _sine_table(features, length, max_timescale):
            fraction = jnp.arange(0, features, 2, dtype=jnp.float32) / features
            inv_timescale = 1.0 / max_timescale ** fraction
            sinusoid = jnp.einsum('i,j->ij', jnp.arange(length), inv_timescale, precision=jax.lax.Precision.HIGHEST)
            sinusoid = jnp.concatenate([sinusoid, sinusoid], axis=-1)
            return (jnp.sin(sinusoid), jnp.cos(sinusoid))

        def _rotate_half(x):
            x1, x2 = jnp.split(x, 2, axis=-1)
            return jnp.concatenate([-x2, x1], axis=-1)

        def _attention(x, q_kernel, k_kernel, v_kernel, out_kernel):
            Bs, Ts, Cs = x.shape
            K, H, Gn = (N_KV_HEADS, HEAD_DIM, G)
            q = jnp.dot(x, q_kernel).reshape(Bs, Ts, K, Gn, H)
            k = jnp.dot(x, k_kernel).reshape(Bs, Ts, K, H)
            v = jnp.dot(x, v_kernel).reshape(Bs, Ts, K, H)
            sin, cos = _sine_table(H, Ts, ROPE_THETA)
            qcos = cos[None, :, None, None, :]
            qsin = sin[None, :, None, None, :]
            kcos = cos[None, :, None, :]
            ksin = sin[None, :, None, :]
            q = (q * qcos + _rotate_half(q) * qsin).astype(q.dtype)
            k = (k * kcos + _rotate_half(k) * ksin).astype(k.dtype)
            pos = jnp.arange(Ts)
            mask = (pos[:, None] >= pos[None, :]) & (pos[:, None] <= pos[None, :] + WINDOW)
            mask = mask[None, None, :, :]
            neg = jnp.asarray(-0.7 * jnp.finfo(jnp.float32).max, dtype=jnp.float32)
            scale = jnp.asarray(H ** (-0.5), dtype=q.dtype)
            encoded = []
            for i in range(Gn):
                qi = q[:, :, :, i] * scale
                logits = jnp.einsum('BTKH,BSKH->BKTS', qi, k)
                logits = jnp.tanh(logits / SOFTCAP) * SOFTCAP
                logits = jnp.where(mask, logits, neg)
                probs = jax.nn.softmax(logits.astype(jnp.float32), axis=-1).astype(logits.dtype)
                encoded.append(jnp.einsum('BKTS,BSKH->BTKH', probs, v))
            encoded = jnp.stack(encoded, axis=3)
            encoded = encoded.reshape(Bs, Ts, N_HEADS * H)
            return jnp.dot(encoded, out_kernel)
        key = jax.random.key(seed)
        kx, kq, kk, kv, ko = jax.random.split(key, 5)
        x = jax.random.normal(kx, (B, T, C), dtype=jnp.float32)
        init = lambda k, shape: 0.02 * jax.random.normal(k, shape, dtype=jnp.float32)
        q_kernel = init(kq, (C, N_HEADS * HEAD_DIM))
        k_kernel = init(kk, (C, N_KV_HEADS * HEAD_DIM))
        v_kernel = init(kv, (C, N_KV_HEADS * HEAD_DIM))
        out_kernel = init(ko, (N_HEADS * HEAD_DIM, C))
        return {'x': x, 'q_kernel': q_kernel, 'k_kernel': k_kernel, 'v_kernel': v_kernel, 'out_kernel': out_kernel}
    _L0_attn_all = _L0_attn_setup()
    _L0_attn_in = {k: v for k, v in _L0_attn_all.items() if k in ('q_kernel', 'k_kernel', 'v_kernel', 'out_kernel')}
    del _L0_attn_all

    def _L0_xattn_setup():
        import jax, jax.numpy as jnp
        import numpy as np
        EPS = 1e-06
        IMAGE_DIMS = 256
        key = jax.random.key(seed)
        k1, k2, k3 = jax.random.split(key, 3)
        B, I, J, D = (16, 256, 256, 64)
        p = jax.random.normal(k1, (B, I, J), dtype=jnp.float32)
        k_v = jax.random.normal(k2, (B, J, D), dtype=jnp.float32)
        W_k = jax.random.normal(k3, (D, D), dtype=jnp.float32) * (1.0 / np.sqrt(D))
        b_k = jnp.zeros((D,), dtype=jnp.float32)
        ln_gamma = jnp.ones((J,), dtype=jnp.float32)
        ln_beta = jnp.zeros((J,), dtype=jnp.float32)
        return {'p': p, 'k_v': k_v, 'W_k': W_k, 'b_k': b_k, 'ln_gamma': ln_gamma, 'ln_beta': ln_beta}
    _L0_xattn_all = _L0_xattn_setup()
    _L0_xattn_in = {k: v for k, v in _L0_xattn_all.items() if k in ('W_k', 'b_k', 'ln_gamma', 'ln_beta')}
    del _L0_xattn_all

    def _L0_ffn_setup():
        import jax, jax.numpy as jnp
        import numpy as np
        E, K, H, F = (64, 6, 256, 96)
        G, KG = (8, 4)
        SHARED_F = 96
        SCALE = 2.5
        T = 2 * 128
        CAP = 2 * (T * K // E)

        def _grouped_topk(logits, bias):
            scores = jax.nn.sigmoid(logits.astype(jnp.float32))
            scores_b = scores + bias[None, :]
            gs = scores_b.reshape(-1, G, E // G)
            group_scores = jnp.sum(jax.lax.top_k(gs, 2)[0], axis=-1)
            gidx = jax.lax.top_k(group_scores, KG)[1]
            rows = jnp.arange(group_scores.shape[0])[:, None]
            group_mask = jnp.zeros_like(group_scores).at[rows, gidx].set(1.0)
            score_mask = jnp.repeat(group_mask, E // G, axis=-1) > 0
            tmp = jnp.where(score_mask, scores_b, -jnp.inf)
            topk_ids = jax.lax.top_k(tmp, K)[1]
            topk_w = jnp.take_along_axis(scores, topk_ids, axis=-1)
            topk_w = topk_w / jnp.sum(topk_w, axis=-1, keepdims=True)
            return (topk_w * SCALE, topk_ids)

        def _routed_moe(x, topk_w, topk_ids, w_gate, w_up, w_down):
            Tn = x.shape[0]
            flat_e = topk_ids.reshape(-1)
            order = jnp.argsort(flat_e)
            se = flat_e[order]
            pos = jnp.arange(Tn * K) - jnp.searchsorted(se, se, side='left')
            tok = order // K
            valid = pos < CAP
            slot = jnp.where(valid, pos, CAP)
            buf = jnp.zeros((E, CAP + 1, H), x.dtype).at[se, slot].set(x[tok])[:, :CAP]
            h = jax.nn.silu(jnp.einsum('ech,ehf->ecf', buf, w_gate)) * jnp.einsum('ech,ehf->ecf', buf, w_up)
            out = jnp.einsum('ecf,efh->ech', h, w_down)
            gathered = out[se, jnp.minimum(pos, CAP - 1)] * valid.astype(x.dtype)[:, None]
            w = topk_w.reshape(-1)[order].astype(x.dtype)[:, None]
            return jax.ops.segment_sum(gathered * w, tok, num_segments=Tn)
        key = jax.random.key(seed)
        ks = jax.random.split(key, 9)
        s = 0.02
        return dict(hidden_states=jax.random.normal(ks[0], (2, 128, H), jnp.float32), gate_w=jax.random.normal(ks[1], (H, E), jnp.float32) * s, bias=jax.random.normal(ks[2], (E,), jnp.float32) * s, w_gate=jax.random.normal(ks[3], (E, H, F), jnp.float32) * s, w_up=jax.random.normal(ks[4], (E, H, F), jnp.float32) * s, w_down=jax.random.normal(ks[5], (E, F, H), jnp.float32) * s, ws_gate=jax.random.normal(ks[6], (H, SHARED_F), jnp.float32) * s, ws_up=jax.random.normal(ks[7], (H, SHARED_F), jnp.float32) * s, ws_down=jax.random.normal(ks[8], (SHARED_F, H), jnp.float32) * s)
    _L0_ffn_all = _L0_ffn_setup()
    _L0_ffn_in = {k: v for k, v in _L0_ffn_all.items() if k in ('gate_w', 'bias', 'w_gate', 'w_up', 'w_down', 'ws_gate', 'ws_up', 'ws_down')}
    del _L0_ffn_all

    def _L1_attn_setup():
        import jax, jax.numpy as jnp
        import numpy as np
        EPS_L2 = 1e-06
        NORM_EPS = 1e-05

        def short_conv(x, w):
            K = w.shape[1]
            T = x.shape[1]
            xp = jnp.pad(x, ((0, 0), (K - 1, 0), (0, 0)))
            y = xp[:, 0:T, :] * w[:, 0]
            for i in range(1, K):
                y = y + xp[:, i:i + T, :] * w[:, i]
            return jax.nn.silu(y)

        def l2norm(x):
            return x * jax.lax.rsqrt(jnp.sum(x * x, axis=-1, keepdims=True) + EPS_L2)

        def gated_delta_rule(q, k, v, g, beta):

            def per_head(qh, kh, vh, gh, bh):

                def step(S, inp):
                    qt, kt, vt, gt, bt = inp
                    S = S * jnp.exp(gt)
                    delta = (vt - kt @ S) * bt
                    S = S + kt[:, None] * delta[None, :]
                    return (S, qt @ S)
                S0 = jnp.zeros((qh.shape[-1], vh.shape[-1]), jnp.float32)
                _, o = jax.lax.scan(jax.checkpoint(step), S0, (qh, kh, vh, gh, bh))
                return o
            fh = jax.vmap(per_head, in_axes=(1, 1, 1, 1, 1), out_axes=1)
            fb = jax.vmap(fh, in_axes=0, out_axes=0)
            return fb(q, k, v, g, beta)
        key = jax.random.key(seed)
        ks = jax.random.split(key, 16)
        B, T, HID = (1, 128, 256)
        H, DK, DV = (12, 128, 32)
        KDIM, VDIM, KS = (H * DK, H * DV, 4)
        s = 0.02
        hidden_states = jax.random.normal(ks[0], (B, T, HID), jnp.float32)
        Wq = jax.random.normal(ks[1], (HID, KDIM), jnp.float32) * s
        Wk = jax.random.normal(ks[2], (HID, KDIM), jnp.float32) * s
        Wv = jax.random.normal(ks[3], (HID, VDIM), jnp.float32) * s
        Wb = jax.random.normal(ks[4], (HID, H), jnp.float32) * s
        Wa = jax.random.normal(ks[5], (HID, H), jnp.float32) * s
        Wg = jax.random.normal(ks[6], (HID, VDIM), jnp.float32) * s
        Wo = jax.random.normal(ks[7], (VDIM, HID), jnp.float32) * s
        conv_wq = jax.random.normal(ks[8], (KDIM, KS), jnp.float32) * 0.1
        conv_wk = jax.random.normal(ks[9], (KDIM, KS), jnp.float32) * 0.1
        conv_wv = jax.random.normal(ks[10], (VDIM, KS), jnp.float32) * 0.1
        A_log = jnp.log(jax.random.uniform(ks[11], (H,), jnp.float32, 0.5, 8.0))
        dt = jnp.exp(jax.random.uniform(ks[12], (H,), jnp.float32) * (np.log(0.1) - np.log(0.001)) + np.log(0.001))
        dt = jnp.clip(dt, 0.0001, None)
        dt_bias = dt + jnp.log(-jnp.expm1(-dt))
        norm_w = jnp.ones((DV,), jnp.float32)
        return {'hidden_states': hidden_states, 'Wq': Wq, 'Wk': Wk, 'Wv': Wv, 'Wb': Wb, 'Wa': Wa, 'Wg': Wg, 'Wo': Wo, 'conv_wq': conv_wq, 'conv_wk': conv_wk, 'conv_wv': conv_wv, 'A_log': A_log, 'dt_bias': dt_bias, 'norm_w': norm_w}
    _L1_attn_all = _L1_attn_setup()
    _L1_attn_in = {k: v for k, v in _L1_attn_all.items() if k in ('Wq', 'Wk', 'Wv', 'Wb', 'Wa', 'Wg', 'Wo', 'conv_wq', 'conv_wk', 'conv_wv', 'A_log', 'dt_bias', 'norm_w')}
    del _L1_attn_all

    def _L1_xattn_setup():
        import jax, jax.numpy as jnp
        import numpy as np
        B, S, L = (2, 128, 128)
        DIM_Q, H, K, D_C, D_CQ, R = (256, 16, 128, 64, 192, 64)

        def _rope_tables(length, dim):
            inv = 1.0 / 10000.0 ** (jnp.arange(0, dim, 2, dtype=jnp.float32) / dim)
            f = jnp.arange(length, dtype=jnp.float32)[:, None] * inv[None, :]
            sin = jnp.repeat(jnp.sin(f), 2, axis=-1)
            cos = jnp.repeat(jnp.cos(f), 2, axis=-1)
            return (sin, cos)

        def _rotate_half(x):
            half = x.shape[-1] // 2
            return jnp.concatenate([-x[..., half:], x[..., :half]], axis=-1)

        def _apply_rope(x, sin, cos):
            return x * cos + _rotate_half(x) * sin
        key = jax.random.key(seed)
        ks = jax.random.split(key, 8)
        return {'hidden_q': jax.random.normal(ks[0], (B, S, DIM_Q), jnp.float32), 'kv_c': jax.random.normal(ks[1], (B, L, D_C), jnp.float32), 'Wq': jax.random.normal(ks[2], (H * K, DIM_Q), jnp.float32) / np.sqrt(DIM_Q).astype(np.float32), 'w_kc_q': jax.random.normal(ks[3], (H, K, D_CQ), jnp.float32) / np.sqrt(K).astype(np.float32), 'w_kc_kv': jax.random.normal(ks[4], (H, K, D_C), jnp.float32) / np.sqrt(K).astype(np.float32), 'W_qr': jax.random.normal(ks[5], (H, D_CQ, R), jnp.float32) / np.float32(np.sqrt(D_CQ) * np.sqrt(R)), 'W_kr': jax.random.normal(ks[6], (H, D_C, R), jnp.float32) / np.sqrt(D_C).astype(np.float32), 'Wo': jax.random.normal(ks[7], (DIM_Q, H * K), jnp.float32) / np.sqrt(H * K).astype(np.float32)}
    _L1_xattn_all = _L1_xattn_setup()
    _L1_xattn_in = {k: v for k, v in _L1_xattn_all.items() if k in ('Wq', 'w_kc_q', 'w_kc_kv', 'W_qr', 'W_kr', 'Wo')}
    del _L1_xattn_all

    def _L1_ffn_setup():
        import jax, jax.numpy as jnp
        import numpy as np
        MIN_EXPERTS = 2
        NEG_INF = -1000000000.0

        def _l2norm(x, axis):
            return x / jnp.maximum(jnp.linalg.norm(x, axis=axis, keepdims=True), 1e-12)

        def _ste(x):
            return x + jax.lax.stop_gradient((x > 0).astype(x.dtype) - x)

        def _forward(hidden_states, sim_matrix, gates, q_proj, k_proj, v_proj, o_proj):
            B, T, C = hidden_states.shape
            E = gates.shape[0]
            H = q_proj.shape[-1]
            x = hidden_states.reshape(B * T, C)
            logits = _l2norm(x, -1) @ _l2norm(sim_matrix, 0) - jax.nn.sigmoid(gates)
            gated = jax.nn.relu(logits)
            mask = _ste(gated)
            inactive = jnp.sum(mask, axis=1) == 0
            fb_idx = jax.lax.top_k(logits, MIN_EXPERTS)[1]
            fb_mask = jnp.max(jax.nn.one_hot(fb_idx, E, dtype=mask.dtype), axis=1)
            mask = jnp.where(inactive[:, None] & (fb_mask > 0), jnp.ones_like(mask), mask)
            masked_logits = jnp.where(mask > 0, gated, jnp.full_like(gated, NEG_INF))
            probs = jax.nn.softmax(masked_logits, axis=-1)
            w = probs * (mask > 0)

            def mix(proj):
                pe = jnp.einsum('nc,ech->neh', x, proj)
                return jnp.einsum('ne,neh->nh', w, pe).reshape(B, T, H)
            q, k, v = (mix(q_proj), mix(k_proj), mix(v_proj))
            scale = 1.0 / jnp.sqrt(jnp.asarray(H, dtype=q.dtype))
            scores = jnp.einsum('bqh,bkh->bqk', q, k) * scale
            causal = jnp.tril(jnp.ones((T, T), dtype=bool))
            scores = jnp.where(causal[None], scores, jnp.full_like(scores, NEG_INF))
            attn = jax.nn.softmax(scores, axis=-1)
            ao = jnp.einsum('bqk,bkh->bqh', attn, v).reshape(B * T, H)
            wa = jnp.einsum('ne,nh->enh', w, ao)
            out = jnp.einsum('enh,ehc->nc', wa, o_proj)
            return out.reshape(B, T, C)
        key = jax.random.key(seed)
        ks = jax.random.split(key, 6)
        B, T, C, H, E = (4, 256, 256, 128, 16)
        xavier_qkv = float(np.sqrt(2.0 / (C + H)))
        return {'hidden_states': jax.random.normal(ks[0], (B, T, C), dtype=jnp.float32), 'sim_matrix': jax.random.normal(ks[1], (C, E), dtype=jnp.float32), 'gates': jnp.full((E,), -6.0, dtype=jnp.float32), 'q_proj': jax.random.normal(ks[2], (E, C, H), dtype=jnp.float32) * xavier_qkv, 'k_proj': jax.random.normal(ks[3], (E, C, H), dtype=jnp.float32) * xavier_qkv, 'v_proj': jax.random.normal(ks[4], (E, C, H), dtype=jnp.float32) * xavier_qkv, 'o_proj': jax.random.normal(ks[5], (E, H, C), dtype=jnp.float32) * xavier_qkv}
    _L1_ffn_all = _L1_ffn_setup()
    _L1_ffn_in = {k: v for k, v in _L1_ffn_all.items() if k in ('sim_matrix', 'gates', 'q_proj', 'k_proj', 'v_proj', 'o_proj')}
    del _L1_ffn_all
    return {'x': x, 'ctx_512': ctx_512, 'L0_attn_q_kernel': _L0_attn_in['q_kernel'], 'L0_attn_k_kernel': _L0_attn_in['k_kernel'], 'L0_attn_v_kernel': _L0_attn_in['v_kernel'], 'L0_attn_out_kernel': _L0_attn_in['out_kernel'], 'L0_xattn_W_k': _L0_xattn_in['W_k'], 'L0_xattn_b_k': _L0_xattn_in['b_k'], 'L0_xattn_ln_gamma': _L0_xattn_in['ln_gamma'], 'L0_xattn_ln_beta': _L0_xattn_in['ln_beta'], 'L0_ffn_gate_w': _L0_ffn_in['gate_w'], 'L0_ffn_bias': _L0_ffn_in['bias'], 'L0_ffn_w_gate': _L0_ffn_in['w_gate'], 'L0_ffn_w_up': _L0_ffn_in['w_up'], 'L0_ffn_w_down': _L0_ffn_in['w_down'], 'L0_ffn_ws_gate': _L0_ffn_in['ws_gate'], 'L0_ffn_ws_up': _L0_ffn_in['ws_up'], 'L0_ffn_ws_down': _L0_ffn_in['ws_down'], 'L1_attn_Wq': _L1_attn_in['Wq'], 'L1_attn_Wk': _L1_attn_in['Wk'], 'L1_attn_Wv': _L1_attn_in['Wv'], 'L1_attn_Wb': _L1_attn_in['Wb'], 'L1_attn_Wa': _L1_attn_in['Wa'], 'L1_attn_Wg': _L1_attn_in['Wg'], 'L1_attn_Wo': _L1_attn_in['Wo'], 'L1_attn_conv_wq': _L1_attn_in['conv_wq'], 'L1_attn_conv_wk': _L1_attn_in['conv_wk'], 'L1_attn_conv_wv': _L1_attn_in['conv_wv'], 'L1_attn_A_log': _L1_attn_in['A_log'], 'L1_attn_dt_bias': _L1_attn_in['dt_bias'], 'L1_attn_norm_w': _L1_attn_in['norm_w'], 'L1_xattn_Wq': _L1_xattn_in['Wq'], 'L1_xattn_w_kc_q': _L1_xattn_in['w_kc_q'], 'L1_xattn_w_kc_kv': _L1_xattn_in['w_kc_kv'], 'L1_xattn_W_qr': _L1_xattn_in['W_qr'], 'L1_xattn_W_kr': _L1_xattn_in['W_kr'], 'L1_xattn_Wo': _L1_xattn_in['Wo'], 'L1_ffn_sim_matrix': _L1_ffn_in['sim_matrix'], 'L1_ffn_gates': _L1_ffn_in['gates'], 'L1_ffn_q_proj': _L1_ffn_in['q_proj'], 'L1_ffn_k_proj': _L1_ffn_in['k_proj'], 'L1_ffn_v_proj': _L1_ffn_in['v_proj'], 'L1_ffn_o_proj': _L1_ffn_in['o_proj']}

def reference(x, ctx_512, L0_attn_q_kernel, L0_attn_k_kernel, L0_attn_v_kernel, L0_attn_out_kernel, L0_xattn_W_k, L0_xattn_b_k, L0_xattn_ln_gamma, L0_xattn_ln_beta, L0_ffn_gate_w, L0_ffn_bias, L0_ffn_w_gate, L0_ffn_w_up, L0_ffn_w_down, L0_ffn_ws_gate, L0_ffn_ws_up, L0_ffn_ws_down, L1_attn_Wq, L1_attn_Wk, L1_attn_Wv, L1_attn_Wb, L1_attn_Wa, L1_attn_Wg, L1_attn_Wo, L1_attn_conv_wq, L1_attn_conv_wk, L1_attn_conv_wv, L1_attn_A_log, L1_attn_dt_bias, L1_attn_norm_w, L1_xattn_Wq, L1_xattn_w_kc_q, L1_xattn_w_kc_kv, L1_xattn_W_qr, L1_xattn_W_kr, L1_xattn_Wo, L1_ffn_sim_matrix, L1_ffn_gates, L1_ffn_q_proj, L1_ffn_k_proj, L1_ffn_v_proj, L1_ffn_o_proj):
    import jax
    import jax.numpy as jnp

    def _L0_attn_ref(x, q_kernel, k_kernel, v_kernel, out_kernel):
        import jax, jax.numpy as jnp
        import numpy as np
        N_HEADS = 16
        N_KV_HEADS = 4
        HEAD_DIM = 128
        ROPE_THETA = 10000.0
        WINDOW = 128
        SOFTCAP = 50.0
        B, T, C = (2, 256, 256)
        G = N_HEADS // N_KV_HEADS

        def _sine_table(features, length, max_timescale):
            fraction = jnp.arange(0, features, 2, dtype=jnp.float32) / features
            inv_timescale = 1.0 / max_timescale ** fraction
            sinusoid = jnp.einsum('i,j->ij', jnp.arange(length), inv_timescale, precision=jax.lax.Precision.HIGHEST)
            sinusoid = jnp.concatenate([sinusoid, sinusoid], axis=-1)
            return (jnp.sin(sinusoid), jnp.cos(sinusoid))

        def _rotate_half(x):
            x1, x2 = jnp.split(x, 2, axis=-1)
            return jnp.concatenate([-x2, x1], axis=-1)

        def _attention(x, q_kernel, k_kernel, v_kernel, out_kernel):
            Bs, Ts, Cs = x.shape
            K, H, Gn = (N_KV_HEADS, HEAD_DIM, G)
            q = jnp.dot(x, q_kernel).reshape(Bs, Ts, K, Gn, H)
            k = jnp.dot(x, k_kernel).reshape(Bs, Ts, K, H)
            v = jnp.dot(x, v_kernel).reshape(Bs, Ts, K, H)
            sin, cos = _sine_table(H, Ts, ROPE_THETA)
            qcos = cos[None, :, None, None, :]
            qsin = sin[None, :, None, None, :]
            kcos = cos[None, :, None, :]
            ksin = sin[None, :, None, :]
            q = (q * qcos + _rotate_half(q) * qsin).astype(q.dtype)
            k = (k * kcos + _rotate_half(k) * ksin).astype(k.dtype)
            pos = jnp.arange(Ts)
            mask = (pos[:, None] >= pos[None, :]) & (pos[:, None] <= pos[None, :] + WINDOW)
            mask = mask[None, None, :, :]
            neg = jnp.asarray(-0.7 * jnp.finfo(jnp.float32).max, dtype=jnp.float32)
            scale = jnp.asarray(H ** (-0.5), dtype=q.dtype)
            encoded = []
            for i in range(Gn):
                qi = q[:, :, :, i] * scale
                logits = jnp.einsum('BTKH,BSKH->BKTS', qi, k)
                logits = jnp.tanh(logits / SOFTCAP) * SOFTCAP
                logits = jnp.where(mask, logits, neg)
                probs = jax.nn.softmax(logits.astype(jnp.float32), axis=-1).astype(logits.dtype)
                encoded.append(jnp.einsum('BKTS,BSKH->BTKH', probs, v))
            encoded = jnp.stack(encoded, axis=3)
            encoded = encoded.reshape(Bs, Ts, N_HEADS * H)
            return jnp.dot(encoded, out_kernel)
        return _attention(x, q_kernel, k_kernel, v_kernel, out_kernel)

    def _L0_xattn_ref(p, k_v, W_k, b_k, ln_gamma, ln_beta):
        import jax, jax.numpy as jnp
        import numpy as np
        EPS = 1e-06
        IMAGE_DIMS = 256
        kv = k_v @ W_k.T + b_k
        out = jnp.einsum('bij,bjd->bid', p, kv)
        scale = IMAGE_DIMS ** (-0.5)
        sim = jnp.einsum('bid,bjd->bij', out, kv) * scale
        mu = jnp.mean(sim, axis=-1, keepdims=True)
        var = jnp.var(sim, axis=-1, keepdims=True)
        sim = (sim - mu) * jax.lax.rsqrt(var + EPS) * ln_gamma + ln_beta
        attn = jax.nn.softmax(sim, axis=-1)
        return attn

    def _L0_ffn_ref(hidden_states, gate_w, bias, w_gate, w_up, w_down, ws_gate, ws_up, ws_down):
        import jax, jax.numpy as jnp
        import numpy as np
        E, K, H, F = (64, 6, 256, 96)
        G, KG = (8, 4)
        SHARED_F = 96
        SCALE = 2.5
        T = 2 * 128
        CAP = 2 * (T * K // E)

        def _grouped_topk(logits, bias):
            scores = jax.nn.sigmoid(logits.astype(jnp.float32))
            scores_b = scores + bias[None, :]
            gs = scores_b.reshape(-1, G, E // G)
            group_scores = jnp.sum(jax.lax.top_k(gs, 2)[0], axis=-1)
            gidx = jax.lax.top_k(group_scores, KG)[1]
            rows = jnp.arange(group_scores.shape[0])[:, None]
            group_mask = jnp.zeros_like(group_scores).at[rows, gidx].set(1.0)
            score_mask = jnp.repeat(group_mask, E // G, axis=-1) > 0
            tmp = jnp.where(score_mask, scores_b, -jnp.inf)
            topk_ids = jax.lax.top_k(tmp, K)[1]
            topk_w = jnp.take_along_axis(scores, topk_ids, axis=-1)
            topk_w = topk_w / jnp.sum(topk_w, axis=-1, keepdims=True)
            return (topk_w * SCALE, topk_ids)

        def _routed_moe(x, topk_w, topk_ids, w_gate, w_up, w_down):
            Tn = x.shape[0]
            flat_e = topk_ids.reshape(-1)
            order = jnp.argsort(flat_e)
            se = flat_e[order]
            pos = jnp.arange(Tn * K) - jnp.searchsorted(se, se, side='left')
            tok = order // K
            valid = pos < CAP
            slot = jnp.where(valid, pos, CAP)
            buf = jnp.zeros((E, CAP + 1, H), x.dtype).at[se, slot].set(x[tok])[:, :CAP]
            h = jax.nn.silu(jnp.einsum('ech,ehf->ecf', buf, w_gate)) * jnp.einsum('ech,ehf->ecf', buf, w_up)
            out = jnp.einsum('ecf,efh->ech', h, w_down)
            gathered = out[se, jnp.minimum(pos, CAP - 1)] * valid.astype(x.dtype)[:, None]
            w = topk_w.reshape(-1)[order].astype(x.dtype)[:, None]
            return jax.ops.segment_sum(gathered * w, tok, num_segments=Tn)
        orig_shape = hidden_states.shape
        x = hidden_states.reshape(-1, H)
        router_logits = x @ gate_w
        topk_w, topk_ids = _grouped_topk(router_logits, bias)
        y = _routed_moe(x, topk_w, topk_ids, w_gate, w_up, w_down)
        shared = jax.nn.silu(x @ ws_gate) * (x @ ws_up) @ ws_down
        return (y + shared).reshape(orig_shape)

    def _L1_attn_ref(hidden_states, Wq, Wk, Wv, Wb, Wa, Wg, Wo, conv_wq, conv_wk, conv_wv, A_log, dt_bias, norm_w):
        import jax, jax.numpy as jnp
        import numpy as np
        EPS_L2 = 1e-06
        NORM_EPS = 1e-05

        def short_conv(x, w):
            K = w.shape[1]
            T = x.shape[1]
            xp = jnp.pad(x, ((0, 0), (K - 1, 0), (0, 0)))
            y = xp[:, 0:T, :] * w[:, 0]
            for i in range(1, K):
                y = y + xp[:, i:i + T, :] * w[:, i]
            return jax.nn.silu(y)

        def l2norm(x):
            return x * jax.lax.rsqrt(jnp.sum(x * x, axis=-1, keepdims=True) + EPS_L2)

        def gated_delta_rule(q, k, v, g, beta):

            def per_head(qh, kh, vh, gh, bh):

                def step(S, inp):
                    qt, kt, vt, gt, bt = inp
                    S = S * jnp.exp(gt)
                    delta = (vt - kt @ S) * bt
                    S = S + kt[:, None] * delta[None, :]
                    return (S, qt @ S)
                S0 = jnp.zeros((qh.shape[-1], vh.shape[-1]), jnp.float32)
                _, o = jax.lax.scan(jax.checkpoint(step), S0, (qh, kh, vh, gh, bh))
                return o
            fh = jax.vmap(per_head, in_axes=(1, 1, 1, 1, 1), out_axes=1)
            fb = jax.vmap(fh, in_axes=0, out_axes=0)
            return fb(q, k, v, g, beta)
        B, T, _ = hidden_states.shape
        H = A_log.shape[0]
        q = short_conv(hidden_states @ Wq, conv_wq)
        k = short_conv(hidden_states @ Wk, conv_wk)
        v = short_conv(hidden_states @ Wv, conv_wv)
        q = l2norm(q.reshape(B, T, H, -1))
        k = l2norm(k.reshape(B, T, H, -1))
        v = v.reshape(B, T, H, -1)
        beta = jax.nn.sigmoid(hidden_states @ Wb)
        g = -jnp.exp(A_log) * jax.nn.softplus(hidden_states @ Wa + dt_bias)
        o = gated_delta_rule(q, k, v, g, beta)
        gg = (hidden_states @ Wg).reshape(B, T, H, -1)
        o_n = o * jax.lax.rsqrt(jnp.mean(o * o, axis=-1, keepdims=True) + NORM_EPS) * norm_w
        o_n = o_n * jax.nn.silu(gg)
        return o_n.reshape(B, T, -1) @ Wo

    def _L1_xattn_ref(hidden_q, kv_c, Wq, w_kc_q, w_kc_kv, W_qr, W_kr, Wo):
        import jax, jax.numpy as jnp
        import numpy as np
        B, S, L = (2, 128, 128)
        DIM_Q, H, K, D_C, D_CQ, R = (256, 16, 128, 64, 192, 64)

        def _rope_tables(length, dim):
            inv = 1.0 / 10000.0 ** (jnp.arange(0, dim, 2, dtype=jnp.float32) / dim)
            f = jnp.arange(length, dtype=jnp.float32)[:, None] * inv[None, :]
            sin = jnp.repeat(jnp.sin(f), 2, axis=-1)
            cos = jnp.repeat(jnp.cos(f), 2, axis=-1)
            return (sin, cos)

        def _rotate_half(x):
            half = x.shape[-1] // 2
            return jnp.concatenate([-x[..., half:], x[..., :half]], axis=-1)

        def _apply_rope(x, sin, cos):
            return x * cos + _rotate_half(x) * sin
        Bv, Sv, _ = hidden_q.shape
        _, Lv, _ = kv_c.shape
        q_hk = (hidden_q @ Wq.T).reshape(Bv, Sv, H, K)
        q_big = jnp.einsum('bshk,hkq->bshq', q_hk, w_kc_q)
        sin_q, cos_q = _rope_tables(Sv, D_CQ)
        q_big = _apply_rope(q_big, sin_q[None, :, None, :], cos_q[None, :, None, :])
        sin_k, cos_k = _rope_tables(Lv, D_C)
        kv_r = _apply_rope(kv_c, sin_k[None], cos_k[None])
        q_r = jnp.einsum('bshq,hqr->bhsr', q_big, W_qr)
        k_r = jnp.einsum('bld,hdr->bhlr', kv_r, W_kr)
        scores = jnp.einsum('bhsr,bhlr->bhsl', q_r, k_r)
        attn = jax.nn.softmax(scores, axis=-1)
        ctx_c = jnp.einsum('bhsl,bld->bhsd', attn, kv_r)
        ctx_lat = jnp.einsum('bhsd,hkd->bhsk', ctx_c, w_kc_kv)
        ctx = ctx_lat.transpose(0, 2, 1, 3).reshape(Bv, Sv, H * K)
        return ctx @ Wo.T

    def _L1_ffn_ref(hidden_states, sim_matrix, gates, q_proj, k_proj, v_proj, o_proj):
        import jax, jax.numpy as jnp
        import numpy as np
        MIN_EXPERTS = 2
        NEG_INF = -1000000000.0

        def _l2norm(x, axis):
            return x / jnp.maximum(jnp.linalg.norm(x, axis=axis, keepdims=True), 1e-12)

        def _ste(x):
            return x + jax.lax.stop_gradient((x > 0).astype(x.dtype) - x)

        def _forward(hidden_states, sim_matrix, gates, q_proj, k_proj, v_proj, o_proj):
            B, T, C = hidden_states.shape
            E = gates.shape[0]
            H = q_proj.shape[-1]
            x = hidden_states.reshape(B * T, C)
            logits = _l2norm(x, -1) @ _l2norm(sim_matrix, 0) - jax.nn.sigmoid(gates)
            gated = jax.nn.relu(logits)
            mask = _ste(gated)
            inactive = jnp.sum(mask, axis=1) == 0
            fb_idx = jax.lax.top_k(logits, MIN_EXPERTS)[1]
            fb_mask = jnp.max(jax.nn.one_hot(fb_idx, E, dtype=mask.dtype), axis=1)
            mask = jnp.where(inactive[:, None] & (fb_mask > 0), jnp.ones_like(mask), mask)
            masked_logits = jnp.where(mask > 0, gated, jnp.full_like(gated, NEG_INF))
            probs = jax.nn.softmax(masked_logits, axis=-1)
            w = probs * (mask > 0)

            def mix(proj):
                pe = jnp.einsum('nc,ech->neh', x, proj)
                return jnp.einsum('ne,neh->nh', w, pe).reshape(B, T, H)
            q, k, v = (mix(q_proj), mix(k_proj), mix(v_proj))
            scale = 1.0 / jnp.sqrt(jnp.asarray(H, dtype=q.dtype))
            scores = jnp.einsum('bqh,bkh->bqk', q, k) * scale
            causal = jnp.tril(jnp.ones((T, T), dtype=bool))
            scores = jnp.where(causal[None], scores, jnp.full_like(scores, NEG_INF))
            attn = jax.nn.softmax(scores, axis=-1)
            ao = jnp.einsum('bqk,bkh->bqh', attn, v).reshape(B * T, H)
            wa = jnp.einsum('ne,nh->enh', w, ao)
            out = jnp.einsum('enh,ehc->nc', wa, o_proj)
            return out.reshape(B, T, C)
        return _forward(hidden_states, sim_matrix, gates, q_proj, k_proj, v_proj, o_proj)
    x = _layernorm(x + _L0_attn_ref(x, L0_attn_q_kernel, L0_attn_k_kernel, L0_attn_v_kernel, L0_attn_out_kernel), axis=-1)
    x = _layernorm(x + _L0_xattn_ref(x, ctx_512, L0_xattn_W_k, L0_xattn_b_k, L0_xattn_ln_gamma, L0_xattn_ln_beta), axis=-1)
    x = _layernorm(x + _L0_ffn_ref(x, L0_ffn_gate_w, L0_ffn_bias, L0_ffn_w_gate, L0_ffn_w_up, L0_ffn_w_down, L0_ffn_ws_gate, L0_ffn_ws_up, L0_ffn_ws_down), axis=-1)
    x = _layernorm(x + _L1_attn_ref(x, L1_attn_Wq, L1_attn_Wk, L1_attn_Wv, L1_attn_Wb, L1_attn_Wa, L1_attn_Wg, L1_attn_Wo, L1_attn_conv_wq, L1_attn_conv_wk, L1_attn_conv_wv, L1_attn_A_log, L1_attn_dt_bias, L1_attn_norm_w), axis=-1)
    x = _layernorm(x + _L1_xattn_ref(x, ctx_512, L1_xattn_Wq, L1_xattn_w_kc_q, L1_xattn_w_kc_kv, L1_xattn_W_qr, L1_xattn_W_kr, L1_xattn_Wo), axis=-1)
    x = _layernorm(x + _L1_ffn_ref(x, L1_ffn_sim_matrix, L1_ffn_gates, L1_ffn_q_proj, L1_ffn_k_proj, L1_ffn_v_proj, L1_ffn_o_proj), axis=-1)
    return x

_drawn_inputs = setup_inputs


def setup_inputs(seed=0):
    import zlib

    import numpy as np

    out = dict(_drawn_inputs(seed))
    spreads = {'L0_xattn_b_k': (0.0, 0.8),
     'L0_xattn_ln_gamma': (1.0, 0.6),
     'L0_xattn_ln_beta': (0.0, 0.8),
     'L1_attn_norm_w': (1.0, 0.6),
     'L1_ffn_gates': (-6.0, 0.6)}
    factors = {'L0_attn_q_kernel': 8.0,
     'L0_attn_k_kernel': 8.0,
     'L0_xattn_W_k': 8.0,
     'L0_ffn_gate_w': 7.787,
     'L0_ffn_bias': 8.0,
     'L0_ffn_w_gate': 5.506,
     'L0_ffn_w_up': 7.399,
     'L0_ffn_w_down': 7.408,
     'L0_ffn_ws_gate': 5.48,
     'L0_ffn_ws_up': 5.417,
     'L0_ffn_ws_down': 5.416,
     'L1_attn_Wb': 7.19,
     'L1_attn_Wa': 8.0,
     'L1_attn_A_log': 6.066,
     'L1_ffn_q_proj': 8.0,
     'L1_ffn_k_proj': 8.0}
    for name, (base, spread) in spreads.items():
        noise = np.random.default_rng([zlib.crc32(name.encode()), seed]).standard_normal(out[name].shape)
        drawn = base * np.exp(spread * noise) if base else spread * noise
        out[name] = jnp.asarray(drawn.astype(out[name].dtype))
    for name, factor in factors.items():
        out[name] = (out[name] * factor).astype(out[name].dtype)
    return out
```

```python
from contextlib import ExitStack

import numpy as np
import concourse.bass as bass
from concourse import mybir

F32 = mybir.dt.float32
I32 = mybir.dt.int32
U32 = mybir.dt.uint32
ALU = mybir.AluOpType
ACT = mybir.ActivationFunctionType
AX = mybir.AxisListType.X
ds = bass.ds

P = 128
BATCH, SEQ, DIM, CTX = 4, 256, 256, 64
TOKENS = BATCH * SEQ
TILES = TOKENS // P
KC = DIM // P
LN_EPS = 1e-5

A_HEADS, A_KV, A_HD, A_WINDOW, A_CAP = 16, 4, 128, 128, 50.0
A_G = A_HEADS // A_KV
M_E, M_K, M_F, M_GROUPS, M_KG, M_SCALE = 64, 6, 96, 8, 4, 2.5
M_CAP = 2 * (2 * 128 * M_K // M_E)
D_H, D_K, D_V, D_CONV = 12, 128, 32, 4
X_H, X_K, X_CQ, X_R = 16, 128, 192, 64
X_HALF = X_CQ // 2
F_E, F_H = 16, 128


def constants():
    f = np.float32
    col, row = np.arange(P)[None, :], np.arange(P)[:, None]
    parts = {}
    parts["ident"] = (row == col)
    parts["ones"] = np.ones((P, P))
    parts["upto"] = (row <= col)
    parts["after"] = (row > col)
    parts["before"] = (row < col)
    frac = (np.arange(0, A_HD, 2, dtype=f) / f(A_HD)).astype(f)
    inv = (f(1.0) / np.power(f(10000.0), frac)).astype(f)
    ang = (np.arange(SEQ, dtype=f)[None, :] * np.concatenate([inv, inv])[:, None]).astype(f)
    sign = np.where(row < P // 2, 1.0, -1.0)
    parts["a_cos"] = np.tile(np.cos(ang), (1, 2))
    parts["a_sin"] = np.tile(np.sin(ang), (1, 2)) * sign
    q = np.arange(SEQ)[None, :]
    m0 = (q >= row) & (q <= row + A_WINDOW)
    parts["a_mask"] = np.concatenate([m0, (row <= col)], 1)
    for lv in range(7):
        w = 1 << lv
        parts[f"level{lv}"] = (row // (2 * w) == col // (2 * w)) & (row // w < col // w)
    def pair_table(dim):
        iv = (f(1.0) / np.power(f(10000.0), (np.arange(0, dim, 2, dtype=f) / f(dim)))).astype(f)
        a = (np.arange(SEQ, dtype=f)[:, None] * iv[None, :]).astype(f)
        return np.repeat(a, 2, axis=1).T
    big = pair_table(X_CQ)
    for n in range(2):
        half = np.zeros((P, SEQ))
        half[:X_HALF] = big[n * X_HALF:(n + 1) * X_HALF]
        parts[f"x_cos{n}"] = np.tile(np.cos(half), (1, 2))
        parts[f"x_sin{n}"] = np.tile(np.sin(half), (1, 2)) * (-1.0 if n == 0 else 1.0)
    small = pair_table(CTX)
    parts["k_cos"] = np.concatenate([np.cos(small)] * 2, 0)
    swapped = np.concatenate([np.sin(small[CTX // 2:]), -np.sin(small[:CTX // 2])], 0)
    parts["k_sin"] = np.concatenate([swapped] * 2, 0)
    parts["f_mask"] = np.where(np.arange(SEQ)[None, :] - P <= row, 0.0, -1e30)
    at, off = {}, 0
    for k, v in parts.items():
        at[k] = (off, v.shape[1])
        off += v.shape[1]
    return np.concatenate([np.asarray(v, f) for v in parts.values()], 1), at


class Env:

    def __init__(self, nc, ctx, at):
        self.nc, self.at = nc, at
        self.x = ctx.enter_context(nc.sbuf_tensor("x", [P, TILES, DIM], F32))
        self.xT = ctx.enter_context(nc.sbuf_tensor("xT", [P, KC, TOKENS], F32))
        self.const = ctx.enter_context(nc.sbuf_tensor("const", [P, sum(n for _, n in at.values())], F32))

    def c(self, name):
        off, n = self.at[name]
        return self.const[:, off:off + n]


CREDIT = 8


def done(i, per, n):
    return i * per + (CREDIT + n)


def credit(engine, *steps):
    for s in steps:
        engine.sem_inc(s, CREDIT)


def tools(nc, ctx, tag):
    own = []

    def clear():
        nc.clear_and_free_semaphores(own)
        nc.all_engine_barrier()

    ctx.callback(clear)

    def sb(name, shape, dt=F32):
        return ctx.enter_context(nc.sbuf_tensor(f"{tag}_{name}", shape, dt))

    def ps(name, shape, dt=F32):
        return ctx.enter_context(nc.psum_tensor(f"{tag}_{name}", shape, dt))

    def sem(name):
        own.append(nc.alloc_semaphore(f"{tag}_{name}"))
        return own[-1]
    return sb, ps, sem


def load_inputs(nc, env, x_in, const_in):
    with ExitStack() as ctx:
        sb, ps, sem = tools(nc, ctx, "load")
        loaded, turned, copied = sem("loaded"), sem("turned"), sem("copied")
        tp = ps("tp", [P, 4, 512])
        with nc.Block() as block:
            @block.sync
            def _(sp):
                sp.dma_start(env.x[:], x_in.rearrange("b (u p) c -> p (b u) c", p=P)).then_inc(loaded, 16)
                sp.dma_start(env.const[:], const_in).then_inc(loaded, 16)
                sp.wait_ge(loaded, 32)

            @block.tensor
            def _(pe):
                pe.wait_ge(loaded, 32)
                turn_x(pe, env, tp, turned, None)

            @block.vector
            def _(dve):
                for n in range(4):
                    dve.wait_ge(turned, n + 1)
                    dve.tensor_copy(env.xT[:, n // 2, 512 * (n % 2):512 * (n % 2) + 512], tp[:, n, :]).then_inc(copied, 1)


def turn_x(pe, env, tp, turned, tile_ready):
    for kc in range(KC):
        for th in range(2):
            for j in range(4):
                t = 4 * th + j
                if tile_ready is not None and kc == 0:
                    pe.wait_ge(tile_ready, t + 1)
                mm = pe.transpose(tp[:, 2 * kc + th, P * j:P * j + P], env.x[:, t, P * kc:P * kc + P], env.c("ident"))
            mm.then_inc(turned, 1)


def normalize(nc, env, tag, out=None):
    with ExitStack() as ctx:
        sb, ps, sem = tools(nc, ctx, tag)
        stats, mv = sb("stats", [P, TILES, 6]), sb("mv", [P, TILES, 2])
        var, rstd, half = sb("var", [P, TILES]), sb("rstd", [P, TILES]), sb("half", [P, TILES])
        tp = ps("tp", [P, 4, 512])
        stats_ready, mv_ready, var_ready, half_ready = sem("stats_ready"), sem("mv_ready"), sem("var_ready"), sem("half_ready")
        rstd_ready, tile_ready, turned, copied, stored = sem("rstd_ready"), sem("tile_ready"), sem("turned"), sem("copied"), sem("stored")
        with nc.Block() as block:
            @block.vector
            def _(dve):
                for t in range(TILES):
                    dve.bn_stats(stats[:, t, :], env.x[:, t, :]).then_inc(stats_ready, 1)
                for t in range(TILES):
                    dve.wait_ge(stats_ready, t + 1)
                    dve.bn_aggr(mv[:, t, :], stats[:, t, :]).then_inc(mv_ready, 1)
                dve.wait_ge(mv_ready, TILES)
                dve.tensor_scalar(var[:], mv[:, :, 1], LN_EPS, None, ALU.add).then_inc(var_ready, 1)
                dve.wait_ge(rstd_ready, 1)
                for t in range(TILES):
                    dve.tensor_scalar(env.x[:, t, :], env.x[:, t, :], mv[:, t, 0:1], rstd[:, t:t + 1],
                                      ALU.subtract, ALU.mult).then_inc(tile_ready, 1)
                if out is None:
                    for n in range(0, 4, 2):
                        dve.wait_ge(turned, n + 1)
                        dve.tensor_copy(env.xT[:, n // 2, 0:512], tp[:, n, :]).then_inc(copied, 1)

            @block.gpsimd
            def _(pool):
                pool.memset(half[:], -0.5).then_inc(half_ready, 1)
                pool.wait_ge(half_ready, 1)
                pool.wait_ge(var_ready, 1)
                pool.tensor_tensor(rstd[:], var[:], half[:], ALU.pow).then_inc(rstd_ready, 1)

            if out is None:
                @block.tensor
                def _(pe):
                    turn_x(pe, env, tp, turned, tile_ready)

                @block.scalar
                def _(act):
                    for n in range(1, 4, 2):
                        act.wait_ge(turned, n + 1)
                        act.copy(env.xT[:, n // 2, 512:1024], tp[:, n, :]).then_inc(copied, 1)
            else:
                @block.sync
                def _(sp):
                    view = out.rearrange("b (u p) c -> p (b u) c", p=P)
                    for n in range(2):
                        sp.wait_ge(tile_ready, 4 * n + 4)
                        sp.dma_start(view[:, 4 * n:4 * n + 4, :], env.x[:, 4 * n:4 * n + 4, :]).then_inc(stored, 16)
                    sp.wait_ge(stored, 32)


def window_attention(nc, env, wq, wk, wv, wo):
    SCALE = float(A_HD) ** -0.5
    HALF = A_HD // 2
    CH = TOKENS // 512
    QCH = CH * (A_G + 1)
    PJ = QCH + 2
    UN = BATCH * A_G
    with ExitStack() as ctx:
        sb, ps, sem = tools(nc, ctx, "wa")
        wqs, wks, wvs = sb("wq", [P, KC, A_G * A_HD]), sb("wk", [P, KC, A_HD]), sb("wv", [P, KC, A_HD])
        wos = sb("wo", [P, A_G, DIM])
        qkT = sb("qkT", [P, A_G + 1, TOKENS])
        v = sb("v", [P, TILES, A_HD])
        t_cos, t_sin = sb("t_cos", [P, 2, 512]), sb("t_sin", [P, 2, 512])
        capped, probs, masked = sb("capped", [P, 2, 384]), sb("probs", [P, 2, 384]), sb("masked", [P, 3, 384])
        rec, encT = sb("rec", [P, 2, SEQ]), sb("encT", [P, A_G, TOKENS])
        pj, lg, pv, po = ps("pj", [P, 2, 512]), ps("lg", [P, 2, 512]), ps("pv", [P, 2, 512]), ps("po", [P, 2, 512])
        w_loaded, wo_loaded = sem("w_loaded"), sem("wo_loaded")
        projected, logits_done, weighted_done, out_done = sem("projected"), sem("logits_done"), sem("weighted_done"), sem("out_done")
        cos_done, sin_done, v_copied, rec_done, normed, added = sem("cos_done"), sem("sin_done"), sem("v_copied"), sem("rec_done"), sem("normed"), sem("added")
        rotated, mask_done, capped_done, exp_done = sem("rotated"), sem("mask_done"), sem("capped_done"), sem("exp_done")

        with nc.Block() as block:
            @block.sync
            def _(sp):
                with sp.Fori(0, A_KV) as g:
                    sp.wait_ge(projected, done(g, PJ, 0))
                    sp.dma_start(wqs[:], wq.rearrange("(k p) n -> p k n", p=P)[:, :, ds(g * (A_G * A_HD), A_G * A_HD)]).then_inc(w_loaded, 16)
                    sp.dma_start(wks[:], wk.rearrange("(k p) n -> p k n", p=P)[:, :, ds(g * A_HD, A_HD)]).then_inc(w_loaded, 16)
                    sp.dma_start(wvs[:], wv.rearrange("(k p) n -> p k n", p=P)[:, :, ds(g * A_HD, A_HD)]).then_inc(w_loaded, 16)
                    sp.wait_ge(out_done, done(g, TILES, 0))
                    sp.dma_start(wos[:], wo.rearrange("(g i p) n -> p g i n", p=P, i=A_G)[:, ds(g, 1), :, :].rearrange("p g i n -> p (g i) n")).then_inc(wo_loaded, 16)

            @block.tensor
            def _(pe):
                credit(pe, projected, logits_done, weighted_done, out_done)
                with pe.Fori(0, A_KV) as g:
                    pe.wait_ge(w_loaded, g * 48 + 48)

                    def bank_free(n):
                        if n < 2:
                            pe.wait_ge(v_copied, done(g, 2, n - 1))
                        else:
                            pe.wait_ge(sin_done, done(g, 2 * QCH, 2 * (n - 1)))

                    for n in range(QCH):
                        m, c = divmod(n, CH)
                        bank_free(n)
                        for k in range(KC):
                            w = wks[:, k, :] if m == 0 else wqs[:, k, A_HD * (m - 1):A_HD * m]
                            mm = pe.matmul(pj[:, n % 2, :], w, env.xT[:, k, 512 * c:512 * c + 512], start=(k == 0), stop=(k == KC - 1))
                        mm.then_inc(projected, 1)
                    for h in range(2):
                        bank_free(QCH + h)
                        for j in range(4):
                            t = 4 * h + j
                            for k in range(KC):
                                mm = pe.matmul(pj[:, h, P * j:P * j + P], env.xT[:, k, P * t:P * t + P], wvs[:, k, :], start=(k == 0), stop=(k == KC - 1))
                        mm.then_inc(projected, 1)

                    def logits(u):
                        b, i = divmod(u, A_G)
                        pe.wait_ge(capped_done, done(g, UN, u - 1))
                        pe.wait_ge(rotated, done(g, QCH, CH * (i + 1) + b // 2 + 1))
                        o = SEQ * b
                        pe.matmul(lg[:, u % 2, 0:SEQ], qkT[:, 0, o:o + P], qkT[:, 1 + i, o:o + SEQ], start=True, stop=True)
                        pe.matmul(lg[:, u % 2, SEQ:SEQ + P], qkT[:, 0, o + P:o + SEQ], qkT[:, 1 + i, o + P:o + SEQ], start=True, stop=True).then_inc(logits_done, 1)

                    def weighted(u):
                        b, i = divmod(u, A_G)
                        pe.wait_ge(mask_done, done(g, UN, u + 1))
                        pe.wait_ge(normed, done(g, UN, u - 1))
                        if u == 0:
                            pe.wait_ge(v_copied, done(g, 2, 2))
                        for col, w0, w1 in ((0, v[:, 2 * b, :], v[:, 2 * b + 1, :]), (SEQ, env.c("ones"), env.c("ones"))):
                            pe.matmul(pv[:, u % 2, col:col + SEQ], w0, masked[:, u % 3, 0:SEQ], start=True, stop=False)
                            mm = pe.matmul(pv[:, u % 2, col + P:col + SEQ], w1, masked[:, u % 3, SEQ:SEQ + P], start=False, stop=True)
                        mm.then_inc(weighted_done, 1)

                    for u in range(UN + 2):
                        if u < UN:
                            logits(u)
                        if u >= 2:
                            weighted(u - 2)
                    pe.wait_ge(wo_loaded, g * 16 + 16)
                    pe.wait_ge(normed, done(g, UN, UN))
                    for t in range(TILES):
                        pe.wait_ge(added, done(g, TILES, t - 1))
                        for i in range(A_G):
                            mm = pe.matmul(po[:, t % 2, 0:DIM], encT[:, i, P * t:P * t + P], wos[:, i, :], start=(i == 0), stop=(i == A_G - 1))
                        mm.then_inc(out_done, 1)

            @block.vector
            def _(dve):
                credit(dve, cos_done, sin_done, v_copied, rec_done, normed, added)
                with dve.Fori(0, A_KV) as g:
                    for n in range(QCH):
                        dve.wait_ge(projected, done(g, PJ, n + 1))
                        dve.wait_ge(rotated, done(g, QCH, n - 1))
                        dve.tensor_tensor(t_cos[:, n % 2, :], pj[:, n % 2, :], env.c("a_cos"), ALU.mult).then_inc(cos_done, 1)
                        dve.tensor_tensor(t_sin[0:HALF, n % 2, :], pj[HALF:P, n % 2, :], env.c("a_sin")[HALF:P, :], ALU.mult).then_inc(sin_done, 1)
                        dve.tensor_tensor(t_sin[HALF:P, n % 2, :], pj[0:HALF, n % 2, :], env.c("a_sin")[0:HALF, :], ALU.mult).then_inc(sin_done, 1)
                    dve.wait_ge(weighted_done, done(g, UN, 0))
                    for h in range(2):
                        dve.wait_ge(projected, done(g, PJ, QCH + h + 1))
                        dve.tensor_copy(v[:, 4 * h:4 * h + 4, :], pj[:, h, :].rearrange("p (j n) -> p j n", n=P)).then_inc(v_copied, 1)
                    dve.wait_ge(out_done, done(g, TILES, 0))
                    for u in range(UN):
                        b, i = divmod(u, A_G)
                        dve.wait_ge(weighted_done, done(g, UN, u + 1))
                        dve.reciprocal(rec[:, u % 2, :], pv[:, u % 2, SEQ:2 * SEQ]).then_inc(rec_done, 1)
                        dve.wait_ge(rec_done, done(g, UN, u + 1))
                        dve.tensor_tensor(encT[:, i, SEQ * b:SEQ * b + SEQ], pv[:, u % 2, 0:SEQ], rec[:, u % 2, :], ALU.mult).then_inc(normed, 1)
                    for t in range(TILES):
                        dve.wait_ge(out_done, done(g, TILES, t + 1))
                        dve.tensor_tensor(env.x[:, t, :], env.x[:, t, :], po[:, t % 2, 0:DIM], ALU.add).then_inc(added, 1)

            @block.gpsimd
            def _(pool):
                credit(pool, rotated, mask_done)
                with pool.Fori(0, A_KV) as g:
                    pool.wait_ge(logits_done, done(g, UN, 0))
                    for n in range(QCH):
                        m, c = divmod(n, CH)
                        pool.wait_ge(sin_done, done(g, 2 * QCH, 2 * n + 2))
                        pool.tensor_tensor(qkT[:, m, 512 * c:512 * c + 512], t_cos[:, n % 2, :], t_sin[:, n % 2, :], ALU.add).then_inc(rotated, 1)
                    for u in range(UN):
                        pool.wait_ge(exp_done, done(g, UN, u + 1))
                        pool.wait_ge(weighted_done, done(g, UN, u - 2))
                        pool.tensor_tensor(masked[:, u % 3, :], probs[:, u % 2, :], env.c("a_mask"), ALU.mult).then_inc(mask_done, 1)

            @block.scalar
            def _(act):
                credit(act, capped_done, exp_done)
                with act.Fori(0, A_KV) as g:
                    for u in range(UN):
                        act.wait_ge(logits_done, done(g, UN, u + 1))
                        act.activation(capped[:, u % 2, :], lg[:, u % 2, 0:384], ACT.Tanh, scale=SCALE / A_CAP).then_inc(capped_done, 1)
                        act.wait_ge(capped_done, done(g, UN, u + 1))
                        act.wait_ge(mask_done, done(g, UN, u - 1))
                        act.activation(probs[:, u % 2, :], capped[:, u % 2, :], ACT.Exp, scale=A_CAP).then_inc(exp_done, 1)


def softmax_cross(nc, env, ctxT, wkT, bk, gamma, beta):
    SCALE, EPS = float(DIM) ** -0.5, 1e-6
    with ExitStack() as ctx:
        sb, ps, sem = tools(nc, ctx, "xc")
        ctx_sb, w_sb, b_sb = sb("ctx", [CTX, TOKENS]), sb("w", [CTX, CTX]), sb("b", [CTX, 1])
        g_sb, be_sb = sb("g", [P, DIM]), sb("be", [P, DIM])
        kvT, kv, oT = sb("kvT", [CTX, TOKENS]), sb("kv", [P, TILES, CTX]), sb("oT", [CTX, TOKENS])
        stats, mv, var, half, rstd = sb("stats", [P, TILES, 6]), sb("mv", [P, TILES, 2]), sb("var", [P, TILES]), sb("half", [P, TILES]), sb("rstd", [P, TILES])
        n1, n2, n3, e = sb("n1", [P, 2, DIM]), sb("n2", [P, 2, DIM]), sb("n3", [P, 2, DIM]), sb("e", [P, 2, DIM])
        mx, total, rec = sb("mx", [P, TILES]), sb("total", [P, TILES]), sb("rec", [P, TILES])
        kp, tp, sp_ = ps("kp", [CTX, 2, 512]), ps("tp", [P, 2, 512]), ps("sp", [P, 4, 512])
        loaded, kv_done, biased, turned, kv_copied = sem("loaded"), sem("kv_done"), sem("biased"), sem("turned"), sem("kv_copied")
        o_done, o_copied, sim_done, stats_done, aggr_done, var_done = sem("o_done"), sem("o_copied"), sem("sim_done"), sem("stats_done"), sem("aggr_done"), sem("var_done")
        half_done, rstd_done, centered, scaled, shifted, max_done, exp_done, rec_done, added = (
            sem("half_done"), sem("rstd_done"), sem("centered"), sem("scaled"), sem("shifted"), sem("max_done"), sem("exp_done"), sem("rec_done"), sem("added"))
        with nc.Block() as block:
            @block.sync
            def _(sp):
                sp.dma_start(ctx_sb[:], ctxT).then_inc(loaded, 16)
                sp.dma_start(w_sb[:], wkT).then_inc(loaded, 16)
                sp.dma_start(b_sb[:], bk.rearrange("(d o) -> d o", o=1)).then_inc(loaded, 16)
                sp.dma_start(g_sb[:], gamma.rearrange("(o d) -> o d", o=1).to_broadcast([P, DIM])).then_inc(loaded, 16)
                sp.dma_start(be_sb[:], beta.rearrange("(o d) -> o d", o=1).to_broadcast([P, DIM])).then_inc(loaded, 16)

            @block.tensor
            def _(pe):
                pe.wait_ge(loaded, 80)
                for c in range(2):
                    pe.matmul(kp[:, c, :], w_sb[:], ctx_sb[:, 512 * c:512 * c + 512], start=True, stop=True).then_inc(kv_done, 1)
                pe.wait_ge(biased, 2)
                for t in range(TILES):
                    mm = pe.transpose(tp[:, 0, CTX * t:CTX * t + CTX], kvT[:, P * t:P * t + P], env.c("ident")[0:CTX, 0:CTX])
                mm.then_inc(turned, 1)
                pe.wait_ge(kv_copied, 1)
                for b in range(BATCH):
                    for k in range(KC):
                        mm = pe.matmul(kp[:, b // 2, SEQ * (b % 2):SEQ * (b % 2) + SEQ], kv[:, 2 * b + k, :], env.xT[:, k, SEQ * b:SEQ * b + SEQ], start=(k == 0), stop=(k == KC - 1))
                    mm.then_inc(o_done, 1)
                for t in range(TILES):
                    if t % 4 == 0:
                        pe.wait_ge(o_copied, t // 4 + 1)
                    if t >= 4:
                        pe.wait_ge(centered, t - 3)
                    b = t // 2
                    pe.matmul(sp_[:, t % 4, 0:DIM], oT[:, P * t:P * t + P], kvT[:, SEQ * b:SEQ * b + SEQ], start=True, stop=True).then_inc(sim_done, 1)

            @block.vector
            def _(dve):
                for c in range(2):
                    dve.wait_ge(kv_done, c + 1)
                    dve.tensor_scalar(kvT[:, 512 * c:512 * c + 512], kp[:, c, :], b_sb[:, 0:1], None, ALU.add).then_inc(biased, 1)
                dve.wait_ge(turned, 1)
                dve.tensor_copy(kv[:], tp[:, 0, :].rearrange("p (t d) -> p t d", d=CTX)).then_inc(kv_copied, 1)
                for c in range(2):
                    dve.wait_ge(o_done, 2 * c + 2)
                    dve.tensor_copy(oT[:, 512 * c:512 * c + 512], kp[:, c, :]).then_inc(o_copied, 1)

                def first(t):
                    dve.wait_ge(sim_done, t + 1)
                    dve.bn_stats(stats[:, t, :], sp_[:, t % 4, 0:DIM]).then_inc(stats_done, 1)
                    dve.wait_ge(stats_done, t + 1)
                    dve.bn_aggr(mv[:, t, :], stats[:, t, :]).then_inc(aggr_done, 1)
                    dve.wait_ge(aggr_done, t + 1)
                    dve.tensor_scalar(var[:, t:t + 1], mv[:, t, 1:2], SCALE * SCALE, EPS, ALU.mult, ALU.add).then_inc(var_done, 1)

                def second(t):
                    dve.wait_ge(rstd_done, 2 * t + 2)
                    if t >= 2:
                        dve.wait_ge(scaled, t - 1)
                    dve.tensor_scalar(n1[:, t % 2, :], sp_[:, t % 4, 0:DIM], mv[:, t, 0:1], rstd[:, t:t + 1], ALU.subtract, ALU.mult).then_inc(centered, 1)
                    dve.wait_ge(shifted, t + 1)
                    dve.tensor_reduce(mx[:, t:t + 1], n3[:, t % 2, :], AX, ALU.max, negate=True).then_inc(max_done, 1)

                def third(t):
                    dve.wait_ge(exp_done, t + 1)
                    dve.reciprocal(rec[:, t:t + 1], total[:, t:t + 1]).then_inc(rec_done, 1)
                    dve.wait_ge(rec_done, t + 1)
                    dve.scalar_tensor_tensor(env.x[:, t, :], e[:, t % 2, :], rec[:, t:t + 1], env.x[:, t, :], ALU.mult, ALU.add).then_inc(added, 1)

                for i in range(TILES + 2):
                    if i < TILES:
                        first(i)
                    if 1 <= i <= TILES:
                        second(i - 1)
                    if i >= 2:
                        third(i - 2)

            @block.gpsimd
            def _(pool):
                pool.memset(half[:], -0.5).then_inc(half_done, 1)
                pool.wait_ge(half_done, 1)
                pool.wait_ge(loaded, 80)

                for t in range(TILES):
                    pool.wait_ge(var_done, t + 1)
                    pool.tensor_tensor(rstd[:, t:t + 1], var[:, t:t + 1], half[:, t:t + 1], ALU.pow).then_inc(rstd_done, 1)
                    pool.wait_ge(rstd_done, 2 * t + 1)
                    pool.tensor_scalar(rstd[:, t:t + 1], rstd[:, t:t + 1], SCALE, None, ALU.mult).then_inc(rstd_done, 1)
                    pool.wait_ge(centered, t + 1)
                    pool.tensor_tensor(n2[:, t % 2, :], n1[:, t % 2, :], g_sb[:], ALU.mult).then_inc(scaled, 1)
                    pool.wait_ge(scaled, t + 1)
                    if t >= 2:
                        pool.wait_ge(exp_done, t - 1)
                    pool.tensor_tensor(n3[:, t % 2, :], n2[:, t % 2, :], be_sb[:], ALU.add).then_inc(shifted, 1)

            @block.scalar
            def _(act):
                for t in range(TILES):
                    act.wait_ge(max_done, t + 1)
                    if t >= 2:
                        act.wait_ge(added, t - 1)
                    act.activation(e[:, t % 2, :], n3[:, t % 2, :], ACT.Exp, bias=mx[:, t:t + 1], accum_out=total[:, t:t + 1]).then_inc(exp_done, 1)


NEG = -1.0e30
M_SLOTS = M_E * M_CAP
M_NONE = 1 << 20
M_IN_ROWS = M_SLOTS // P


def moe_shared_and_route(nc, env, zeros, wr, bias, ws_gate, ws_up, ws_down, slot_x, out_rows, key, wkey):
    G, GE = M_GROUPS, M_E // M_GROUPS
    with ExitStack() as ctx:
        sb, ps, sem = tools(nc, ctx, "mr")
        wr_sb, bias_sb = sb("wr", [P, KC, M_E]), sb("bias", [P, M_E])
        wg_sb, wu_sb, wd_sb = sb("wsg", [P, KC, M_F]), sb("wsu", [P, KC, M_F]), sb("wsd", [M_F, DIM])
        base_i, base = sb("base_i", [P, M_E], I32), sb("base", [P, M_E])
        sc, scb = sb("sc", [P, TILES, M_E]), sb("scb", [P, TILES, M_E])
        hi2, lo2 = sb("hi2", [P, TILES * G, 4]), sb("lo2", [P, TILES * G, 4])
        hi1, lo1, mn1, ml1 = sb("hi1", [P, TILES * G, 2]), sb("lo1", [P, TILES * G, 2]), sb("mn1", [P, TILES * G, 2]), sb("ml1", [P, TILES * G, 2])
        hi0, lo0, mn0, ml0 = sb("hi0", [P, TILES * G]), sb("lo0", [P, TILES * G]), sb("mn0", [P, TILES * G]), sb("ml0", [P, TILES * G])
        gs, gr, g8 = sb("gs", [P, TILES, 16]), sb("gr", [P, TILES, 16]), sb("g8", [P, TILES, 8])
        gm, gpen = sb("gm", [P, TILES, G]), sb("gpen", [P, TILES, G])
        cand, cand2, c8, crep = sb("cand", [P, TILES, M_E]), sb("cand2", [P, TILES, M_E]), sb("c8", [P, TILES, 8]), sb("crep", [P, TILES, M_E])
        sel, wsel, wsum, wrec = sb("sel", [P, TILES, M_E]), sb("wsel", [P, TILES, M_E]), sb("wsum", [P, TILES]), sb("wrec", [P, TILES])
        fits, pos, slot, keyed, wfit, junk = (sb("fits", [P, TILES, M_E]), sb("pos", [P, TILES, M_E]), sb("slot", [P, TILES, M_E]),
                                            sb("keyed", [P, TILES, M_E]), sb("wfit", [P, TILES, M_E]), sb("junk", [P, M_E]))
        kf, far = sb("kf", [P, TILES, 8]), sb("far", [P, TILES, 8])
        idx = sb("idx", [P, TILES, 8], I32)
        zrow = sb("zrow", [P, DIM])
        s_h, h = sb("s_h", [M_F, 2, 512]), sb("h", [M_F, TOKENS])
        lp, gp, pp, up, dp = ps("lp", [P, 512]), ps("gp", [M_F, 512]), ps("pp", [P, 512]), ps("up", [M_F, 512]), ps("dp", [P, 2, 512])
        loaded, zeroed, zfilled = sem("loaded"), sem("zeroed"), sem("zfilled")
        routed, counted, gate_done, up_done, down_done = sem("routed"), sem("counted"), sem("gate_done"), sem("up_done"), sem("down_done")
        sig_done, silu_done, iota_done = sem("sig_done"), sem("silu_done"), sem("iota_done")
        step, selected, keys_done, h_done, added, scattered = sem("step"), sem("selected"), sem("keys_done"), sem("h_done"), sem("added"), sem("scattered")
        with nc.Block() as block:
            @block.sync
            def _(sp):
                sp.dma_start(wr_sb[:], wr.rearrange("(k p) n -> p k n", p=P)).then_inc(loaded, 16)
                sp.dma_start(bias_sb[:], bias.rearrange("(o d) -> o d", o=1).to_broadcast([P, M_E])).then_inc(loaded, 16)
                sp.dma_start(wg_sb[:], ws_gate.rearrange("(k p) n -> p k n", p=P)).then_inc(loaded, 16)
                sp.dma_start(wu_sb[:], ws_up.rearrange("(k p) n -> p k n", p=P)).then_inc(loaded, 16)
                sp.dma_start(wd_sb[:], ws_down).then_inc(loaded, 16)
                sp.wait_ge(zeroed, 1)
                sp.dma_start(slot_x[1:1 + M_SLOTS, :].rearrange("(n p) c -> p n c", p=P), zeros[:]).then_inc(zfilled, 16)
                sp.dma_start(out_rows[0:1, :], zrow[0:1, :]).then_inc(zfilled, 16)
                sp.wait_ge(zfilled, 32)

            @block.tensor
            def _(pe):
                pe.wait_ge(loaded, 80)
                for t in range(TILES):
                    for k in range(KC):
                        mm = pe.matmul(lp[:, M_E * t:M_E * t + M_E], env.xT[:, k, P * t:P * t + P], wr_sb[:, k, :], start=(k == 0), stop=(k == KC - 1))
                mm.then_inc(routed, 1)
                for c in range(2):
                    if c:
                        pe.wait_ge(h_done, 1)
                    for w, bank, s in ((wg_sb, gp, gate_done), (wu_sb, up, up_done)):
                        for k in range(KC):
                            mm = pe.matmul(bank[:], w[:, k, :], env.xT[:, k, 512 * c:512 * c + 512], start=(k == 0), stop=(k == KC - 1))
                        mm.then_inc(s, 1)
                pe.wait_ge(selected, 1)
                for t in range(TILES):
                    for u in range(t + 1):
                        w = env.c("before") if u == t else env.c("ones")
                        mm = pe.matmul(pp[:, M_E * t:M_E * t + M_E], w, sel[:, u, :], start=(u == 0), stop=(u == t))
                mm.then_inc(counted, 1)
                for t in range(TILES):
                    pe.wait_ge(h_done, t // 4 + 1)
                    if t >= 2:
                        pe.wait_ge(added, t - 1)
                    pe.matmul(dp[:, t % 2, 0:DIM], h[:, P * t:P * t + P], wd_sb[:], start=True, stop=True).then_inc(down_done, 1)

            @block.scalar
            def _(act):
                act.wait_ge(routed, 1)
                act.activation(sc[:], lp[:].rearrange("p (t e) -> p t e", e=M_E), ACT.Sigmoid).then_inc(sig_done, 1)
                for c in range(2):
                    act.wait_ge(gate_done, c + 1)
                    act.activation(s_h[:, c, :], gp[:], ACT.Silu).then_inc(silu_done, 1)

            @block.vector
            def _(dve):
                count = [0]

                def chain(ins):
                    count[0] += 1
                    ins.then_inc(step, 1)
                    dve.wait_ge(step, count[0])

                dve.memset(zeros[:], 0.0)
                dve.memset(zrow[:], 0.0).then_inc(zeroed, 1)
                chain(dve.memset(gs[:], NEG))
                for c in range(2):
                    dve.wait_ge(silu_done, c + 1)
                    dve.wait_ge(up_done, c + 1)
                    dve.tensor_tensor(h[:, 512 * c:512 * c + 512], s_h[:, c, :], up[:], ALU.mult).then_inc(h_done, 1)
                dve.wait_ge(sig_done, 1)
                chain(dve.tensor_tensor(scb[:], sc[:], bias_sb[:].rearrange("p (o e) -> p o e", o=1).to_broadcast([P, TILES, M_E]), ALU.add))
                v8 = scb[:].rearrange("p t (g e) -> p (t g) e", e=GE)
                chain(dve.tensor_tensor(hi2[:], v8[:, :, 0:4], v8[:, :, 4:8], ALU.max))
                chain(dve.tensor_tensor(lo2[:], v8[:, :, 0:4], v8[:, :, 4:8], ALU.min))
                for hi, lo, n, hn, ln_, mn, ml in ((hi2[:], lo2[:], 2, hi1[:], lo1[:], mn1[:], ml1[:]),
                                                  (hi1[:], lo1[:], 1, hi0[:].rearrange("p (g o) -> p g o", o=1), lo0[:].rearrange("p (g o) -> p g o", o=1),
                                                   mn0[:].rearrange("p (g o) -> p g o", o=1), ml0[:].rearrange("p (g o) -> p g o", o=1))):
                    chain(dve.tensor_tensor(hn, hi[:, :, 0:n], hi[:, :, n:2 * n], ALU.max))
                    chain(dve.tensor_tensor(mn, hi[:, :, 0:n], hi[:, :, n:2 * n], ALU.min))
                    chain(dve.tensor_tensor(ml, lo[:, :, 0:n], lo[:, :, n:2 * n], ALU.max))
                    chain(dve.tensor_tensor(ln_, mn, ml, ALU.max))
                chain(dve.tensor_tensor(gs[:, :, 0:G], hi0[:].rearrange("p (t g) -> p t g", g=G), lo0[:].rearrange("p (t g) -> p t g", g=G), ALU.add))
                for t in range(TILES):
                    chain(dve.max(g8[:, t, :], gs[:, t, :]))
                chain(dve.memset(g8[:, :, M_KG:8], NEG))
                for t in range(TILES):
                    chain(dve.match_replace(gr[:, t, :], g8[:, t, :], gs[:, t, :], NEG))
                chain(dve.tensor_tensor(gm[:], gr[:, :, 0:G], gs[:, :, 0:G], ALU.not_equal))
                chain(dve.tensor_scalar(gpen[:], gm[:], -NEG, NEG, ALU.mult, ALU.add))
                wide = lambda a: a.rearrange("p t (g o) -> p (t g) o", o=1).to_broadcast([P, TILES * G, GE])
                grouped = lambda a: a.rearrange("p t (g e) -> p (t g) e", e=GE)
                chain(dve.tensor_tensor(grouped(cand[:]), grouped(scb[:]), wide(gm[:]), ALU.mult))
                chain(dve.tensor_tensor(grouped(cand2[:]), grouped(cand[:]), wide(gpen[:]), ALU.add))
                for t in range(TILES):
                    chain(dve.max(c8[:, t, :], cand2[:, t, :]))
                chain(dve.memset(c8[:, :, M_K:8], NEG))
                for t in range(TILES):
                    chain(dve.match_replace(crep[:, t, :], c8[:, t, :], cand2[:, t, :], NEG))
                chain(dve.tensor_tensor(sel[:], crep[:], cand2[:], ALU.not_equal))
                dve.sem_inc(selected, 1)
                chain(dve.tensor_tensor(wsel[:], sc[:], sel[:], ALU.mult))
                chain(dve.tensor_reduce(wsum[:], wsel[:], AX, ALU.add))
                chain(dve.reciprocal(wrec[:], wsum[:]))
                dve.wait_ge(counted, 1)
                dve.wait_ge(iota_done, 1)
                p3 = pp[:].rearrange("p (t e) -> p t e", e=M_E)
                chain(dve.tensor_scalar(fits[:], p3, float(M_CAP), None, ALU.is_lt))
                chain(dve.tensor_tensor(fits[:], fits[:], sel[:], ALU.mult))
                chain(dve.tensor_copy(base[:], base_i[:]))
                chain(dve.tensor_tensor(slot[:], p3, base[:].rearrange("p (o e) -> p o e", o=1).to_broadcast([P, TILES, M_E]), ALU.add))
                chain(dve.tensor_tensor(keyed[:], slot[:], fits[:], ALU.mult))
                chain(dve.tensor_tensor(wfit[:], wsel[:], fits[:], ALU.mult))
                for t in range(TILES):
                    chain(dve.max(kf[:, t, :], keyed[:, t, :]))
                chain(dve.tensor_scalar(far[:], kf[:], 0.0, float(M_NONE), ALU.is_equal, ALU.mult))
                chain(dve.tensor_tensor(far[:], far[:], kf[:], ALU.add))
                chain(dve.tensor_copy(idx[:], far[:]))
                dve.sem_inc(keys_done, 1)
                chain(dve.tensor_copy(key[:], kf[:]))
                for t in range(TILES):
                    for k in range(M_K):
                        chain(dve.scalar_tensor_tensor(junk[:], keyed[:, t, :], kf[:, t, k:k + 1], wfit[:, t, :], ALU.is_equal, ALU.mult, accum_out=wkey[:, t, k:k + 1]))
                    chain(dve.tensor_scalar(wkey[:, t, 0:M_K], wkey[:, t, 0:M_K], wrec[:, t:t + 1], M_SCALE, ALU.mult, ALU.mult))
                dve.wait_ge(scattered, 16 * TILES * M_K)
                for t in range(TILES):
                    dve.wait_ge(down_done, t + 1)
                    dve.tensor_tensor(env.x[:, t, :], env.x[:, t, :], dp[:, t % 2, 0:DIM], ALU.add).then_inc(added, 1)

            @block.gpsimd
            def _(pool):
                pool.iota(base_i[:], pattern=[[M_CAP, M_E]], base=1, channel_multiplier=0).then_inc(iota_done, 1)
                pool.wait_ge(zfilled, 32)
                pool.wait_ge(keys_done, 1)
                for t in range(TILES):
                    for k in range(M_K):
                        pool.indirect_dma_start(slot_x[:], bass.IndirectOffsetOnAxis(ap=idx[:, t, k:k + 1], axis=0), env.x[:, t, :], None,
                                                bounds_check=M_SLOTS, oob_is_err=False).then_inc(scattered, 16)
                pool.wait_ge(scattered, 16 * TILES * M_K)


def moe_experts(nc, env, slot_x, out_rows, w_gate, w_up, w_down, key, wkey):
    Q, HALVES = 4, 2
    ITER = M_E // (Q * HALVES)
    NQ = Q * M_CAP
    with ExitStack() as ctx:
        sb, ps, sem = tools(nc, ctx, "me")
        xs_tok, xsT = sb("xs_tok", [P, 6, DIM]), sb("xsT", [P, KC, M_SLOTS])
        wg, wu, wd = sb("wg", [P, HALVES, Q, KC, M_F]), sb("wu", [P, HALVES, Q, KC, M_F]), sb("wd", [M_F, HALVES, Q, DIM])
        act_h, h = sb("act_h", [M_F, HALVES, NQ]), sb("h", [M_F, HALVES, NQ])
        o_sb = sb("o", [M_CAP, HALVES, Q, DIM])
        got = sb("got", [P, 6, DIM])
        tp, hp, op = ps("tp", [P, 2, 512]), ps("hp", [M_F, 2, 512]), ps("op", [M_CAP, 4, 512])
        rows_loaded, turned, xs_copied = sem("rows_loaded"), sem("turned"), sem("xs_copied")
        wg_loaded, wd_loaded, hidden, silu_done, h_done, down_done, o_copied, stored = (
            [sem("wg_loaded0"), sem("wg_loaded1")], [sem("wd_loaded0"), sem("wd_loaded1")], sem("hidden"), sem("silu_done"), sem("h_done"), sem("down_done"), sem("o_copied"), sem("stored"))
        o_copied2, o_stored = sem("o_copied2"), sem("o_stored")
        gathered, summed = [sem(f"gathered{k}") for k in range(M_K)], sem("summed")
        NT = M_SLOTS // P
        with nc.Block() as block:
            @block.sync
            def _(sp):
                view = slot_x[1:1 + M_SLOTS, :].rearrange("(n p) c -> p n c", p=P)
                for n in range(4):
                    if n:
                        sp.wait_ge(turned, 3 * n)
                    sp.dma_start(xs_tok[:], view[:, 6 * n:6 * n + 6, :]).then_inc(rows_loaded, 16)
                gv = w_gate.rearrange("e (k p) f -> p e k f", p=P)
                uv = w_up.rearrange("e (k p) f -> p e k f", p=P)
                dv = w_down.rearrange("e f c -> f e c")
                with sp.Fori(0, ITER) as i:
                    for s in range(HALVES):
                        sp.wait_ge(hidden, done(i, HALVES, s - 1))
                        for e in range(Q):
                            sp.dma_start(wg[:, s, e, :, :], gv[:, ds(i * (Q * HALVES) + (s * Q + e), 1), :, :].rearrange("p e k f -> p (e k) f")).then_inc(wg_loaded[s], 16)
                            sp.dma_start(wu[:, s, e, :, :], uv[:, ds(i * (Q * HALVES) + (s * Q + e), 1), :, :].rearrange("p e k f -> p (e k) f")).then_inc(wg_loaded[s], 16)
                        sp.wait_ge(down_done, done(i, 2 * HALVES, 2 * (s - 1)))
                        sp.dma_start(wd[:, s, :, :], dv[:, ds(i * (Q * HALVES) + s * Q, Q), :]).then_inc(wd_loaded[s], 16)

            @block.tensor
            def _(pe):
                credit(pe, hidden, down_done)
                for n in range(4):
                    pe.wait_ge(rows_loaded, 16 * n + 16)
                    for m in range(3):
                        q = 3 * n + m
                        if q >= 2:
                            pe.wait_ge(xs_copied, q - 1)
                        for j in range(4):
                            mm = pe.transpose(tp[:, q % 2, P * j:P * j + P], xs_tok[:, 2 * m + j % 2, P * (j // 2):P * (j // 2) + P], env.c("ident"))
                        mm.then_inc(turned, 1)
                pe.wait_ge(xs_copied, 12)

                def down(i, s):
                    pe.wait_ge(h_done, done(i, HALVES, s + 1))
                    pe.wait_ge(wd_loaded[s], i * 16 + 16)
                    for e in range(Q):
                        if e % 2 == 0:
                            pe.wait_ge(o_copied if e == 0 else o_copied2, done(i, HALVES, s - 1))
                        mm = pe.matmul(op[:, 2 * s + e // 2, DIM * (e % 2):DIM * (e % 2) + DIM], h[:, s, M_CAP * e:M_CAP * e + M_CAP], wd[:, s, e, :], start=True, stop=True)
                        if e % 2:
                            mm.then_inc(down_done, 1)

                with pe.Fori(0, ITER) as i:
                    for s in range(HALVES):
                        pe.wait_ge(wg_loaded[s], i * (32 * Q) + 32 * Q)
                        pe.wait_ge(h_done, done(i, HALVES, s - 1))
                        for e in range(Q):
                            for w, o in ((wg, 0), (wu, NQ)):
                                for k in range(KC):
                                    mm = pe.matmul(hp[:, s, o + M_CAP * e:o + M_CAP * e + M_CAP], w[:, s, e, k, :], xsT[:, k, ds(i * (NQ * HALVES) + (s * NQ + M_CAP * e), M_CAP)], start=(k == 0), stop=(k == KC - 1))
                        mm.then_inc(hidden, 1)
                    for s in range(HALVES):
                        down(i, s)

            @block.scalar
            def _(act):
                credit(act, silu_done, o_copied2)
                with act.Fori(0, ITER) as i:
                    for s in range(HALVES):
                        act.wait_ge(hidden, done(i, HALVES, s + 1))
                        act.wait_ge(h_done, done(i, HALVES, s - 1))
                        act.activation(act_h[:, s, :], hp[:, s, 0:NQ], ACT.Silu).then_inc(silu_done, 1)
                    for s in range(HALVES):
                        act.wait_ge(down_done, done(i, 2 * HALVES, 2 * s + 2))
                        if s == 0:
                            act.wait_ge(o_stored, done(i, 1, 0))
                        act.copy(o_sb[:, s, 2:4, :], op[:, 2 * s + 1, :].rearrange("p (e c) -> p e c", c=DIM)).then_inc(o_copied2, 1)

            @block.vector
            def _(dve):
                credit(dve, h_done, o_copied)
                for q in range(12):
                    dve.wait_ge(turned, q + 1)
                    dve.tensor_copy(xsT[:, :, 2 * P * q:2 * P * q + 2 * P], tp[:, q % 2, :].rearrange("p (k n) -> p k n", k=KC)).then_inc(xs_copied, 1)
                with dve.Fori(0, ITER) as i:
                    for s in range(HALVES):
                        dve.wait_ge(silu_done, done(i, HALVES, s + 1))
                        dve.wait_ge(down_done, done(i, 2 * HALVES, 2 * (s - 1)))
                        dve.tensor_tensor(h[:, s, :], act_h[:, s, :], hp[:, s, NQ:2 * NQ], ALU.mult).then_inc(h_done, 1)
                    for s in range(HALVES):
                        dve.wait_ge(down_done, done(i, 2 * HALVES, 2 * s + 1))
                        if s == 0:
                            dve.wait_ge(o_stored, done(i, 1, 0))
                        dve.tensor_copy(o_sb[:, s, 0:2, :], op[:, 2 * s, :].rearrange("p (e c) -> p e c", c=DIM)).then_inc(o_copied, 1)
                for t in range(TILES):
                    for k in range(M_K):
                        dve.wait_ge(gathered[k], 16 * t + 16)
                        if t or k:
                            dve.wait_ge(summed, t * M_K + k)
                        dve.scalar_tensor_tensor(env.x[:, t, :], got[:, k, :], wkey[:, t, k:k + 1], env.x[:, t, :], ALU.mult, ALU.add).then_inc(summed, 1)

            @block.gpsimd
            def _(pool):
                credit(pool, o_stored)
                view = out_rows[1:1 + M_SLOTS, :].rearrange("(e s) c -> s e c", s=M_CAP)
                with pool.Fori(0, ITER) as i:
                    for s in range(HALVES):
                        pool.wait_ge(o_copied, done(i, HALVES, s + 1))
                        pool.wait_ge(o_copied2, done(i, HALVES, s + 1))
                        pool.dma_start(view[:, ds(i * (Q * HALVES) + s * Q, Q), :], o_sb[:, s, :, :]).then_inc(stored, 16)
                    pool.wait_ge(stored, i * 32 + 32)
                    pool.sem_inc(o_stored, 1)
                for t in range(TILES):
                    for k in range(M_K):
                        if t:
                            pool.wait_ge(summed, (t - 1) * M_K + k + 1)
                        pool.indirect_dma_start(got[:, k, :], None, out_rows[:], bass.IndirectOffsetOnAxis(ap=key[:, t, k:k + 1], axis=0),
                                                bounds_check=M_SLOTS, oob_is_err=False).then_inc(gathered[k], 16)


def routed_experts(nc, env, a, slot_x, out_rows):
    with ExitStack() as ctx:
        zeros = ctx.enter_context(nc.sbuf_tensor("m_zeros", [P, M_IN_ROWS, DIM], F32))
        key = ctx.enter_context(nc.sbuf_tensor("m_key", [P, TILES, 8], I32))
        wkey = ctx.enter_context(nc.sbuf_tensor("m_wkey", [P, TILES, 8], F32))
        moe_shared_and_route(nc, env, zeros, a["L0_ffn_gate_w"], a["L0_ffn_bias"], a["L0_ffn_ws_gate"], a["L0_ffn_ws_up"], a["L0_ffn_ws_down"], slot_x, out_rows, key, wkey)
        moe_experts(nc, env, slot_x, out_rows, a["L0_ffn_w_gate"], a["L0_ffn_w_up"], a["L0_ffn_w_down"], key, wkey)


D_N = D_H * D_V
G_, B_, GAM_, END_ = range(4)


def delta_prepare(nc, env, a, v, gate, par):
    with ExitStack() as ctx:
        sb, ps, sem = tools(nc, ctx, "dp")
        wv, wg = sb("wv", [P, KC, D_N]), sb("wg", [P, KC, D_N])
        wab = sb("wab", [P, KC, 2 * D_H])
        cw = sb("cw", [P, 3, D_CONV])
        dt_b, a_log, a_exp = sb("dt_b", [P, D_H]), sb("a_log", [P, D_H]), sb("a_exp", [P, D_H])
        raw, acc = sb("raw", [P, 3, BATCH, SEQ + 3]), sb("acc", [P, 3, BATCH, SEQ])
        vT = sb("vT", [P, 3, TOKENS])
        z, u, s, s2, poly, up2, sp_ = (sb(n, [P, TILES, D_H]) for n in ("z", "u", "s", "s2", "poly", "up2", "sp"))
        pj, gp, tp, dec, ab = ps("pj", [P, 2, 512]), ps("gp", [P, 2, 512]), ps("tp", [P, 2, 512]), ps("dec", [P, 2, TILES * D_H]), ps("ab", [P, TILES, 2 * D_H])
        loaded, projected, raw_copied, conv_done, silu_done, turned, v_copied = (sem(n) for n in ("loaded", "projected", "raw_copied", "conv_done", "silu_done", "turned", "v_copied"))
        ab_done, gate_done, gate_silu, dec_done, step, exps, z_done, g_done, beta_done, padded, dec_exp = (
            sem(n) for n in ("ab_done", "gate_done", "gate_silu", "dec_done", "step", "exps", "z_done", "g_done", "beta_done", "padded", "dec_exp"))
        NL = 8
        with nc.Block() as block:
            @block.sync
            def _(sp):
                sp.dma_start(wv[:], a["L1_attn_Wv"].rearrange("(k p) n -> p k n", p=P)).then_inc(loaded, 16)
                sp.dma_start(wg[:], a["L1_attn_Wg"].rearrange("(k p) n -> p k n", p=P)).then_inc(loaded, 16)
                sp.dma_start(wab[:, :, 0:D_H], a["L1_attn_Wb"].rearrange("(k p) n -> p k n", p=P)).then_inc(loaded, 16)
                sp.dma_start(wab[:, :, D_H:2 * D_H], a["L1_attn_Wa"].rearrange("(k p) n -> p k n", p=P)).then_inc(loaded, 16)
                sp.dma_start(cw[:], a["L1_attn_conv_wv"].rearrange("(m p) k -> p m k", p=P)).then_inc(loaded, 16)
                sp.dma_start(dt_b[:], a["L1_attn_dt_bias"].rearrange("(o d) -> o d", o=1).to_broadcast([P, D_H])).then_inc(loaded, 16)
                sp.dma_start(a_log[:], a["L1_attn_A_log"].rearrange("(o d) -> o d", o=1).to_broadcast([P, D_H])).then_inc(loaded, 16)

            @block.tensor
            def _(pe):
                pe.wait_ge(loaded, 112)
                for t in range(TILES):
                    for k in range(KC):
                        mm = pe.matmul(ab[:, t, :], env.xT[:, k, P * t:P * t + P], wab[:, k, :], start=(k == 0), stop=(k == KC - 1))
                mm.then_inc(ab_done, 1)
                for n in range(6):
                    m, c = divmod(n, 2)
                    if n >= 2:
                        pe.wait_ge(raw_copied, n - 1)
                    for k in range(KC):
                        mm = pe.matmul(pj[:, n % 2, :], wv[:, k, P * m:P * m + P], env.xT[:, k, 512 * c:512 * c + 512], start=(k == 0), stop=(k == KC - 1))
                    mm.then_inc(projected, 1)
                for t in range(TILES):
                    if t >= 2:
                        pe.wait_ge(gate_silu, t - 1)
                    for k in range(KC):
                        mm = pe.matmul(gp[:, t % 2, 0:D_N], env.xT[:, k, P * t:P * t + P], wg[:, k, :], start=(k == 0), stop=(k == KC - 1))
                    mm.then_inc(gate_done, 1)
                for t in range(TILES):
                    pe.wait_ge(silu_done, 3)
                    if t >= 2:
                        pe.wait_ge(v_copied, t - 1)
                    for m in range(3):
                        mm = pe.transpose(tp[:, t % 2, P * m:P * m + P], vT[:, m, P * t:P * t + P], env.c("ident"))
                    mm.then_inc(turned, 1)
                pe.wait_ge(g_done, 1)
                gsrc = par[:, :, G_, :].rearrange("p h t -> p h t")
                pe.matmul(dec[:, 0, :].rearrange("p (h t) -> p h t", t=TILES), env.c("upto"), gsrc, start=True, stop=True)
                pe.matmul(dec[:, 1, :].rearrange("p (h t) -> p h t", t=TILES), env.c("after"), gsrc, start=True, stop=True).then_inc(dec_done, 1)

            @block.scalar
            def _(act):
                act.wait_ge(loaded, 112)
                act.activation(a_exp[:], a_log[:], ACT.Exp).then_inc(exps, 1)
                act.wait_ge(z_done, 1)
                act.activation(u[:], u[:], ACT.Exp, scale=-1.0).then_inc(exps, 1)
                act.wait_ge(padded, 1)
                for n in range(6):
                    m, c = divmod(n, 2)
                    act.wait_ge(projected, n + 1)
                    act.copy(raw[:, m, 2 * c:2 * c + 2, 3:SEQ + 3], pj[:, n % 2, :].rearrange("p (b t) -> p b t", t=SEQ)).then_inc(raw_copied, 1)
                act.wait_ge(ab_done, 1)
                act.activation(par[:, :, B_, :], ab[:, :, 0:D_H].rearrange("p t h -> p h t"), ACT.Sigmoid).then_inc(beta_done, 1)
                for m in range(3):
                    act.wait_ge(conv_done, 4 * m + 4)
                    act.activation(vT[:, m, :].rearrange("p (b t) -> p b t", t=SEQ), acc[:, m, :, :], ACT.Silu).then_inc(silu_done, 1)
                for t in range(TILES):
                    act.wait_ge(gate_done, t + 1)
                    act.activation(gate[:, t, :], gp[:, t % 2, 0:D_N], ACT.Silu).then_inc(gate_silu, 1)
                act.wait_ge(dec_done, 1)
                act.activation(par[:, :, GAM_, :], dec[:, 0, :].rearrange("p (h t) -> p h t", t=TILES), ACT.Exp)
                act.activation(par[:, :, END_, :], dec[:, 1, :].rearrange("p (h t) -> p h t", t=TILES), ACT.Exp).then_inc(dec_exp, 1)

            @block.vector
            def _(dve):
                dve.memset(raw[:, :, :, 0:3], 0.0).then_inc(padded, 1)
                count = [0]

                def chain(ins):
                    count[0] += 1
                    ins.then_inc(step, 1)
                    dve.wait_ge(step, count[0])

                dve.wait_ge(ab_done, 1)
                dve.wait_ge(loaded, 112)
                chain(dve.tensor_tensor(z[:], ab[:, :, D_H:2 * D_H], dt_b[:].rearrange("p (o h) -> p o h", o=1).to_broadcast([P, TILES, D_H]), ALU.add))
                chain(dve.scalar_tensor_tensor(u[:], z[:], -1.0, z[:], ALU.mult, ALU.max))
                dve.sem_inc(z_done, 1)
                dve.wait_ge(exps, 2)
                chain(dve.tensor_scalar(up2[:], u[:], 2.0, None, ALU.add))
                chain(dve.reciprocal(s[:], up2[:]))
                chain(dve.tensor_tensor(s[:], s[:], u[:], ALU.mult))
                chain(dve.tensor_tensor(s2[:], s[:], s[:], ALU.mult))
                chain(dve.tensor_scalar(poly[:], s2[:], 1.0 / (2 * NL + 1), 1.0 / (2 * NL - 1), ALU.mult, ALU.add))
                for n in range(NL - 2, -1, -1):
                    chain(dve.tensor_tensor(poly[:], poly[:], s2[:], ALU.mult))
                    chain(dve.tensor_scalar(poly[:], poly[:], 1.0 / (2 * n + 1), None, ALU.add))
                chain(dve.tensor_tensor(poly[:], poly[:], s[:], ALU.mult))
                chain(dve.tensor_scalar(sp_[:], z[:], 0.0, None, ALU.max))
                chain(dve.scalar_tensor_tensor(sp_[:], poly[:], 2.0, sp_[:], ALU.mult, ALU.add))
                chain(dve.scalar_tensor_tensor(sp_[:], sp_[:], -1.0, a_exp[:].rearrange("p (o h) -> p o h", o=1).to_broadcast([P, TILES, D_H]), ALU.mult, ALU.mult))
                chain(dve.tensor_copy(par[:, :, G_, :], sp_[:].rearrange("p t h -> p h t")))
                dve.sem_inc(g_done, 1)
                for m in range(3):
                    dve.wait_ge(raw_copied, 2 * m + 2)
                    dve.tensor_scalar(acc[:, m, :, :], raw[:, m, :, 0:SEQ], cw[:, m, 0:1], None, ALU.mult).then_inc(conv_done, 1)
                    for i in range(1, D_CONV):
                        dve.wait_ge(conv_done, 4 * m + i)
                        dve.scalar_tensor_tensor(acc[:, m, :, :], raw[:, m, :, i:i + SEQ], cw[:, m, i:i + 1], acc[:, m, :, :], ALU.mult, ALU.add).then_inc(conv_done, 1)
                for t in range(TILES):
                    dve.wait_ge(turned, t + 1)
                    dve.tensor_copy(v[:, :, t, :], tp[:, t % 2, 0:D_N].rearrange("p (h d) -> p h d", d=D_V)).then_inc(v_copied, 1)


def delta_heads(nc, env, wq, wk, cq, ck, v, par, o):
    NLEV, C = 7, 2
    EPS = 1e-6
    with ExitStack() as ctx:
        sb, ps, sem = tools(nc, ctx, "dh")
        wk_s, wq_s = sb("wk", [P, KC, D_K]), sb("wq", [P, KC, D_K])
        conv_all, conv_w = sb("conv_all", [P, D_H, 2, D_CONV]), sb("conv_w", [P, 2, D_CONV])
        raw, acc, th, silu = sb("raw", [P, BATCH, SEQ + 3]), sb("acc", [P, BATCH, SEQ]), sb("th", [P, BATCH, SEQ]), sb("silu", [P, 2, TOKENS])
        sq, ss, ssc, rn = sb("sq", [P, 4, P]), sb("ss", [P, 2, TILES]), sb("ssc", [P, 2, TILES]), sb("rn", [P, 2, TILES])
        half, plus_half = sb("half", [P, TILES]), sb("plus_half", [P, TILES])
        kq, kqT = sb("kq", [P, 2, TILES, P]), sb("kqT", [P, TILES, 2, P])
        hp, hv = sb("hp", [P, 4, TILES]), sb("hv", [P, TILES, D_V])
        mats = {n: [sb(f"{n}{c}", [P, BATCH, P]) for c in range(C)] for n in ("gm", "E", "Em", "Eb", "AT", "PT", "T", "TT", "X")}
        OT = [[sb(f"OT{c}{n}", [P, BATCH, P]) for n in range(2)] for c in range(C)]
        R, U, DL, DE, QS = sb("R", [P, BATCH, D_V]), sb("U", [P, C, BATCH, D_V]), sb("DL", [P, C, BATCH, D_V]), sb("DE", [P, BATCH, D_V]), sb("QS", [P, BATCH, D_V])
        S = sb("S", [P, BATCH, D_V])
        pj, tp = ps("pj", [P, 2, 512]), ps("tp", [P, 2, 512])
        W = [[ps(f"W{c}{n}", [P, 512]) for n in range(2)] for c in range(C)]
        w_loaded, projected, turned, returned, seg_done, kk_done = (sem(n) for n in ("w_loaded", "projected", "turned", "returned", "seg_done", "kk_done"))
        x_done, tx_done, flip_done = ([sem(f"{n}{c}") for c in range(C)] for n in ("x_done", "tx_done", "flip_done"))
        u_done, o_done, s_done, ks_done = (sem(n) for n in ("u_done", "o_done", "s_done", "ks_done"))
        raw_copied, tanh_done, squared, kqT_copied, exp_done = (sem(n) for n in ("raw_copied", "tanh_done", "squared", "kqT_copied", "exp_done"))
        x_copied, flip_copied = ([sem(f"{n}{c}") for c in range(C)] for n in ("x_copied", "flip_copied"))
        conv_done, silu_done, sum_done, ssc_done, normed = (sem(n) for n in ("conv_done", "silu_done", "sum_done", "ssc_done", "normed"))
        a_done, p_done, step_done = (sem(n) for n in ("a_done", "p_done", "step_done"))
        t_done = [sem(f"t_done{c}") for c in range(C)]
        small, o_stored = sem("small"), sem("o_stored")
        hp_copied, gm_done, em_done, eb_done, pow_done, zeroed = (sem(n) for n in ("hp_copied", "gm_done", "em_done", "eb_done", "pow_done", "zeroed"))
        ot_done = [sem(f"ot_done{c}") for c in range(C)]
        conv_loaded, conv_picked = sem("conv_loaded"), sem("conv_picked")
        SM = 10

        with nc.Block() as block:
            @block.sync
            def _(sp):
                for m, w in enumerate((ck, cq)):
                    sp.dma_start(conv_all[:, :, m, :], w.rearrange("(h p) k -> p h k", p=D_K)).then_inc(conv_loaded, 16)
                with sp.Fori(0, D_H) as h:
                    head = sp.snap(h * D_K)
                    sp.wait_ge(projected, done(h, 4, 0))
                    sp.dma_start(wk_s[:], wk.rearrange("(k p) n -> p k n", p=P)[:, :, ds(head, D_K)]).then_inc(w_loaded, 16)
                    sp.dma_start(wq_s[:], wq.rearrange("(k p) n -> p k n", p=P)[:, :, ds(head, D_K)]).then_inc(w_loaded, 16)

            @block.tensor
            def _(pe):
                credit(pe, projected, turned, returned, seg_done, kk_done, *x_done, *tx_done, *flip_done, u_done, o_done, s_done, ks_done)
                tiles = lambda c, b: 2 * b + c
                with pe.Fori(0, D_H) as h:
                    pe.wait_ge(w_loaded, h * 32 + 32)
                    for n in range(4):
                        m, c = divmod(n, 2)
                        pe.wait_ge(raw_copied, done(h, 4, n - 1))
                        for k in range(KC):
                            mm = pe.matmul(pj[:, n % 2, :], (wk_s, wq_s)[m][:, k, :], env.xT[:, k, 512 * c:512 * c + 512], start=(k == 0), stop=(k == KC - 1))
                        mm.then_inc(projected, 1)
                    for c in range(C):
                        pe.wait_ge(gm_done, done(h, C, c + 1))
                        pe.wait_ge(o_stored, done(h, C, 0))
                        for b in range(BATCH):
                            mm = pe.matmul(W[c][0][:, P * b:P * b + P], mats["gm"][c][:, b, :], env.c("upto"), start=True, stop=True)
                        mm.then_inc(seg_done, 1)
                    for n in range(4):
                        m, c = divmod(n, 2)
                        pe.wait_ge(silu_done, done(h, 2, m + 1))
                        pe.wait_ge(normed, done(h, 4, n - 1))
                        for j in range(4):
                            t = 4 * c + j
                            mm = pe.transpose(tp[:, n % 2, P * j:P * j + P], silu[:, m, P * t:P * t + P], env.c("ident"))
                        mm.then_inc(turned, 1)
                    for n in range(4):
                        m, c = divmod(n, 2)
                        pe.wait_ge(normed, done(h, 4, n + 1))
                        if n < 2:
                            pe.wait_ge(raw_copied, done(h, 4, 4))
                        else:
                            pe.wait_ge(kqT_copied, done(h, 4, n - 1))
                        for j in range(4):
                            mm = pe.transpose(pj[:, n % 2, P * j:P * j + P], kq[:, m, 4 * c + j, :], env.c("ident"))
                        mm.then_inc(returned, 1)
                    for c in range(C):
                        pe.wait_ge(exp_done, done(h, C, c + 1))
                        pe.wait_ge(kqT_copied, done(h, 4, 4))
                        for b in range(BATCH):
                            t = tiles(c, b)
                            mm = pe.matmul(W[c][b // 2][:, SEQ * (b % 2):SEQ * (b % 2) + SEQ], kqT[:, t, 0, :], kqT[:, t, :, :].rearrange("p a n -> p (a n)"), start=True, stop=True)
                        mm.then_inc(kk_done, 1)

                    def flip(c, n, src, evid, val):
                        pe.wait_ge(evid, val)
                        for b in range(BATCH):
                            mm = pe.transpose(W[c][1][:, P * b:P * b + P], src[:, b, :], env.c("ident"))
                        mm.then_inc(flip_done[c], 1)

                    for c in range(C):
                        pe.wait_ge(p_done, done(h, C, c + 1))
                        flip(c, 0, mats["TT"][c], t_done[c], done(h, NLEV, 1))
                    for lv in range(1, NLEV):
                        for c in range(C):
                            pe.wait_ge(ot_done[c], done(h, NLEV, lv + 1))
                            pe.wait_ge(flip_copied[c], done(h, NLEV - 1, lv))
                            for b in range(BATCH):
                                mm = pe.matmul(W[c][0][:, P * b:P * b + P], OT[c][lv % 2][:, b, :], mats["T"][c][:, b, :], start=True, stop=True)
                            mm.then_inc(x_done[c], 1)
                        for c in range(C):
                            pe.wait_ge(x_copied[c], done(h, NLEV - 1, lv))
                            for b in range(BATCH):
                                l, r = (mats["TT"][c], mats["X"][c]) if lv < NLEV - 1 else (mats["X"][c], mats["TT"][c])
                                mm = pe.matmul(W[c][0][:, P * b:P * b + P], l[:, b, :], r[:, b, :], start=True, stop=True)
                            mm.then_inc(tx_done[c], 1)
                        if lv < NLEV - 1:
                            for c in range(C):
                                flip(c, lv, mats["T"][c], t_done[c], done(h, NLEV, lv + 1))

                    def small_products(bank, col, l, r, s):
                        for b in range(BATCH):
                            mm = pe.matmul(bank[:, col + D_V * b:col + D_V * b + D_V], l(b), r(b), start=True, stop=True)
                        mm.then_inc(s, 1)

                    TT = mats["TT"]
                    pe.wait_ge(t_done[0], done(h, NLEV, NLEV))
                    small_products(W[0][0], 0, lambda b: TT[0][:, b, :], lambda b: hv[:, tiles(0, b), :], u_done)
                    pe.wait_ge(small, done(h, SM, 1))
                    pe.wait_ge(small, done(h, SM, 2))
                    small_products(W[0][1], 0, lambda b: kq[:, 0, tiles(0, b), :], lambda b: DE[:, b, :], s_done)
                    small_products(W[0][0], 256, lambda b: mats["PT"][0][:, b, :], lambda b: DL[:, 0, b, :], o_done)
                    pe.wait_ge(small, done(h, SM, 3))
                    pe.wait_ge(t_done[1], done(h, NLEV, NLEV))
                    small_products(W[1][1], 0, lambda b: kqT[:, tiles(1, b), 0, :], lambda b: S[:, b, :], ks_done)
                    small_products(W[1][1], 128, lambda b: kqT[:, tiles(1, b), 1, :], lambda b: S[:, b, :], ks_done)
                    pe.wait_ge(small, done(h, SM, 5))
                    small_products(W[1][0], 0, lambda b: TT[1][:, b, :], lambda b: R[:, b, :], u_done)
                    pe.wait_ge(small, done(h, SM, 7))
                    small_products(W[1][0], 256, lambda b: mats["PT"][1][:, b, :], lambda b: DL[:, 1, b, :], o_done)

            @block.scalar
            def _(act):
                credit(act, raw_copied, tanh_done, squared, kqT_copied, exp_done, *x_copied, *flip_copied)
                act.wait_ge(zeroed, 1)
                with act.Fori(0, D_H) as h:
                    for m in range(2):
                        act.wait_ge(conv_done, done(h, 8, 4 * m))
                        for c in range(2):
                            act.wait_ge(projected, done(h, 4, 2 * m + c + 1))
                            act.copy(raw[:, 2 * c:2 * c + 2, 3:SEQ + 3], pj[:, c, :].rearrange("p (b t) -> p b t", t=SEQ)).then_inc(raw_copied, 1)
                        act.wait_ge(conv_done, done(h, 8, 4 * m + 4))
                        act.wait_ge(silu_done, done(h, 2, m))
                        act.activation(th[:], acc[:], ACT.Tanh, scale=0.5).then_inc(tanh_done, 1)
                        if m == 0:
                            for c in range(C):
                                act.wait_ge(seg_done, done(h, C, c + 1))
                                act.wait_ge(em_done, done(h, C, c))
                                act.activation(mats["E"][c][:], W[c][0][:].rearrange("p (b i) -> p b i", b=BATCH), ACT.Exp).then_inc(exp_done, 1)
                    for n in range(4):
                        act.wait_ge(turned, done(h, 4, n + 1))
                        act.wait_ge(sum_done, done(h, 4, n))
                        act.activation(sq[:], tp[:, n % 2, :].rearrange("p (j n) -> p j n", n=P), ACT.Square).then_inc(squared, 1)
                    act.wait_ge(o_done, done(h, C, 0))
                    for n in range(4):
                        m, c = divmod(n, 2)
                        act.wait_ge(returned, done(h, 4, n + 1))
                        act.copy(kqT[:, 4 * c:4 * c + 4, m, :], pj[:, n % 2, :].rearrange("p (j n) -> p j n", n=P)).then_inc(kqT_copied, 1)

                    def copy_flip(c, n):
                        act.wait_ge(flip_done[c], done(h, NLEV - 1, n + 1))
                        dst = mats["T"][c] if n == 0 else mats["TT"][c]
                        act.copy(dst[:], W[c][1][:].rearrange("p (b i) -> p b i", b=BATCH)).then_inc(flip_copied[c], 1)

                    for c in range(C):
                        copy_flip(c, 0)
                    for lv in range(1, NLEV):
                        for c in range(C):
                            act.wait_ge(x_done[c], done(h, NLEV - 1, lv))
                            act.copy(mats["X"][c][:], W[c][0][:].rearrange("p (b i) -> p b i", b=BATCH)).then_inc(x_copied[c], 1)
                        if lv < NLEV - 1:
                            for c in range(C):
                                copy_flip(c, lv)

            @block.vector
            def _(dve):
                credit(dve, conv_done, silu_done, sum_done, ssc_done, normed, a_done, p_done, *t_done, small, o_stored, step_done)
                dve.memset(raw[:, :, 0:3], 0.0)
                dve.memset(plus_half[:], 0.5)
                dve.memset(half[:], -0.5).then_inc(zeroed, 1)
                four = lambda x, c: hp[:, x, c:TILES:2].rearrange("p (b o) -> p b o", o=1)
                with dve.Fori(0, D_H) as h:
                    dve.wait_ge(conv_picked, done(h, 1, 1))
                    for m in range(2):
                        dve.wait_ge(raw_copied, done(h, 4, 2 * m + 2))
                        dve.wait_ge(silu_done, done(h, 2, m))
                        dve.tensor_scalar(acc[:], raw[:, :, 0:SEQ], conv_w[:, m, 0:1], None, ALU.mult).then_inc(conv_done, 1)
                        for i in range(1, D_CONV):
                            dve.wait_ge(conv_done, done(h, 8, 4 * m + i))
                            dve.scalar_tensor_tensor(acc[:], raw[:, :, i:i + SEQ], conv_w[:, m, i:i + 1], acc[:], ALU.mult, ALU.add).then_inc(conv_done, 1)
                        dve.wait_ge(tanh_done, done(h, 2, m + 1))
                        dve.wait_ge(turned, done(h, 4, 2 * m))
                        dve.scalar_tensor_tensor(silu[:, m, :].rearrange("p (b t) -> p b t", t=SEQ), th[:], 1.0, acc[:], ALU.add, ALU.mult).then_inc(silu_done, 1)
                    dve.wait_ge(o_done, done(h, C, 0))
                    for n in range(4):
                        m, c = divmod(n, 2)
                        dve.wait_ge(squared, done(h, 4, n + 1))
                        dve.tensor_reduce(ss[:, m, 4 * c:4 * c + 4], sq[:], AX, ALU.add).then_inc(sum_done, 1)
                        dve.wait_ge(sum_done, done(h, 4, n + 1))
                        dve.tensor_scalar(ssc[:, m, 4 * c:4 * c + 4], ss[:, m, 4 * c:4 * c + 4], 0.25, EPS, ALU.mult, ALU.add).then_inc(ssc_done, 1)
                        dve.wait_ge(pow_done, done(h, 8, 2 * n + 2))
                        dve.tensor_tensor(kq[:, m, 4 * c:4 * c + 4, :], tp[:, n % 2, :].rearrange("p (j n) -> p j n", n=P),
                                          rn[:, m, 4 * c:4 * c + 4].rearrange("p (j o) -> p j o", o=1).to_broadcast([P, 4, P]), ALU.mult).then_inc(normed, 1)
                    for c in range(C):
                        dve.wait_ge(kk_done, done(h, C, c + 1))
                        dve.wait_ge(eb_done, done(h, C, c + 1))
                        for n in range(2):
                            dve.tensor_tensor(mats["AT"][c][:, 2 * n:2 * n + 2, :], W[c][n][:].rearrange("p (b a i) -> p b a i", b=2, a=2)[:, :, 0, :], mats["Eb"][c][:, 2 * n:2 * n + 2, :], ALU.mult).then_inc(a_done, 1)
                        for n in range(2):
                            ins = dve.tensor_tensor(mats["PT"][c][:, 2 * n:2 * n + 2, :], W[c][n][:].rearrange("p (b a i) -> p b a i", b=2, a=2)[:, :, 1, :], mats["Em"][c][:, 2 * n:2 * n + 2, :], ALU.mult)
                        ins.then_inc(p_done, 1)
                    for c in range(C):
                        dve.wait_ge(ot_done[c], done(h, NLEV, 1))
                        dve.tensor_tensor(mats["TT"][c][:], env.c("ident").rearrange("p (o i) -> p o i", o=1).to_broadcast([P, BATCH, P]), OT[c][0][:], ALU.subtract).then_inc(t_done[c], 1)
                    for lv in range(1, NLEV):
                        for c in range(C):
                            m = mats["T"][c] if lv < NLEV - 1 else mats["TT"][c]
                            dve.wait_ge(tx_done[c], done(h, NLEV - 1, lv))
                            dve.tensor_tensor(m[:], m[:], W[c][0][:].rearrange("p (b i) -> p b i", b=BATCH), ALU.subtract).then_inc(t_done[c], 1)
                    wide = [P, BATCH, D_V]
                    w4 = lambda bank, col: bank[:, col:col + BATCH * D_V].rearrange("p (b d) -> p b d", d=D_V)
                    dve.wait_ge(u_done, done(h, C, 1))
                    dve.tensor_tensor(DL[:, 0, :, :], w4(W[0][0], 0), four(B_, 0).to_broadcast(wide), ALU.mult).then_inc(small, 1)
                    dve.wait_ge(small, done(h, SM, 1))
                    dve.tensor_tensor(DE[:], DL[:, 0, :, :], four(END_, 0).to_broadcast(wide), ALU.mult).then_inc(small, 1)
                    dve.wait_ge(s_done, done(h, 1, 1))
                    dve.tensor_copy(S[:], w4(W[0][1], 0)).then_inc(small, 1)
                    dve.wait_ge(o_done, done(h, C, 1))
                    dve.tensor_copy(o[:, 0:TILES:2, ds(h * D_V, D_V)], w4(W[0][0], 256)).then_inc(o_stored, 1)
                    dve.wait_ge(ks_done, done(h, 2, 2))
                    dve.tensor_tensor(R[:], w4(W[1][1], 0), four(GAM_, 1).to_broadcast(wide), ALU.mult).then_inc(small, 1)
                    dve.wait_ge(small, done(h, SM, 4))
                    dve.tensor_tensor(R[:], hv[:, 1:TILES:2, :], R[:], ALU.subtract).then_inc(small, 1)
                    dve.tensor_tensor(QS[:], w4(W[1][1], 128), four(GAM_, 1).to_broadcast(wide), ALU.mult).then_inc(small, 1)
                    dve.wait_ge(u_done, done(h, C, 2))
                    dve.tensor_tensor(DL[:, 1, :, :], w4(W[1][0], 0), four(B_, 1).to_broadcast(wide), ALU.mult).then_inc(small, 1)
                    dve.wait_ge(small, done(h, SM, 6))
                    dve.wait_ge(o_done, done(h, C, 2))
                    dve.tensor_tensor(o[:, 1:TILES:2, ds(h * D_V, D_V)], w4(W[1][0], 256), QS[:], ALU.add).then_inc(o_stored, 1)
                    dve.sem_inc(small, SM - 7)

            @block.gpsimd
            def _(pool):
                credit(pool, conv_picked, hp_copied, gm_done, em_done, eb_done, pow_done, *ot_done)
                pool.wait_ge(zeroed, 1)
                pool.wait_ge(conv_loaded, 32)
                with pool.Fori(0, D_H) as h:
                    pool.wait_ge(conv_done, done(h, 8, 0))
                    pool.tensor_copy(conv_w[:].rearrange("p (o m) k -> p o m k", o=1), conv_all[:, ds(h, 1), :, :]).then_inc(conv_picked, 1)
                    pool.wait_ge(o_stored, done(h, C, 0))
                    pool.tensor_copy(hp[:].rearrange("p (o k) t -> p o k t", o=1), par[:, ds(h, 1), :, :]).then_inc(hp_copied, 1)
                    pool.tensor_copy(hv[:].rearrange("p (o t) d -> p o t d", o=1), v[:, ds(h, 1), :, :]).then_inc(hp_copied, 1)
                    pool.wait_ge(hp_copied, done(h, 2, 2))
                    four = lambda x, c: hp[:, x, c:TILES:2].rearrange("p (b o) -> p b o", o=1).to_broadcast([P, BATCH, P])
                    all4 = lambda n: env.c(n).rearrange("p (o i) -> p o i", o=1).to_broadcast([P, BATCH, P])
                    for c in range(C):
                        pool.tensor_tensor(mats["gm"][c][:], all4("after"), four(G_, c), ALU.mult).then_inc(gm_done, 1)
                    for c in range(C):
                        pool.wait_ge(exp_done, done(h, C, c + 1))
                        pool.tensor_tensor(mats["Em"][c][:], mats["E"][c][:], all4("upto"), ALU.mult).then_inc(em_done, 1)
                        pool.wait_ge(em_done, done(h, C, c + 1))
                        pool.tensor_tensor(mats["Eb"][c][:], mats["Em"][c][:], four(B_, c), ALU.mult).then_inc(eb_done, 1)
                    for n in range(4):
                        m, c = divmod(n, 2)
                        r = rn[:, m, 4 * c:4 * c + 4]
                        pool.wait_ge(ssc_done, done(h, 4, n + 1))
                        pool.tensor_tensor(r, ssc[:, m, 4 * c:4 * c + 4], half[:, 0:4], ALU.pow).then_inc(pow_done, 1)
                        pool.wait_ge(pow_done, done(h, 8, 2 * n + 1))
                        pool.tensor_tensor(r, r, plus_half[:, 0:4], ALU.mult).then_inc(pow_done, 1)
                    for lv in range(NLEV):
                        for c in range(C):
                            if lv == 0:
                                pool.wait_ge(a_done, done(h, 2 * C, 2 * c + 2))
                            elif lv == 2:
                                pool.wait_ge(t_done[c], done(h, NLEV, 1))
                            if lv >= 3:
                                pool.wait_ge(x_done[c], done(h, NLEV - 1, lv - 2))
                            pool.tensor_tensor(OT[c][lv % 2][:], mats["AT"][c][:], all4(f"level{lv}"), ALU.mult).then_inc(ot_done[c], 1)


def delta_finish(nc, env, wo, norm_w, o, gate):
    with ExitStack() as ctx:
        sb, ps, sem = tools(nc, ctx, "df")
        wo_s, nw = sb("wo", [P, 3, DIM]), sb("nw", [P, D_V])
        sq, ms, half, rstd = sb("sq", [P, TILES, D_N]), sb("ms", [P, TILES * D_H]), sb("half", [P, TILES * D_H]), sb("rstd", [P, TILES * D_H])
        msc = sb("msc", [P, TILES * D_H])
        oT = sb("oT", [P, 2, 3, P])
        tp, po = ps("tp", [P, 2, 512]), ps("po", [P, 2, 512])
        loaded, squared, summed, scaled, half_done, rstd_done, normed, weighted, gated, turned, copied, out_done, added = (
            sem(n) for n in ("loaded", "squared", "summed", "scaled", "half_done", "rstd_done", "normed", "weighted", "gated", "turned", "copied", "out_done", "added"))
        by_head = lambda x: x.rearrange("p t (h d) -> p (t h) d", d=D_V)
        with nc.Block() as block:
            @block.sync
            def _(sp):
                sp.dma_start(wo_s[:], wo.rearrange("(m p) n -> p m n", p=P)).then_inc(loaded, 16)
                sp.dma_start(nw[:], norm_w.rearrange("(o d) -> o d", o=1).to_broadcast([P, D_V])).then_inc(loaded, 16)

            @block.vector
            def _(dve):
                dve.tensor_tensor(sq[:], o[:], o[:], ALU.mult).then_inc(squared, 1)
                dve.wait_ge(squared, 1)
                dve.tensor_reduce(ms[:], by_head(sq[:]), AX, ALU.add).then_inc(summed, 1)
                dve.wait_ge(summed, 1)
                dve.tensor_scalar(msc[:], ms[:], 1.0 / D_V, 1e-5, ALU.mult, ALU.add).then_inc(scaled, 1)
                dve.wait_ge(rstd_done, 1)
                for t in range(TILES):
                    r = rstd[:, D_H * t:D_H * t + D_H].rearrange("p (h o) -> p h o", o=1).to_broadcast([P, D_H, D_V])
                    oh = o[:, t, :].rearrange("p (h d) -> p h d", d=D_V)
                    dve.tensor_tensor(oh, oh, r, ALU.mult).then_inc(normed, 1)
                for t in range(TILES):
                    if t == 0:
                        dve.wait_ge(loaded, 32)
                    dve.wait_ge(normed, t + 1)
                    oh = o[:, t, :].rearrange("p (h d) -> p h d", d=D_V)
                    dve.tensor_tensor(oh, oh, nw[:].rearrange("p (o d) -> p o d", o=1).to_broadcast([P, D_H, D_V]), ALU.mult).then_inc(weighted, 1)
                for t in range(TILES + 1):
                    if t < TILES:
                        dve.wait_ge(turned, t + 1)
                        if t >= 2:
                            dve.wait_ge(out_done, t - 1)
                        dve.tensor_copy(oT[:, t % 2, :, :], tp[:, t % 2, 0:D_N].rearrange("p (m n) -> p m n", n=P)).then_inc(copied, 1)
                    if t >= 1:
                        dve.wait_ge(out_done, t)
                        dve.tensor_tensor(env.x[:, t - 1, :], env.x[:, t - 1, :], po[:, (t - 1) % 2, 0:DIM], ALU.add).then_inc(added, 1)

            @block.gpsimd
            def _(pool):
                pool.memset(half[:], -0.5).then_inc(half_done, 1)
                pool.wait_ge(half_done, 1)
                pool.wait_ge(scaled, 1)
                pool.tensor_tensor(rstd[:], msc[:], half[:], ALU.pow).then_inc(rstd_done, 1)
                for t in range(TILES):
                    pool.wait_ge(weighted, t + 1)
                    pool.tensor_tensor(o[:, t, :], o[:, t, :], gate[:, t, :], ALU.mult).then_inc(gated, 1)

            @block.tensor
            def _(pe):
                pe.wait_ge(loaded, 32)
                for t in range(TILES):
                    pe.wait_ge(gated, t + 1)
                    if t >= 2:
                        pe.wait_ge(copied, t - 1)
                    for m in range(3):
                        mm = pe.transpose(tp[:, t % 2, P * m:P * m + P], o[:, t, P * m:P * m + P], env.c("ident"))
                    mm.then_inc(turned, 1)
                    pe.wait_ge(copied, t + 1)
                    if t >= 2:
                        pe.wait_ge(added, t - 1)
                    for m in range(3):
                        mm = pe.matmul(po[:, t % 2, 0:DIM], oT[:, t % 2, m, :], wo_s[:, m, :], start=(m == 0), stop=(m == 2))
                    mm.then_inc(out_done, 1)


def delta_attention(nc, env, a):
    with ExitStack() as ctx:
        v = ctx.enter_context(nc.sbuf_tensor("d_v", [P, D_H, TILES, D_V], F32))
        gate = ctx.enter_context(nc.sbuf_tensor("d_gate", [P, TILES, D_N], F32))
        par = ctx.enter_context(nc.sbuf_tensor("d_par", [P, D_H, 4, TILES], F32))
        o = ctx.enter_context(nc.sbuf_tensor("d_o", [P, TILES, D_N], F32))
        delta_prepare(nc, env, a, v, gate, par)
        delta_heads(nc, env, a["L1_attn_Wq"], a["L1_attn_Wk"], a["L1_attn_conv_wq"], a["L1_attn_conv_wk"], v, par, o)
        delta_finish(nc, env, a["L1_attn_Wo"], a["L1_attn_norm_w"], o, gate)


def latent_attention(nc, env, ctxT, wq, wkcq, wqrT, wkrT, wkv, woT):
    NH = 2
    ITER = X_H // NH
    CH = TOKENS // 512
    H3 = CTX // 2
    with ExitStack() as ctx:
        sb, ps, sem = tools(nc, ctx, "la")
        kraw, kprod, kcos, kvT, kvt = sb("kraw", [CTX, TOKENS]), sb("kprod", [CTX, BATCH, SEQ]), sb("kcos", [CTX, BATCH, SEQ]), sb("kvT", [P, TOKENS]), sb("kvt", [P, TILES, CTX])
        w_q, w_kcq, w_qr, w_kr, w_kv, w_o = (sb("wq", [X_K, NH, DIM]), sb("wkcq", [X_K, NH, X_CQ]), sb("wqr", [X_R, NH, X_CQ]),
                                             sb("wkr", [X_R, NH, CTX]), sb("wkv", [X_K, NH, CTX]), sb("wo", [X_K, NH, DIM]))
        wabs, mabs, mo = sb("wabs", [P, NH, KC, X_CQ]), sb("mabs", [X_HALF, NH, 2, CTX]), sb("mo", [P, DIM])
        prod, qrot = sb("prod", [X_HALF, 2, 4, 512]), sb("qrot", [X_HALF, 2, 2, 512])
        qc = sb("qc", [P, NH, TOKENS])
        nmax, total, rec = sb("nmax", [P, NH, TILES]), sb("total", [P, NH, TILES]), sb("rec", [P, NH, TILES])
        e, en, eT = sb("e", [P, 2, 2, SEQ]), sb("en", [P, 2, 2, SEQ]), sb("eT", [P, 2, 4, P])
        cxT = sb("cxT", [P, TOKENS])
        qb, qcp, sc, tr, cxp = ps("qb", [P, 2, 512]), ps("qcp", [P, 512]), ps("sc", [P, 2, 2, SEQ]), ps("tr", [P, 512]), ps("cxp", [P, 2, 512])
        flat = sc[:].rearrange("p a n l -> p a (n l)")
        loaded, k_done, k_rot, kt_done, kt_copied = (sem(n) for n in ("loaded", "k_done", "k_rot", "kt_done", "kt_copied"))
        w_loaded, absorbed, mo_done, qb_done, qc_done, sc_done, tr_done, cx_done, po_done = (
            sem(n) for n in ("w_loaded", "absorbed", "mo_done", "qb_done", "qc_done", "sc_done", "tr_done", "cx_done", "po_done"))
        absorbed_copied, qc_copied, exp_done, eT_copied = (sem(n) for n in ("absorbed_copied", "qc_copied", "exp_done", "eT_copied"))
        mo_copied, rope_done, max_done, rec_done, normed, cx_copied, added, rotated, padded = (
            sem(n) for n in ("mo_copied", "rope_done", "max_done", "rec_done", "normed", "cx_copied", "added", "rotated", "padded"))
        ORDER = ("w0 q00 w1 q01 l00 s0 s1 n0 n1 q10 l01 t0 s2 a0 t1 s3 n2 l10 a1 t2 n3 q11 a2 t3 s4 n4 s5 n5 a3 "
                 "l11 t4 s6 n6 a4 t5 s7 n7 a5 t6 o0 a6 t7 o1 a7 o2 o3").split()
        NT = NH * BATCH

        with nc.Block() as block:
            @block.sync
            def _(sp):
                sp.dma_start(kraw[:], ctxT).then_inc(loaded, 16)
                with sp.Fori(0, ITER) as i:
                    head = sp.snap(i * NH)
                    sp.wait_ge(mo_done, done(i, NH, 0))
                    for dst, src in ((w_q, wq.rearrange("(h p) n -> p h n", p=X_K)), (w_kcq, wkcq.rearrange("h p n -> p h n")),
                                     (w_qr, wqrT.rearrange("h p n -> p h n")), (w_kr, wkrT.rearrange("h p n -> p h n")),
                                     (w_kv, wkv.rearrange("h p n -> p h n")), (w_o, woT.rearrange("(h p) n -> p h n", p=X_K))):
                        sp.dma_start(dst[:], src[:, ds(head, NH), :]).then_inc(w_loaded, 16)

            @block.tensor
            def _(pe):
                credit(pe, absorbed, mo_done, qb_done, qc_done, sc_done, tr_done, cx_done, po_done)
                pe.wait_ge(k_rot, 1)
                for t in range(TILES):
                    mm = pe.transpose(qb[:, 0, CTX * t:CTX * t + CTX], kvT[0:CTX, P * t:P * t + P], env.c("ident")[0:CTX, 0:CTX])
                mm.then_inc(kt_done, 1)
                pe.wait_ge(kt_copied, 1)
                pe.wait_ge(padded, 1)
                with pe.Fori(0, ITER) as i:
                    pe.wait_ge(w_loaded, i * 96 + 96)

                    def absorb(a):
                        pe.wait_ge(exp_done, done(i, NT, 0))
                        for k in range(KC):
                            pe.matmul(flat[:, a, X_CQ * k:X_CQ * k + X_CQ], w_q[:, a, P * k:P * k + P], w_kcq[:, a, :], start=True, stop=True)
                        for n in range(2):
                            mm = pe.matmul(flat[0:X_HALF, a, 384 + CTX * n:384 + CTX * n + CTX], w_qr[:, a, X_HALF * n:X_HALF * n + X_HALF], w_kr[:, a, :], start=True, stop=True)
                        mm.then_inc(absorbed, 1)
                        pe.wait_ge(qc_copied, done(i, 2 * NH, 0))
                        pe.wait_ge(mo_copied, done(i, NH, a))
                        pe.matmul(qcp[CTX * a:CTX * a + CTX, 0:DIM], w_kv[:, a, :], w_o[:, a, :], start=True, stop=True).then_inc(mo_done, 1)

                    def queries(a, c):
                        pe.wait_ge(absorbed_copied, done(i, NH, a + 1))
                        pe.wait_ge(rope_done, done(i, 2 * NH, 2 * a + c))
                        pe.wait_ge(added, done(i, BATCH, 0))
                        for n in range(2):
                            for k in range(KC):
                                mm = pe.matmul(qb[0:X_HALF, n, :], wabs[:, a, k, X_HALF * n:X_HALF * n + X_HALF], env.xT[:, k, 512 * c:512 * c + 512], start=(k == 0), stop=(k == KC - 1))
                        mm.then_inc(qb_done, 1)

                    def latent_queries(a, c):
                        pe.wait_ge(rotated, done(i, 4 * NH, 4 * a + 2 * c + 2))
                        pe.wait_ge(qc_copied, done(i, 2 * NH, 2 * a + c))
                        pe.wait_ge(mo_copied, done(i, NH, NH))
                        for n in range(2):
                            mm = pe.matmul(qcp[0:CTX, :], mabs[:, a, n, :], qrot[:, c, n, :], start=(n == 0), stop=(n == 1))
                        mm.then_inc(qc_done, 1)

                    def scores(a, b):
                        u = BATCH * a + b
                        pe.wait_ge(qc_copied, done(i, 2 * NH, 2 * a + b // 2 + 1))
                        pe.wait_ge(exp_done, done(i, NT, u - 1))
                        if u < 2:
                            pe.wait_ge(absorbed_copied, done(i, NH, NH))
                        for n in range(2):
                            t = 2 * b + n
                            mm = pe.matmul(sc[:, u % 2, n, :], qc[:, a, P * t:P * t + P], kvT[:, SEQ * b:SEQ * b + SEQ], start=True, stop=True)
                        mm.then_inc(sc_done, 1)

                    def turn(a, b):
                        u = BATCH * a + b
                        pe.wait_ge(normed, done(i, NT, u + 1))
                        pe.wait_ge(eT_copied, done(i, NT, u))
                        for l in range(2):
                            for n in range(2):
                                mm = pe.transpose(tr[:, P * (2 * l + n):P * (2 * l + n) + P], en[:, u % 2, n, P * l:P * l + P], env.c("ident"))
                        mm.then_inc(tr_done, 1)

                    def attend(a, b):
                        u = BATCH * a + b
                        pe.wait_ge(eT_copied, done(i, NT, u + 1))
                        if u == 0:
                            pe.wait_ge(cx_copied, done(i, 2, 0))
                        for l in range(2):
                            mm = pe.matmul(cxp[CTX * a:CTX * a + CTX, b // 2, SEQ * (b % 2):SEQ * (b % 2) + SEQ], kvt[:, 2 * b + l, :],
                                           eT[:, u % 2, 2 * l:2 * l + 2, :].rearrange("p n q -> p (n q)"), start=(l == 0), stop=(l == 1))
                        mm.then_inc(cx_done, 1)

                    def outputs(b):
                        pe.wait_ge(rope_done, done(i, 2 * NH, 2 * NH))
                        pe.wait_ge(cx_copied, done(i, 2, b // 2 + 1))
                        pe.wait_ge(added, done(i, BATCH, b - 1))
                        for n in range(2):
                            t = 2 * b + n
                            mm = pe.matmul(qb[:, b % 2, DIM * n:DIM * n + DIM], cxT[:, P * t:P * t + P], mo[:], start=True, stop=True)
                        mm.then_inc(po_done, 1)

                    for kind, *at in ORDER:
                        at = [int(x) for x in at]
                        if kind == "q":
                            queries(*at)
                        elif kind == "l":
                            latent_queries(*at)
                        elif kind == "o":
                            outputs(*at)
                        elif kind == "w":
                            absorb(*at)
                        elif kind != "n":
                            {"s": scores, "t": turn, "a": attend}[kind](*divmod(at[0], BATCH))

            @block.scalar
            def _(act):
                credit(act, absorbed_copied, qc_copied, exp_done, eT_copied)
                with act.Fori(0, ITER) as i:
                    def copy_absorbed(a):
                        act.wait_ge(absorbed, done(i, NH, a + 1))
                        act.copy(wabs[:, a, :, :], flat[:, a, 0:2 * X_CQ].rearrange("p (k n) -> p k n", k=KC))
                        act.copy(mabs[:, a, :, :], flat[0:X_HALF, a, 2 * X_CQ:512].rearrange("p (k n) -> p k n", k=2)).then_inc(absorbed_copied, 1)

                    def copy_qc(a, c):
                        act.wait_ge(qc_done, done(i, 2 * NH, 2 * a + c + 1))
                        act.copy(qc[0:CTX, a, 512 * c:512 * c + 512], qcp[0:CTX, :]).then_inc(qc_copied, 1)

                    def exp(u):
                        a, b = divmod(u, BATCH)
                        act.wait_ge(max_done, done(i, NT, u + 1))
                        act.wait_ge(normed, done(i, NT, u - 1))
                        for n in range(2):
                            t = 2 * b + n
                            ins = act.activation(e[:, u % 2, n, :], sc[:, u % 2, n, :], ACT.Exp, bias=nmax[:, a, t:t + 1], accum_out=total[:, a, t:t + 1])
                        ins.then_inc(exp_done, 1)

                    def copy_eT(u):
                        act.wait_ge(tr_done, done(i, NT, u + 1))
                        act.wait_ge(cx_done, done(i, NT, u - 1))
                        act.copy(eT[:, u % 2, :, :], tr[:].rearrange("p (n l) -> p n l", n=4)).then_inc(eT_copied, 1)

                    for kind, *at in ORDER:
                        at = [int(x) for x in at]
                        if kind == "w":
                            copy_absorbed(*at)
                        elif kind == "l":
                            copy_qc(*at)
                        elif kind == "s":
                            exp(*at)
                        elif kind == "t":
                            copy_eT(*at)

            @block.vector
            def _(dve):
                credit(dve, mo_copied, rope_done, max_done, rec_done, normed, cx_copied, added)
                dve.memset(kvT[CTX:P, :], 0.0)
                dve.memset(qc[CTX:P, :, :], 0.0).then_inc(padded, 1)
                dve.wait_ge(loaded, 16)
                per_batch = lambda x: x.rearrange("p (o t) -> p o t", o=1).to_broadcast([H3, BATCH, SEQ])
                kr = kraw[:].rearrange("p (b t) -> p b t", t=SEQ)
                for lo in (0, H3):
                    dve.tensor_tensor(kcos[lo:lo + H3, :, :], kr[lo:lo + H3, :, :], per_batch(env.c("k_cos")[lo:lo + H3, :]), ALU.mult)
                    dve.tensor_tensor(kprod[H3 - lo:2 * H3 - lo, :, :], kr[lo:lo + H3, :, :], per_batch(env.c("k_sin")[lo:lo + H3, :]), ALU.mult).then_inc(k_done, 1)
                dve.wait_ge(k_done, 2)
                dve.tensor_tensor(kvT[0:CTX, :].rearrange("p (b t) -> p b t", t=SEQ), kcos[:], kprod[:], ALU.add).then_inc(k_rot, 1)
                dve.wait_ge(kt_done, 1)
                dve.tensor_copy(kvt[:], qb[:, 0, :].rearrange("p (t d) -> p t d", d=CTX)).then_inc(kt_copied, 1)
                with dve.Fori(0, ITER) as i:
                    def copy_mo(a):
                        dve.wait_ge(mo_done, done(i, NH, a + 1))
                        if a == 0:
                            dve.wait_ge(po_done, done(i, BATCH, 0))
                        dve.tensor_copy(mo[CTX * a:CTX * a + CTX, :], qcp[CTX * a:CTX * a + CTX, 0:DIM]).then_inc(mo_copied, 1)

                    def rope(a, c):
                        dve.wait_ge(qb_done, done(i, 2 * NH, 2 * a + c + 1))
                        dve.wait_ge(rotated, done(i, 4 * NH, 2 * (2 * a + c - 1)))
                        for j, (n, tab) in enumerate(((0, "x_cos0"), (1, "x_sin0"), (1, "x_cos1"), (0, "x_sin1"))):
                            ins = dve.tensor_tensor(prod[:, c, j, :], qb[0:X_HALF, n, :], env.c(tab)[0:X_HALF, :], ALU.mult)
                        ins.then_inc(rope_done, 1)

                    def maximum(u):
                        a, b = divmod(u, BATCH)
                        dve.wait_ge(sc_done, done(i, NT, u + 1))
                        dve.tensor_reduce(nmax[:, a, 2 * b:2 * b + 2], sc[:, u % 2, :, :], AX, ALU.max, negate=True).then_inc(max_done, 1)

                    def norm(u):
                        a, b = divmod(u, BATCH)
                        dve.wait_ge(exp_done, done(i, NT, u + 1))
                        dve.reciprocal(rec[:, a, 2 * b:2 * b + 2], total[:, a, 2 * b:2 * b + 2]).then_inc(rec_done, 1)
                        dve.wait_ge(rec_done, done(i, NT, u + 1))
                        dve.wait_ge(tr_done, done(i, NT, u - 1))
                        for n in range(2):
                            ins = dve.tensor_scalar(en[:, u % 2, n, :], e[:, u % 2, n, :], rec[:, a, 2 * b + n:2 * b + n + 1], None, ALU.mult)
                        ins.then_inc(normed, 1)

                    def copy_cx(g):
                        dve.wait_ge(cx_done, done(i, NT, BATCH + 2 * g + 2))
                        dve.tensor_copy(cxT[:, 512 * g:512 * g + 512], cxp[:, g, :]).then_inc(cx_copied, 1)

                    def add(b):
                        dve.wait_ge(po_done, done(i, BATCH, b + 1))
                        dve.tensor_tensor(env.x[:, 2 * b:2 * b + 2, :], env.x[:, 2 * b:2 * b + 2, :], qb[:, b % 2, :].rearrange("p (n c) -> p n c", n=2), ALU.add).then_inc(added, 1)

                    for kind, *at in ORDER:
                        at = [int(x) for x in at]
                        if kind == "w":
                            copy_mo(*at)
                        elif kind == "q":
                            rope(*at)
                        elif kind == "s":
                            maximum(*at)
                        elif kind == "n":
                            norm(*at)
                        elif kind == "a" and at[0] in (BATCH + 1, BATCH + 3):
                            copy_cx((at[0] - BATCH) // 2)
                        elif kind == "o":
                            add(*at)

            @block.gpsimd
            def _(pool):
                credit(pool, rotated)
                with pool.Fori(0, ITER) as i:
                    for a in range(NH):
                        for c in range(CH):
                            pool.wait_ge(rope_done, done(i, 2 * NH, 2 * a + c + 1))
                            pool.wait_ge(qc_done, done(i, 2 * NH, 2 * a + c - 1))
                            for n in range(2):
                                pool.tensor_tensor(qrot[:, c, n, :], prod[:, c, 2 * n, :], prod[:, c, 2 * n + 1, :], ALU.add).then_inc(rotated, 1)


def gate_projections(nc, env, sim, gates, w_table, wT):
    MIN, OFF = 2, 1e9
    with ExitStack() as ctx:
        sb, ps, sem = tools(nc, ctx, "fg")
        sim_s, sim2, thr_in, thr = sb("sim", [P, KC, F_E]), sb("sim2", [P, KC, F_E]), sb("thr_in", [P, F_E]), sb("thr", [P, F_E])
        xsq, xss = sb("xsq", [P, 2, DIM]), sb("xss", [P, TILES])
        norms, half, inv = sb("norms", [P, TILES + F_E]), sb("half", [P, TILES + F_E]), sb("inv", [P, TILES + F_E])
        lg, lpad, l8, lrep, fb = sb("lg", [P, TILES, F_E]), sb("lpad", [P, TILES, F_E + 8]), sb("l8", [P, TILES, 8]), sb("lrep", [P, TILES, F_E + 8]), sb("fb", [P, TILES, F_E])
        gated, on, cnt, idle, m, off = (sb("gated", [P, TILES, F_E]), sb("on", [P, TILES, F_E]), sb("cnt", [P, TILES]), sb("idle", [P, TILES]), sb("m", [P, TILES, F_E]), sb("off", [P, TILES, F_E]))
        mx, ex, tot, w = sb("mx", [P, TILES]), sb("ex", [P, TILES, F_E]), sb("tot", [P, TILES]), sb("w", [P, TILES, F_E])
        rp, tp = ps("rp", [P, TILES + 1, F_E]), ps("tp", [F_E, 2, 512])
        loaded, sim_sq, raw_done, sq_done, sig_done, pow_done, exp_done, turned, wT_copied, stored, norms_done, sub_done, w_done, step = (
            sem(n) for n in ("loaded", "sim_sq", "raw_done", "sq_done", "sig_done", "pow_done", "exp_done", "turned", "wT_copied", "stored", "norms_done", "sub_done", "w_done", "step"))
        with nc.Block() as block:
            @block.sync
            def _(sp):
                sp.dma_start(sim_s[:], sim.rearrange("(k p) n -> p k n", p=P)).then_inc(loaded, 16)
                sp.dma_start(thr_in[:], gates.rearrange("(o d) -> o d", o=1).to_broadcast([P, F_E])).then_inc(loaded, 16)
                sp.wait_ge(wT_copied, 2)
                sp.dma_start(w_table, wT[:]).then_inc(stored, 16)
                sp.wait_ge(stored, 16)

            @block.tensor
            def _(pe):
                pe.wait_ge(loaded, 32)
                for t in range(TILES):
                    for k in range(KC):
                        pe.matmul(rp[:, t, :], env.xT[:, k, P * t:P * t + P], sim_s[:, k, :], start=(k == 0), stop=(k == KC - 1))
                pe.wait_ge(sim_sq, 1)
                for k in range(KC):
                    mm = pe.matmul(rp[:, TILES, :], env.c("ones"), sim2[:, k, :], start=(k == 0), stop=(k == KC - 1))
                mm.then_inc(raw_done, 1)
                pe.wait_ge(w_done, 1)
                for t in range(TILES):
                    mm = pe.transpose(tp[:, t // 4, P * (t % 4):P * (t % 4) + P], w[:, t, :], env.c("ident"))
                    if t % 4 == 3:
                        mm.then_inc(turned, 1)

            @block.scalar
            def _(act):
                act.wait_ge(loaded, 32)
                act.activation(thr[:], thr_in[:], ACT.Sigmoid).then_inc(sig_done, 1)
                for t in range(TILES):
                    if t >= 2:
                        act.wait_ge(sq_done, t - 1)
                    act.activation(xsq[:, t % 2, :], env.x[:, t, :], ACT.Square, accum_out=xss[:, t:t + 1]).then_inc(sq_done, 1)
                act.wait_ge(sub_done, 1)
                act.activation(ex[:], ex[:], ACT.Exp).then_inc(exp_done, 1)

            @block.gpsimd
            def _(pool):
                pool.wait_ge(norms_done, 1)
                pool.tensor_tensor(inv[:], norms[:], half[:], ALU.pow).then_inc(pow_done, 1)

            @block.vector
            def _(dve):
                count = [0]

                def chain(ins):
                    count[0] += 1
                    ins.then_inc(step, 1)
                    dve.wait_ge(step, count[0])

                experts = lambda a: a.rearrange("p (t o) -> p t o", o=1).to_broadcast([P, TILES, F_E])
                rows = lambda a: a.rearrange("p (o e) -> p o e", o=1).to_broadcast([P, TILES, F_E])
                dve.memset(half[:], -0.5)
                dve.memset(lpad[:], NEG)
                dve.wait_ge(loaded, 32)
                dve.tensor_tensor(sim2[:], sim_s[:], sim_s[:], ALU.mult).then_inc(sim_sq, 1)
                dve.wait_ge(raw_done, 1)
                dve.wait_ge(sq_done, TILES)
                dve.tensor_scalar(norms[:, 0:TILES], xss[:], 1e-24, None, ALU.max)
                chain(dve.tensor_scalar(norms[:, TILES:], rp[:, TILES, :], 1e-24, None, ALU.max))
                dve.sem_inc(norms_done, 1)
                dve.wait_ge(pow_done, 1)
                chain(dve.tensor_tensor(lg[:], rp[:, 0:TILES, :], experts(inv[:, 0:TILES]), ALU.mult))
                chain(dve.tensor_tensor(lg[:], lg[:], rows(inv[:, TILES:]), ALU.mult))
                dve.wait_ge(sig_done, 1)
                chain(dve.tensor_tensor(lpad[:, :, 0:F_E], lg[:], rows(thr[:]), ALU.subtract))
                l = lpad[:, :, 0:F_E]
                for t in range(TILES):
                    chain(dve.max(l8[:, t, :], lpad[:, t, :]))
                chain(dve.memset(l8[:, :, MIN:8], NEG))
                for t in range(TILES):
                    chain(dve.match_replace(lrep[:, t, :], l8[:, t, :], lpad[:, t, :], NEG))
                chain(dve.tensor_tensor(fb[:], lrep[:, :, 0:F_E], l, ALU.not_equal))
                chain(dve.tensor_scalar(gated[:], l, 0.0, None, ALU.max))
                chain(dve.tensor_scalar(on[:], gated[:], 0.0, None, ALU.is_gt))
                chain(dve.tensor_reduce(cnt[:], on[:], AX, ALU.add))
                chain(dve.tensor_scalar(idle[:], cnt[:], 0.0, None, ALU.is_equal))
                chain(dve.tensor_tensor(m[:], fb[:], experts(idle[:]), ALU.mult))
                chain(dve.tensor_tensor(m[:], m[:], on[:], ALU.max))
                chain(dve.tensor_scalar(off[:], m[:], OFF, -OFF, ALU.mult, ALU.add))
                chain(dve.tensor_tensor(gated[:], gated[:], m[:], ALU.mult))
                chain(dve.tensor_tensor(gated[:], gated[:], off[:], ALU.add))
                chain(dve.tensor_reduce(mx[:], gated[:], AX, ALU.max))
                chain(dve.tensor_tensor(ex[:], gated[:], experts(mx[:]), ALU.subtract))
                dve.sem_inc(sub_done, 1)
                dve.wait_ge(exp_done, 1)
                chain(dve.tensor_reduce(tot[:], ex[:], AX, ALU.add))
                chain(dve.reciprocal(tot[:], tot[:]))
                chain(dve.tensor_tensor(w[:], ex[:], experts(tot[:]), ALU.mult))
                chain(dve.tensor_tensor(w[:], w[:], m[:], ALU.mult))
                dve.sem_inc(w_done, 1)
                for n in range(2):
                    dve.wait_ge(turned, n + 1)
                    dve.tensor_copy(wT[:, 512 * n:512 * n + 512], tp[:, n, :]).then_inc(wT_copied, 1)


def mixed_attention(nc, env, w_table, wq, wk, wv, wo):
    SCALE = float(F_H) ** -0.5
    with ExitStack() as ctx:
        sb, ps, sem = tools(nc, ctx, "fa")
        wb = sb("wb", [P, F_E, TOKENS])
        qkv, vt, aT = sb("qkv", [P, 3, TOKENS]), sb("vt", [P, TILES, F_H]), sb("aT", [P, TOKENS])
        wb_loaded = sem("wb_loaded")
        with ExitStack() as inner:
            sb, ps, sem = tools(nc, inner, "fp")
            w_s, xe = sb("w", [P, 2, 3, KC, F_H]), sb("xe", [P, 2, KC, TOKENS])
            acc = ps("acc", [P, 3, 2, 512])
            w_loaded, scaled, projected, copied = [sem("w_loaded0"), sem("w_loaded1")], sem("scaled"), sem("projected"), sem("copied")
            PAIRS = F_E // 2
            with nc.Block() as block:
                @block.gpsimd
                def _(pool):
                    for n in range(4):
                        pool.dma_start(wb[:, 4 * n:4 * n + 4, :], w_table[4 * n:4 * n + 4, :].rearrange("(o e) t -> o e t", o=1).to_broadcast([P, 4, TOKENS])).then_inc(wb_loaded, 16)
                    pool.wait_ge(wb_loaded, 64)

                @block.sync
                def _(sp):
                    with sp.Fori(0, PAIRS) as i:
                        pair = sp.snap(i * 2)
                        for s in range(2):
                            sp.wait_ge(projected, done(i, 2, s - 1))
                            for m, w in enumerate((wq, wk, wv)):
                                sp.dma_start(w_s[:, s, m, :, :], w.rearrange("e (k p) h -> p e k h", p=P)[:, ds(pair + s, 1), :, :].rearrange("p e k h -> p (e k) h")).then_inc(w_loaded[s], 16)

                @block.vector
                def _(dve):
                    credit(dve, scaled)
                    dve.wait_ge(wb_loaded, 64)
                    with dve.Fori(0, PAIRS) as i:
                        for s in range(2):
                            dve.wait_ge(projected, done(i, 2, s - 1))
                            dve.tensor_tensor(xe[:, s, :, :], env.xT[:], wb[:, ds(i * 2 + s, 1), :].to_broadcast([P, KC, TOKENS]), ALU.mult).then_inc(scaled, 1)
                    for n in range(6):
                        dve.wait_ge(projected, CREDIT + F_E)
                        dve.tensor_copy(qkv[:, n // 2, 512 * (n % 2):512 * (n % 2) + 512], acc[:, n // 2, n % 2, :]).then_inc(copied, 1)

                @block.tensor
                def _(pe):
                    credit(pe, projected)

                    def expert(i, s, first, last):
                        pe.wait_ge(w_loaded[s], i * 48 + 48)
                        pe.wait_ge(scaled, done(i, 2, s + 1))
                        for m in range(3):
                            for k in range(KC):
                                for c in range(2):
                                    mm = pe.matmul(acc[:, m, c, :], w_s[:, s, m, k, :], xe[:, s, k, 512 * c:512 * c + 512], start=first and k == 0, stop=last and k == KC - 1)
                        mm.then_inc(projected, 1)

                    expert(0, 0, True, False)
                    expert(0, 1, False, False)
                    with pe.Fori(1, PAIRS - 1) as i:
                        expert(i, 0, False, False)
                        expert(i, 1, False, False)
                    expert(PAIRS - 1, 0, False, False)
                    expert(PAIRS - 1, 1, False, True)
        with ExitStack() as inner:
            sb, ps, sem = tools(nc, inner, "fc")
            sm, mx, e, tot, rec, pn, pT = (sb("sm", [P, 2, 2, SEQ]), sb("mx", [P, TILES]), sb("e", [P, 2, 2, SEQ]), sb("tot", [P, TILES]),
                                           sb("rec", [P, TILES]), sb("pn", [P, 2, 2, SEQ]), sb("pT", [P, 2, 4, P]))
            nmx = sb("nmx", [P, TILES])
            tv, sc, tr, ap_ = ps("tv", [P, 2, 512]), ps("sc", [P, 2, 2, SEQ]), ps("tr", [P, 2, 512]), ps("ap", [P, 2, 512])
            v_turned, v_copied, sc_done, masked, max_done, scaled, exp_done, rec_done, normed, turned, copied, a_done, a_copied = (
                sem(n) for n in ("v_turned", "v_copied", "sc_done", "masked", "max_done", "scaled", "exp_done", "rec_done", "normed", "turned", "copied", "a_done", "a_copied"))
            q, k, v = qkv[:, 0, :], qkv[:, 1, :], qkv[:, 2, :]
            with nc.Block() as block:
                @block.tensor
                def _(pe):
                    for n in range(2):
                        for j in range(4):
                            t = 4 * n + j
                            mm = pe.transpose(tv[:, n, P * j:P * j + P], v[:, P * t:P * t + P], env.c("ident"))
                        mm.then_inc(v_turned, 1)
                    for u in range(BATCH + 2):
                        if u < BATCH:
                            if u >= 2:
                                pe.wait_ge(masked, 2 * (u - 1))
                            for n in range(2):
                                t = 2 * u + n
                                mm = pe.matmul(sc[:, u % 2, n, :], q[:, P * t:P * t + P], k[:, SEQ * u:SEQ * u + SEQ], start=True, stop=True)
                            mm.then_inc(sc_done, 1)
                        if 1 <= u <= BATCH:
                            w = u - 1
                            pe.wait_ge(normed, 2 * w + 2)
                            if w >= 2:
                                pe.wait_ge(copied, w - 1)
                            for n in range(2):
                                for l in range(2):
                                    mm = pe.transpose(tr[:, w % 2, P * (2 * l + n):P * (2 * l + n) + P], pn[:, w % 2, n, P * l:P * l + P], env.c("ident"))
                            mm.then_inc(turned, 1)
                        if u >= 2:
                            w = u - 2
                            pe.wait_ge(copied, w + 1)
                            pe.wait_ge(v_copied, 2)
                            if w >= 2:
                                pe.wait_ge(a_copied, w - 1)
                            for l in range(2):
                                mm = pe.matmul(ap_[:, w % 2, 0:SEQ], vt[:, 2 * w + l, :], pT[:, w % 2, 2 * l:2 * l + 2, :].rearrange("p n q -> p (n q)"), start=(l == 0), stop=(l == 1))
                            mm.then_inc(a_done, 1)

                @block.scalar
                def _(act):
                    for u in range(BATCH + 1):
                        if u < BATCH:
                            act.wait_ge(scaled, u + 1)
                            if u >= 2:
                                act.wait_ge(normed, 2 * (u - 1))
                            for n in range(2):
                                t = 2 * u + n
                                ins = act.activation(e[:, u % 2, n, :], sm[:, u % 2, n, :], ACT.Exp, bias=nmx[:, t:t + 1], scale=SCALE, accum_out=tot[:, t:t + 1])
                            ins.then_inc(exp_done, 1)
                        if u >= 1:
                            w = u - 1
                            act.wait_ge(turned, w + 1)
                            if w >= 2:
                                act.wait_ge(a_done, w - 1)
                            act.copy(pT[:, w % 2, :, :], tr[:, w % 2, :].rearrange("p (n l) -> p n l", n=4)).then_inc(copied, 1)

                @block.vector
                def _(dve):
                    for n in range(2):
                        dve.wait_ge(v_turned, n + 1)
                        dve.tensor_copy(vt[:, 4 * n:4 * n + 4, :], tv[:, n, :].rearrange("p (j h) -> p j h", j=4)).then_inc(v_copied, 1)
                    mask = env.c("f_mask")
                    for u in range(BATCH + 1):
                        if u < BATCH:
                            dve.wait_ge(sc_done, u + 1)
                            if u >= 2:
                                dve.wait_ge(exp_done, u - 1)
                            for n in range(2):
                                for l in range(2):
                                    src = mask[:, P:SEQ] if l == n else mask[:, 0:P]
                                    if n == 0 and l == 1:
                                        ins = dve.tensor_scalar(sm[:, u % 2, n, P:SEQ], sc[:, u % 2, n, P:SEQ], 0.0, NEG, ALU.mult, ALU.add)
                                    else:
                                        ins = dve.tensor_tensor(sm[:, u % 2, n, P * l:P * l + P], sc[:, u % 2, n, P * l:P * l + P], src, ALU.add)
                                ins.then_inc(masked, 1)
                            dve.wait_ge(masked, 2 * u + 2)
                            dve.tensor_reduce(mx[:, 2 * u:2 * u + 2], sm[:, u % 2, :, :], AX, ALU.max, negate=True).then_inc(max_done, 1)
                            dve.wait_ge(max_done, u + 1)
                            dve.tensor_scalar(nmx[:, 2 * u:2 * u + 2], mx[:, 2 * u:2 * u + 2], SCALE, None, ALU.mult).then_inc(scaled, 1)
                        if u >= 1:
                            w = u - 1
                            dve.wait_ge(exp_done, w + 1)
                            dve.reciprocal(rec[:, 2 * w:2 * w + 2], tot[:, 2 * w:2 * w + 2]).then_inc(rec_done, 1)
                            dve.wait_ge(rec_done, w + 1)
                            if w >= 2:
                                dve.wait_ge(turned, w - 1)
                            for n in range(2):
                                t = 2 * w + n
                                dve.tensor_scalar(pn[:, w % 2, n, :], e[:, w % 2, n, :], rec[:, t:t + 1], None, ALU.mult).then_inc(normed, 1)
                    for u in range(BATCH):
                        dve.wait_ge(a_done, u + 1)
                        dve.tensor_copy(aT[:, SEQ * u:SEQ * u + SEQ], ap_[:, u % 2, 0:SEQ]).then_inc(a_copied, 1)
        with ExitStack() as inner:
            sb, ps, sem = tools(nc, inner, "fo")
            w_s, ae = sb("w", [P, 2, DIM]), sb("ae", [P, 2, TOKENS])
            acc = ps("acc", [P, TILES, 512])
            w_loaded, scaled, out_done, added = [sem("w_loaded0"), sem("w_loaded1")], sem("scaled"), sem("out_done"), sem("added")
            PAIRS = F_E // 2
            with nc.Block() as block:
                @block.sync
                def _(sp):
                    with sp.Fori(0, PAIRS) as i:
                        pair = sp.snap(i * 2)
                        for s in range(2):
                            sp.wait_ge(out_done, done(i, 2, s - 1))
                            sp.dma_start(w_s[:, s, :].rearrange("p (o n) -> p o n", o=1), wo.rearrange("e p n -> p e n")[:, ds(pair + s, 1), :]).then_inc(w_loaded[s], 16)

                @block.vector
                def _(dve):
                    credit(dve, scaled)
                    with dve.Fori(0, PAIRS) as i:
                        for s in range(2):
                            dve.wait_ge(out_done, done(i, 2, s - 1))
                            dve.tensor_tensor(ae[:, s, :].rearrange("p (o t) -> p o t", o=1), aT[:].rearrange("p (o t) -> p o t", o=1), wb[:, ds(i * 2 + s, 1), :], ALU.mult).then_inc(scaled, 1)
                    dve.wait_ge(out_done, CREDIT + F_E)
                    for t in range(TILES):
                        dve.tensor_tensor(env.x[:, t, :], env.x[:, t, :], acc[:, t, 0:DIM], ALU.add).then_inc(added, 1)

                @block.tensor
                def _(pe):
                    credit(pe, out_done)

                    def expert(i, s, first, last):
                        pe.wait_ge(w_loaded[s], i * 16 + 16)
                        pe.wait_ge(scaled, done(i, 2, s + 1))
                        for t in range(TILES):
                            mm = pe.matmul(acc[:, t, 0:DIM], ae[:, s, P * t:P * t + P], w_s[:, s, :], start=first, stop=last)
                        mm.then_inc(out_done, 1)

                    expert(0, 0, True, False)
                    expert(0, 1, False, False)
                    with pe.Fori(1, PAIRS - 1) as i:
                        expert(i, 0, False, False)
                        expert(i, 1, False, False)
                    expert(PAIRS - 1, 0, False, False)
                    expert(PAIRS - 1, 1, False, True)


def mixture_attention(nc, env, a, w_table):
    with ExitStack() as ctx:
        wT = ctx.enter_context(nc.sbuf_tensor("f_wT", [F_E, TOKENS], F32))
        gate_projections(nc, env, a["L1_ffn_sim_matrix"], a["L1_ffn_gates"], w_table, wT)
        mixed_attention(nc, env, w_table, a["L1_ffn_q_proj"], a["L1_ffn_k_proj"], a["L1_ffn_v_proj"], a["L1_ffn_o_proj"])


def build(nc, a, const_at, out):
    slot_x = nc.dram_tensor("slot_x", [1 + M_SLOTS, DIM], F32).ap()
    out_rows = nc.dram_tensor("out_rows", [1 + M_SLOTS, DIM], F32).ap()
    w_table = nc.dram_tensor("w_table", [F_E, TOKENS], F32).ap()
    with ExitStack() as ctx:
        env = Env(nc, ctx, const_at)
        load_inputs(nc, env, a["x"], a["const"])
        window_attention(nc, env, a["L0_attn_q_kernel"], a["L0_attn_k_kernel"], a["L0_attn_v_kernel"], a["L0_attn_out_kernel"])
        normalize(nc, env, "n0")
        softmax_cross(nc, env, a["ctxT"], a["L0_xattn_W_kT"], a["L0_xattn_b_k"], a["L0_xattn_ln_gamma"], a["L0_xattn_ln_beta"])
        normalize(nc, env, "n1")
        routed_experts(nc, env, a, slot_x, out_rows)
        normalize(nc, env, "n2")
        delta_attention(nc, env, a)
        normalize(nc, env, "n3")
        latent_attention(nc, env, a["ctxT"], a["L1_xattn_Wq"], a["L1_xattn_w_kc_q"], a["L1_xattn_W_qrT"], a["L1_xattn_W_krT"], a["L1_xattn_w_kc_kv"], a["L1_xattn_WoT"])
        normalize(nc, env, "n4")
        mixture_attention(nc, env, a, w_table)
        normalize(nc, env, "n5", out)


def kernel(**inputs):
    import concourse.bacc as bacc
    from concourse.bass_utils import run_bass_kernel_spmd

    given = {k: np.asarray(v) for k, v in inputs.items()}
    turned = {
        "ctxT": given.pop("ctx_512").reshape(TOKENS, CTX).T,
        "L0_xattn_W_kT": given.pop("L0_xattn_W_k").T,
        "L1_xattn_W_qrT": given.pop("L1_xattn_W_qr").transpose(0, 2, 1),
        "L1_xattn_W_krT": given.pop("L1_xattn_W_kr").transpose(0, 2, 1),
        "L1_xattn_WoT": given.pop("L1_xattn_Wo").T,
    }
    const, const_at = constants()
    arrays = {k: np.ascontiguousarray(v) for k, v in {**given, **turned, "const": const}.items()}
    nc = bacc.Bacc("TRN2", target_bir_lowering=False, num_devices=1)
    a = {k: nc.dram_tensor(f"in_{k}", v.shape, mybir.dt.from_np(v.dtype), kind="ExternalInput").ap() for k, v in arrays.items()}
    out = nc.dram_tensor("out_x", [BATCH, SEQ, DIM], F32, kind="ExternalOutput").ap()
    build(nc, a, const_at, out)
    r = run_bass_kernel_spmd(nc, [{f"in_{k}": v for k, v in arrays.items()}], core_ids=[0])
    return r.results[0]["out_x"]
```

```python
from contextlib import ExitStack

import numpy as np
import concourse.bass as bass
from concourse import mybir

F32 = mybir.dt.float32
I32 = mybir.dt.int32
U32 = mybir.dt.uint32
ALU = mybir.AluOpType
ACT = mybir.ActivationFunctionType
AX = mybir.AxisListType.X
ds = bass.ds

P = 128
BATCH, SEQ, DIM, CTX = 4, 256, 256, 64
TOKENS = BATCH * SEQ
TILES = TOKENS // P
KC = DIM // P
LN_EPS = 1e-5

A_HEADS, A_KV, A_HD, A_WINDOW, A_CAP = 16, 4, 128, 128, 50.0
A_G = A_HEADS // A_KV
M_E, M_K, M_F, M_GROUPS, M_KG, M_SCALE = 64, 6, 96, 8, 4, 2.5
M_CAP = 2 * (2 * 128 * M_K // M_E)
D_H, D_K, D_V, D_CONV = 12, 128, 32, 4
X_H, X_K, X_CQ, X_R = 16, 128, 192, 64
X_HALF = X_CQ // 2
F_E, F_H = 16, 128


def constants():
    f = np.float32
    col, row = np.arange(P)[None, :], np.arange(P)[:, None]
    parts = {}
    parts["ident"] = (row == col)
    parts["ones"] = np.ones((P, P))
    parts["upto"] = (row <= col)
    parts["after"] = (row > col)
    parts["before"] = (row < col)
    frac = (np.arange(0, A_HD, 2, dtype=f) / f(A_HD)).astype(f)
    inv = (f(1.0) / np.power(f(10000.0), frac)).astype(f)
    ang = (np.arange(SEQ, dtype=f)[None, :] * np.concatenate([inv, inv])[:, None]).astype(f)
    sign = np.where(row < P // 2, 1.0, -1.0)
    parts["a_cos"] = np.tile(np.cos(ang), (1, 2))
    parts["a_sin"] = np.tile(np.sin(ang), (1, 2)) * sign
    q = np.arange(SEQ)[None, :]
    m0 = (q >= row) & (q <= row + A_WINDOW)
    parts["a_mask"] = np.concatenate([m0, (row <= col)], 1)
    for lv in range(7):
        w = 1 << lv
        parts[f"level{lv}"] = (row // (2 * w) == col // (2 * w)) & (row // w < col // w)
    def pair_table(dim):
        iv = (f(1.0) / np.power(f(10000.0), (np.arange(0, dim, 2, dtype=f) / f(dim)))).astype(f)
        a = (np.arange(SEQ, dtype=f)[:, None] * iv[None, :]).astype(f)
        return np.repeat(a, 2, axis=1).T
    big = pair_table(X_CQ)
    for n in range(2):
        half = np.zeros((P, SEQ))
        half[:X_HALF] = big[n * X_HALF:(n + 1) * X_HALF]
        parts[f"x_cos{n}"] = np.tile(np.cos(half), (1, 2))
        parts[f"x_sin{n}"] = np.tile(np.sin(half), (1, 2)) * (-1.0 if n == 0 else 1.0)
    small = pair_table(CTX)
    parts["k_cos"] = np.concatenate([np.cos(small)] * 2, 0)
    swapped = np.concatenate([np.sin(small[CTX // 2:]), -np.sin(small[:CTX // 2])], 0)
    parts["k_sin"] = np.concatenate([swapped] * 2, 0)
    parts["f_mask"] = np.where(np.arange(SEQ)[None, :] - P <= row, 0.0, -1e30)
    at, off = {}, 0
    for k, v in parts.items():
        at[k] = (off, v.shape[1])
        off += v.shape[1]
    return np.concatenate([np.asarray(v, f) for v in parts.values()], 1), at


class Env:

    def __init__(self, nc, ctx, at):
        self.nc, self.at = nc, at
        self.x = ctx.enter_context(nc.sbuf_tensor("x", [P, TILES, DIM], F32))
        self.xT = ctx.enter_context(nc.sbuf_tensor("xT", [P, KC, TOKENS], F32))
        self.const = ctx.enter_context(nc.sbuf_tensor("const", [P, sum(n for _, n in at.values())], F32))

    def c(self, name):
        off, n = self.at[name]
        return self.const[:, off:off + n]


CREDIT = 8


def done(i, per, n):
    return i * per + (CREDIT + n)


def credit(engine, *steps):
    for s in steps:
        engine.sem_inc(s, CREDIT)


def tools(nc, ctx, tag):
    own = []

    def clear():
        nc.clear_and_free_semaphores(own)
        nc.all_engine_barrier()

    ctx.callback(clear)

    def sb(name, shape, dt=F32):
        return ctx.enter_context(nc.sbuf_tensor(f"{tag}_{name}", shape, dt))

    def ps(name, shape, dt=F32):
        return ctx.enter_context(nc.psum_tensor(f"{tag}_{name}", shape, dt))

    def sem(name):
        own.append(nc.alloc_semaphore(f"{tag}_{name}"))
        return own[-1]
    return sb, ps, sem


def load_inputs(nc, env, x_in, const_in):
    with ExitStack() as ctx:
        sb, ps, sem = tools(nc, ctx, "load")
        loaded, turned, copied = sem("loaded"), sem("turned"), sem("copied")
        tp = ps("tp", [P, 4, 512])
        with nc.Block() as block:
            @block.sync
            def _(sp):
                sp.dma_start(env.x[:], x_in.rearrange("b (u p) c -> p (b u) c", p=P)).then_inc(loaded, 16)
                sp.dma_start(env.const[:], const_in).then_inc(loaded, 16)
                sp.wait_ge(loaded, 32)

            @block.tensor
            def _(pe):
                pe.wait_ge(loaded, 32)
                turn_x(pe, env, tp, turned, None)

            @block.vector
            def _(dve):
                for n in range(4):
                    dve.wait_ge(turned, n + 1)
                    dve.tensor_copy(env.xT[:, n // 2, 512 * (n % 2):512 * (n % 2) + 512], tp[:, n, :]).then_inc(copied, 1)


def turn_x(pe, env, tp, turned, tile_ready):
    for kc in range(KC):
        for th in range(2):
            for j in range(4):
                t = 4 * th + j
                if tile_ready is not None and kc == 0:
                    pe.wait_ge(tile_ready, t + 1)
                mm = pe.transpose(tp[:, 2 * kc + th, P * j:P * j + P], env.x[:, t, P * kc:P * kc + P], env.c("ident"))
            mm.then_inc(turned, 1)


def normalize(nc, env, tag, out=None):
    with ExitStack() as ctx:
        sb, ps, sem = tools(nc, ctx, tag)
        H = TILES // 2
        stats, mv = sb("stats", [P, TILES, 6]), sb("mv", [P, TILES, 2])
        var, rstd, half = sb("var", [P, TILES]), sb("rstd", [P, TILES]), sb("half", [P, TILES])
        tp = ps("tp", [P, 4, 512])
        stats_ready, mv_ready, var_ready, half_ready = sem("stats_ready"), sem("mv_ready"), sem("var_ready"), sem("half_ready")
        rstd_ready, tile_ready, turned, copied, stored = sem("rstd_ready"), sem("tile_ready"), sem("turned"), sem("copied"), sem("stored")
        with nc.Block() as block:
            @block.vector
            def _(dve):
                for c in range(2):
                    for t in range(H * c, H * c + H):
                        dve.bn_stats(stats[:, t, :], env.x[:, t, :]).then_inc(stats_ready, 1)
                    for t in range(H * c, H * c + H):
                        dve.wait_ge(stats_ready, t + 1)
                        dve.bn_aggr(mv[:, t, :], stats[:, t, :]).then_inc(mv_ready, 1)
                    dve.wait_ge(mv_ready, H * c + H)
                    dve.tensor_scalar(var[:, H * c:H * c + H], mv[:, H * c:H * c + H, 1], LN_EPS, None, ALU.add).then_inc(var_ready, 1)
                for t in range(TILES):
                    if t % H == 0:
                        dve.wait_ge(rstd_ready, t // H + 1)
                    dve.tensor_scalar(env.x[:, t, :], env.x[:, t, :], mv[:, t, 0:1], rstd[:, t:t + 1],
                                      ALU.subtract, ALU.mult).then_inc(tile_ready, 1)
                if out is None:
                    for n in range(0, 4, 2):
                        dve.wait_ge(turned, n + 1)
                        dve.tensor_copy(env.xT[:, n // 2, 0:512], tp[:, n, :]).then_inc(copied, 1)

            @block.gpsimd
            def _(pool):
                pool.memset(half[:], -0.5).then_inc(half_ready, 1)
                pool.wait_ge(half_ready, 1)
                for c in range(2):
                    pool.wait_ge(var_ready, c + 1)
                    pool.tensor_tensor(rstd[:, H * c:H * c + H], var[:, H * c:H * c + H], half[:, H * c:H * c + H], ALU.pow).then_inc(rstd_ready, 1)

            if out is None:
                @block.tensor
                def _(pe):
                    turn_x(pe, env, tp, turned, tile_ready)

                @block.scalar
                def _(act):
                    for n in range(1, 4, 2):
                        act.wait_ge(turned, n + 1)
                        act.copy(env.xT[:, n // 2, 512:1024], tp[:, n, :]).then_inc(copied, 1)
            else:
                @block.sync
                def _(sp):
                    view = out.rearrange("b (u p) c -> p (b u) c", p=P)
                    for n in range(2):
                        sp.wait_ge(tile_ready, 4 * n + 4)
                        sp.dma_start(view[:, 4 * n:4 * n + 4, :], env.x[:, 4 * n:4 * n + 4, :]).then_inc(stored, 16)
                    sp.wait_ge(stored, 32)


def window_attention(nc, env, wq, wk, wv, wo):
    SCALE = float(A_HD) ** -0.5
    HALF = A_HD // 2
    CH = TOKENS // 512
    QCH = CH * (A_G + 1)
    PJ = QCH + 2
    UN = BATCH * A_G
    with ExitStack() as ctx:
        sb, ps, sem = tools(nc, ctx, "wa")
        wqs, wks, wvs = sb("wq", [P, KC, A_G * A_HD]), sb("wk", [P, KC, A_HD]), sb("wv", [P, KC, A_HD])
        wos = sb("wo", [P, A_G, DIM])
        qkT = sb("qkT", [P, A_G + 1, TOKENS])
        v = sb("v", [P, TILES, A_HD + 1])
        t_cos, t_sin = sb("t_cos", [P, 2, 512]), sb("t_sin", [P, 2, 512])
        capped, probs, masked = sb("capped", [P, 2, 384]), sb("probs", [P, 2, 384]), sb("masked", [P, 3, 384])
        rec, enc, encT = sb("rec", [P, 2, 2]), sb("enc", [P, 4, 2, A_HD]), sb("encT", [P, A_G, TOKENS])
        pj, lg, pv, po = ps("pj", [P, 2, 512]), ps("lg", [P, 2, 512]), ps("pv", [P, 2, 512]), ps("po", [P, 2, 512])
        w_loaded, wo_loaded = sem("w_loaded"), sem("wo_loaded")
        projected, logits_done, weighted_done, out_done = sem("projected"), sem("logits_done"), sem("weighted_done"), sem("out_done")
        cos_done, sin_done, v_copied, rec_done, normed, added = sem("cos_done"), sem("sin_done"), sem("v_copied"), sem("rec_done"), sem("normed"), sem("added")
        turned, enc_copied = sem("turned"), sem("enc_copied")
        rotated, mask_done, capped_done, exp_done = sem("rotated"), sem("mask_done"), sem("capped_done"), sem("exp_done")

        with nc.Block() as block:
            @block.sync
            def _(sp):
                with sp.Fori(0, A_KV) as g:
                    sp.wait_ge(projected, done(g, PJ, 0))
                    sp.dma_start(wqs[:], wq.rearrange("(k p) n -> p k n", p=P)[:, :, ds(g * (A_G * A_HD), A_G * A_HD)]).then_inc(w_loaded, 16)
                    sp.dma_start(wks[:], wk.rearrange("(k p) n -> p k n", p=P)[:, :, ds(g * A_HD, A_HD)]).then_inc(w_loaded, 16)
                    sp.dma_start(wvs[:], wv.rearrange("(k p) n -> p k n", p=P)[:, :, ds(g * A_HD, A_HD)]).then_inc(w_loaded, 16)
                    sp.wait_ge(out_done, done(g, TILES, 0))
                    sp.dma_start(wos[:], wo.rearrange("(g i p) n -> p g i n", p=P, i=A_G)[:, ds(g, 1), :, :].rearrange("p g i n -> p (g i) n")).then_inc(wo_loaded, 16)

            @block.tensor
            def _(pe):
                credit(pe, projected, logits_done, weighted_done, out_done, turned)
                with pe.Fori(0, A_KV) as g:
                    pe.wait_ge(w_loaded, g * 48 + 48)

                    def bank_free(n):
                        if n < 2:
                            pe.wait_ge(v_copied, done(g, 2, n - 1))
                        else:
                            pe.wait_ge(sin_done, done(g, 2 * QCH, 2 * (n - 1)))

                    for n in range(QCH):
                        m, c = divmod(n, CH)
                        bank_free(n)
                        for k in range(KC):
                            w = wks[:, k, :] if m == 0 else wqs[:, k, A_HD * (m - 1):A_HD * m]
                            mm = pe.matmul(pj[:, n % 2, :], w, env.xT[:, k, 512 * c:512 * c + 512], start=(k == 0), stop=(k == KC - 1))
                        mm.then_inc(projected, 1)
                    for h in range(2):
                        bank_free(QCH + h)
                        for j in range(4):
                            t = 4 * h + j
                            for k in range(KC):
                                mm = pe.matmul(pj[:, h, P * j:P * j + P], env.xT[:, k, P * t:P * t + P], wvs[:, k, :], start=(k == 0), stop=(k == KC - 1))
                        mm.then_inc(projected, 1)

                    def logits(u):
                        b, i = divmod(u, A_G)
                        pe.wait_ge(capped_done, done(g, UN, u - 1))
                        pe.wait_ge(rotated, done(g, QCH, CH * (i + 1) + b // 2 + 1))
                        o = SEQ * b
                        pe.matmul(lg[:, u % 2, 0:SEQ], qkT[:, 0, o:o + P], qkT[:, 1 + i, o:o + SEQ], start=True, stop=True)
                        pe.matmul(lg[:, u % 2, SEQ:SEQ + P], qkT[:, 0, o + P:o + SEQ], qkT[:, 1 + i, o + P:o + SEQ], start=True, stop=True).then_inc(logits_done, 1)

                    def weighted(u):
                        b, i = divmod(u, A_G)
                        pe.wait_ge(mask_done, done(g, UN, u + 1))
                        pe.wait_ge(normed, done(g, UN, u - 1))
                        if u == 0:
                            pe.wait_ge(v_copied, done(g, 2, 2))
                        pe.matmul(pv[:, u % 2, 0:A_HD + 1], masked[:, u % 3, 0:P], v[:, 2 * b, :], start=True, stop=True)
                        pe.matmul(pv[:, u % 2, SEQ:SEQ + A_HD + 1], masked[:, u % 3, P:SEQ], v[:, 2 * b, :], start=True, stop=False)
                        pe.matmul(pv[:, u % 2, SEQ:SEQ + A_HD + 1], masked[:, u % 3, SEQ:SEQ + P], v[:, 2 * b + 1, :], start=False, stop=True).then_inc(weighted_done, 1)

                    def turn(j):
                        pe.wait_ge(normed, done(g, UN, 2 * j + 2))
                        if j == 0:
                            pe.wait_ge(added, done(g, TILES, 0))
                        else:
                            pe.wait_ge(enc_copied, done(g, UN // 2, j - 1))
                        for n in range(4):
                            mm = pe.transpose(po[:, j % 2, P * n:P * n + P], enc[:, (2 * j + n // 2) % 4, n % 2, :], env.c("ident"))
                        mm.then_inc(turned, 1)

                    for u in range(UN + 3):
                        if u < UN:
                            logits(u)
                        if 2 <= u < UN + 2:
                            weighted(u - 2)
                        if u >= 4 and u % 2 == 0:
                            turn((u - 4) // 2)
                    pe.wait_ge(wo_loaded, g * 16 + 16)
                    pe.wait_ge(enc_copied, done(g, UN // 2, UN // 2))
                    for t in range(TILES):
                        pe.wait_ge(added, done(g, TILES, t - 1))
                        for i in range(A_G):
                            mm = pe.matmul(po[:, t % 2, 0:DIM], encT[:, i, P * t:P * t + P], wos[:, i, :], start=(i == 0), stop=(i == A_G - 1))
                        mm.then_inc(out_done, 1)

            @block.vector
            def _(dve):
                credit(dve, cos_done, sin_done, v_copied, rec_done, normed, added)
                dve.memset(v[:, :, A_HD:A_HD + 1], 1.0)
                with dve.Fori(0, A_KV) as g:
                    for n in range(QCH):
                        dve.wait_ge(projected, done(g, PJ, n + 1))
                        dve.wait_ge(rotated, done(g, QCH, n - 1))
                        dve.tensor_tensor(t_cos[:, n % 2, :], pj[:, n % 2, :], env.c("a_cos"), ALU.mult).then_inc(cos_done, 1)
                        dve.tensor_tensor(t_sin[0:HALF, n % 2, :], pj[HALF:P, n % 2, :], env.c("a_sin")[HALF:P, :], ALU.mult).then_inc(sin_done, 1)
                        dve.tensor_tensor(t_sin[HALF:P, n % 2, :], pj[0:HALF, n % 2, :], env.c("a_sin")[0:HALF, :], ALU.mult).then_inc(sin_done, 1)
                    dve.wait_ge(weighted_done, done(g, UN, 0))
                    for h in range(2):
                        dve.wait_ge(projected, done(g, PJ, QCH + h + 1))
                        dve.tensor_copy(v[:, 4 * h:4 * h + 4, 0:A_HD], pj[:, h, :].rearrange("p (j n) -> p j n", n=P)).then_inc(v_copied, 1)
                    for u in range(UN):
                        tiles = pv[:, u % 2, :].rearrange("p (n c) -> p n c", n=2)
                        dve.wait_ge(weighted_done, done(g, UN, u + 1))
                        dve.reciprocal(rec[:, u % 2, :].rearrange("p (n o) -> p n o", o=1), tiles[:, :, A_HD:A_HD + 1]).then_inc(rec_done, 1)
                        dve.wait_ge(rec_done, done(g, UN, u + 1))
                        dve.wait_ge(turned, done(g, UN // 2, u // 2 - 1))
                        dve.tensor_tensor(enc[:, u % 4, :, :], tiles[:, :, 0:A_HD], rec[:, u % 2, :].rearrange("p (n o) -> p n o", o=1).to_broadcast([P, 2, A_HD]), ALU.mult).then_inc(normed, 1)
                    for t in range(TILES):
                        dve.wait_ge(out_done, done(g, TILES, t + 1))
                        dve.tensor_tensor(env.x[:, t, :], env.x[:, t, :], po[:, t % 2, 0:DIM], ALU.add).then_inc(added, 1)

            @block.gpsimd
            def _(pool):
                credit(pool, rotated, mask_done)
                with pool.Fori(0, A_KV) as g:
                    pool.wait_ge(logits_done, done(g, UN, 0))
                    for n in range(QCH):
                        m, c = divmod(n, CH)
                        pool.wait_ge(sin_done, done(g, 2 * QCH, 2 * n + 2))
                        pool.tensor_tensor(qkT[:, m, 512 * c:512 * c + 512], t_cos[:, n % 2, :], t_sin[:, n % 2, :], ALU.add).then_inc(rotated, 1)
                    for u in range(UN):
                        pool.wait_ge(exp_done, done(g, UN, u + 1))
                        pool.wait_ge(weighted_done, done(g, UN, u - 2))
                        pool.tensor_tensor(masked[:, u % 3, :], probs[:, u % 2, :], env.c("a_mask"), ALU.mult).then_inc(mask_done, 1)

            @block.scalar
            def _(act):
                credit(act, capped_done, exp_done, enc_copied)

                def cap_and_exp(g, u):
                    act.wait_ge(logits_done, done(g, UN, u + 1))
                    act.activation(capped[:, u % 2, :], lg[:, u % 2, 0:384], ACT.Tanh, scale=SCALE / A_CAP).then_inc(capped_done, 1)
                    act.wait_ge(capped_done, done(g, UN, u + 1))
                    act.wait_ge(mask_done, done(g, UN, u - 1))
                    act.activation(probs[:, u % 2, :], capped[:, u % 2, :], ACT.Exp, scale=A_CAP).then_inc(exp_done, 1)

                def copy_turned(g, j):
                    b, i = divmod(2 * j, A_G)
                    act.wait_ge(turned, done(g, UN // 2, j + 1))
                    act.wait_ge(out_done, done(g, TILES, 0))
                    act.copy(encT[:, i:i + 2, SEQ * b:SEQ * b + SEQ], po[:, j % 2, :].rearrange("p (i t) -> p i t", i=2)).then_inc(enc_copied, 1)

                with act.Fori(0, A_KV) as g:
                    for u in range(UN + 3):
                        if u < UN:
                            cap_and_exp(g, u)
                        if u >= 4 and u % 2 == 0:
                            copy_turned(g, (u - 4) // 2)


def softmax_cross(nc, env, ctxT, wkT, bk, gamma, beta):
    SCALE, EPS = float(DIM) ** -0.5, 1e-6
    with ExitStack() as ctx:
        sb, ps, sem = tools(nc, ctx, "xc")
        ctx_sb, w_sb, b_sb = sb("ctx", [CTX, TOKENS]), sb("w", [CTX, CTX]), sb("b", [CTX, 1])
        g_sb, be_sb = sb("g", [P, DIM]), sb("be", [P, DIM])
        kvT, kv, oT = sb("kvT", [CTX, TOKENS]), sb("kv", [P, TILES, CTX]), sb("oT", [CTX, TOKENS])
        stats, mv, var, half, rstd = sb("stats", [P, TILES, 6]), sb("mv", [P, TILES, 2]), sb("var", [P, TILES]), sb("half", [P, TILES]), sb("rstd", [P, TILES])
        n1, n2, n3, e = sb("n1", [P, 2, DIM]), sb("n2", [P, 2, DIM]), sb("n3", [P, 2, DIM]), sb("e", [P, 2, DIM])
        mx, total, rec = sb("mx", [P, TILES]), sb("total", [P, TILES]), sb("rec", [P, TILES])
        kp, tp, sp_ = ps("kp", [CTX, 2, 512]), ps("tp", [P, 2, 512]), ps("sp", [P, 4, 512])
        loaded, kv_done, biased, turned, kv_copied = sem("loaded"), sem("kv_done"), sem("biased"), sem("turned"), sem("kv_copied")
        o_done, o_copied, sim_done, stats_done, aggr_done, var_done = sem("o_done"), sem("o_copied"), sem("sim_done"), sem("stats_done"), sem("aggr_done"), sem("var_done")
        half_done, rstd_done, centered, scaled, shifted, max_done, exp_done, rec_done, added = (
            sem("half_done"), sem("rstd_done"), sem("centered"), sem("scaled"), sem("shifted"), sem("max_done"), sem("exp_done"), sem("rec_done"), sem("added"))
        with nc.Block() as block:
            @block.sync
            def _(sp):
                sp.dma_start(ctx_sb[:], ctxT).then_inc(loaded, 16)
                sp.dma_start(w_sb[:], wkT).then_inc(loaded, 16)
                sp.dma_start(b_sb[:], bk.rearrange("(d o) -> d o", o=1)).then_inc(loaded, 16)
                sp.dma_start(g_sb[:], gamma.rearrange("(o d) -> o d", o=1).to_broadcast([P, DIM])).then_inc(loaded, 16)
                sp.dma_start(be_sb[:], beta.rearrange("(o d) -> o d", o=1).to_broadcast([P, DIM])).then_inc(loaded, 16)

            @block.tensor
            def _(pe):
                pe.wait_ge(loaded, 80)
                for c in range(2):
                    pe.matmul(kp[:, c, :], w_sb[:], ctx_sb[:, 512 * c:512 * c + 512], start=True, stop=True).then_inc(kv_done, 1)
                pe.wait_ge(biased, 2)
                for t in range(TILES):
                    mm = pe.transpose(tp[:, 0, CTX * t:CTX * t + CTX], kvT[:, P * t:P * t + P], env.c("ident")[0:CTX, 0:CTX])
                mm.then_inc(turned, 1)
                pe.wait_ge(kv_copied, 1)
                for b in range(BATCH):
                    for k in range(KC):
                        mm = pe.matmul(kp[:, b // 2, SEQ * (b % 2):SEQ * (b % 2) + SEQ], kv[:, 2 * b + k, :], env.xT[:, k, SEQ * b:SEQ * b + SEQ], start=(k == 0), stop=(k == KC - 1))
                    mm.then_inc(o_done, 1)
                for t in range(TILES):
                    if t % 4 == 0:
                        pe.wait_ge(o_copied, t // 4 + 1)
                    if t >= 4:
                        pe.wait_ge(centered, t - 3)
                    b = t // 2
                    pe.matmul(sp_[:, t % 4, 0:DIM], oT[:, P * t:P * t + P], kvT[:, SEQ * b:SEQ * b + SEQ], start=True, stop=True).then_inc(sim_done, 1)

            @block.vector
            def _(dve):
                for c in range(2):
                    dve.wait_ge(kv_done, c + 1)
                    dve.tensor_scalar(kvT[:, 512 * c:512 * c + 512], kp[:, c, :], b_sb[:, 0:1], None, ALU.add).then_inc(biased, 1)
                dve.wait_ge(turned, 1)
                dve.tensor_copy(kv[:], tp[:, 0, :].rearrange("p (t d) -> p t d", d=CTX)).then_inc(kv_copied, 1)
                for c in range(2):
                    dve.wait_ge(o_done, 2 * c + 2)
                    dve.tensor_copy(oT[:, 512 * c:512 * c + 512], kp[:, c, :]).then_inc(o_copied, 1)

                def first(t):
                    dve.wait_ge(sim_done, t + 1)
                    dve.bn_stats(stats[:, t, :], sp_[:, t % 4, 0:DIM]).then_inc(stats_done, 1)
                    dve.wait_ge(stats_done, t + 1)
                    dve.bn_aggr(mv[:, t, :], stats[:, t, :]).then_inc(aggr_done, 1)
                    dve.wait_ge(aggr_done, t + 1)
                    dve.tensor_scalar(var[:, t:t + 1], mv[:, t, 1:2], SCALE * SCALE, EPS, ALU.mult, ALU.add).then_inc(var_done, 1)

                def second(t):
                    dve.wait_ge(rstd_done, 2 * t + 2)
                    if t >= 2:
                        dve.wait_ge(scaled, t - 1)
                    dve.tensor_scalar(n1[:, t % 2, :], sp_[:, t % 4, 0:DIM], mv[:, t, 0:1], rstd[:, t:t + 1], ALU.subtract, ALU.mult).then_inc(centered, 1)
                    dve.wait_ge(shifted, t + 1)
                    dve.tensor_reduce(mx[:, t:t + 1], n3[:, t % 2, :], AX, ALU.max, negate=True).then_inc(max_done, 1)

                def third(t):
                    dve.wait_ge(exp_done, t + 1)
                    dve.reciprocal(rec[:, t:t + 1], total[:, t:t + 1]).then_inc(rec_done, 1)
                    dve.wait_ge(rec_done, t + 1)
                    dve.scalar_tensor_tensor(env.x[:, t, :], e[:, t % 2, :], rec[:, t:t + 1], env.x[:, t, :], ALU.mult, ALU.add).then_inc(added, 1)

                for i in range(TILES + 2):
                    if i < TILES:
                        first(i)
                    if 1 <= i <= TILES:
                        second(i - 1)
                    if i >= 2:
                        third(i - 2)

            @block.gpsimd
            def _(pool):
                pool.memset(half[:], -0.5).then_inc(half_done, 1)
                pool.wait_ge(half_done, 1)
                pool.wait_ge(loaded, 80)

                for t in range(TILES):
                    pool.wait_ge(var_done, t + 1)
                    pool.tensor_tensor(rstd[:, t:t + 1], var[:, t:t + 1], half[:, t:t + 1], ALU.pow).then_inc(rstd_done, 1)
                    pool.wait_ge(rstd_done, 2 * t + 1)
                    pool.tensor_scalar(rstd[:, t:t + 1], rstd[:, t:t + 1], SCALE, None, ALU.mult).then_inc(rstd_done, 1)
                    pool.wait_ge(centered, t + 1)
                    pool.tensor_tensor(n2[:, t % 2, :], n1[:, t % 2, :], g_sb[:], ALU.mult).then_inc(scaled, 1)
                    pool.wait_ge(scaled, t + 1)
                    if t >= 2:
                        pool.wait_ge(exp_done, t - 1)
                    pool.tensor_tensor(n3[:, t % 2, :], n2[:, t % 2, :], be_sb[:], ALU.add).then_inc(shifted, 1)

            @block.scalar
            def _(act):
                for t in range(TILES):
                    act.wait_ge(max_done, t + 1)
                    if t >= 2:
                        act.wait_ge(added, t - 1)
                    act.activation(e[:, t % 2, :], n3[:, t % 2, :], ACT.Exp, bias=mx[:, t:t + 1], accum_out=total[:, t:t + 1]).then_inc(exp_done, 1)


NEG = -1.0e30
M_SLOTS = M_E * M_CAP
M_NONE = 1 << 20
M_IN_ROWS = M_SLOTS // P
M_Q, M_STEPS = 4, 4


class ExpertWeights:

    def __init__(self, sb, sem, a):
        self.wg, self.wu = sb("wg", [P, M_STEPS, M_Q, KC * M_F]), sb("wu", [P, M_STEPS, M_Q, KC * M_F])
        self.wd = sb("wd", [M_F, M_STEPS, M_Q, DIM])
        self.gate_up_loaded, self.down_loaded = ([sem(f"{n}{s}") for s in range(M_STEPS)] for n in ("gate_up_loaded", "down_loaded"))
        self.gv, self.uv = (a[n].rearrange("e (p k) f -> p e (k f)", k=KC) for n in ("L0_ffn_w_gate", "L0_ffn_w_up"))
        self.dv = a["L0_ffn_w_down"].rearrange("e f c -> f e c")

    def load_gate_up(self, sp, s, first):
        for dst, src in ((self.wg, self.gv), (self.wu, self.uv)):
            sp.dma_start(dst[:, s, :, :], src[:, ds(first, M_Q), :]).then_inc(self.gate_up_loaded[s], 16)

    def load_down(self, sp, s, first):
        sp.dma_start(self.wd[:, s, :, :], self.dv[:, ds(first, M_Q), :]).then_inc(self.down_loaded[s], 16)


def moe_shared_and_route(nc, env, ew, zeros, wr, bias, ws_gate, ws_up, ws_down, slot_x, out_rows, key, wkey):
    G, GE = M_GROUPS, M_E // M_GROUPS
    with ExitStack() as ctx:
        sb, ps, sem = tools(nc, ctx, "mr")
        wr_sb, bias_sb = sb("wr", [P, KC, M_E]), sb("bias", [P, M_E])
        wg_sb, wu_sb, wd_sb = sb("wsg", [P, KC, M_F]), sb("wsu", [P, KC, M_F]), sb("wsd", [M_F, DIM])
        base_i, base = sb("base_i", [P, M_E], I32), sb("base", [P, M_E])
        sc, scb = sb("sc", [P, TILES, M_E]), sb("scb", [P, TILES, M_E])
        hi2, lo2 = sb("hi2", [P, TILES * G, 4]), sb("lo2", [P, TILES * G, 4])
        hi1, lo1, mn1, ml1 = sb("hi1", [P, TILES * G, 2]), sb("lo1", [P, TILES * G, 2]), sb("mn1", [P, TILES * G, 2]), sb("ml1", [P, TILES * G, 2])
        hi0, lo0, mn0, ml0 = sb("hi0", [P, TILES * G]), sb("lo0", [P, TILES * G]), sb("mn0", [P, TILES * G]), sb("ml0", [P, TILES * G])
        gs, gr, g8 = sb("gs", [P, TILES, 16]), sb("gr", [P, TILES, 16]), sb("g8", [P, TILES, 8])
        gm, gpen = sb("gm", [P, TILES, G]), sb("gpen", [P, TILES, G])
        cand, cand2, c8, crep = sb("cand", [P, TILES, M_E]), sb("cand2", [P, TILES, M_E]), sb("c8", [P, TILES, 8]), sb("crep", [P, TILES, M_E])
        sel, wsel, wsum, wrec = sb("sel", [P, TILES, M_E]), sb("wsel", [P, TILES, M_E]), sb("wsum", [P, TILES]), sb("wrec", [P, TILES])
        fits, pos, slot, keyed, wfit, junk = (sb("fits", [P, TILES, M_E]), sb("pos", [P, TILES, M_E]), sb("slot", [P, TILES, M_E]),
                                            sb("keyed", [P, TILES, M_E]), sb("wfit", [P, TILES, M_E]), sb("junk", [P, M_E]))
        kf, far = sb("kf", [P, TILES, 8]), sb("far", [P, TILES, 8])
        idx = sb("idx", [P, TILES, 8], I32)
        zrow = sb("zrow", [P, DIM])
        s_h, h = sb("s_h", [M_F, 2, 512]), sb("h", [M_F, TOKENS])
        lp, gp, pp, up, dp = ps("lp", [P, 512]), ps("gp", [M_F, 512]), ps("pp", [P, 512]), ps("up", [M_F, 512]), ps("dp", [P, 2, 512])
        loaded, zeroed, zfilled = sem("loaded"), sem("zeroed"), sem("zfilled")
        routed, counted, gate_done, up_done, down_done = sem("routed"), sem("counted"), sem("gate_done"), sem("up_done"), sem("down_done")
        sig_done, silu_done, iota_done = sem("sig_done"), sem("silu_done"), sem("iota_done")
        step, selected, keys_done, h_done, added, scattered = sem("step"), sem("selected"), sem("keys_done"), sem("h_done"), sem("added"), sem("scattered")
        with nc.Block() as block:
            @block.sync
            def _(sp):
                sp.dma_start(wr_sb[:], wr.rearrange("(k p) n -> p k n", p=P)).then_inc(loaded, 16)
                sp.dma_start(bias_sb[:], bias.rearrange("(o d) -> o d", o=1).to_broadcast([P, M_E])).then_inc(loaded, 16)
                sp.dma_start(wg_sb[:], ws_gate.rearrange("(k p) n -> p k n", p=P)).then_inc(loaded, 16)
                sp.dma_start(wu_sb[:], ws_up.rearrange("(k p) n -> p k n", p=P)).then_inc(loaded, 16)
                sp.dma_start(wd_sb[:], ws_down).then_inc(loaded, 16)
                sp.wait_ge(zeroed, 1)
                sp.dma_start(slot_x[1:1 + M_SLOTS, :].rearrange("(n p) c -> p n c", p=P), zeros[:]).then_inc(zfilled, 16)
                sp.dma_start(out_rows[0:1, :], zrow[0:1, :]).then_inc(zfilled, 16)
                for s in range(M_STEPS):
                    ew.load_gate_up(sp, s, s * M_Q)
                    ew.load_down(sp, s, s * M_Q)
                sp.wait_ge(zfilled, 32)

            @block.tensor
            def _(pe):
                pe.wait_ge(loaded, 80)
                for t in range(TILES):
                    for k in range(KC):
                        mm = pe.matmul(lp[:, M_E * t:M_E * t + M_E], env.xT[:, k, P * t:P * t + P], wr_sb[:, k, :], start=(k == 0), stop=(k == KC - 1))
                mm.then_inc(routed, 1)
                for c in range(2):
                    if c:
                        pe.wait_ge(h_done, 1)
                    for w, bank, s in ((wg_sb, gp, gate_done), (wu_sb, up, up_done)):
                        for k in range(KC):
                            mm = pe.matmul(bank[:], w[:, k, :], env.xT[:, k, 512 * c:512 * c + 512], start=(k == 0), stop=(k == KC - 1))
                        mm.then_inc(s, 1)
                pe.wait_ge(selected, 1)
                for t in range(TILES):
                    for u in range(t + 1):
                        w = env.c("before") if u == t else env.c("ones")
                        mm = pe.matmul(pp[:, M_E * t:M_E * t + M_E], w, sel[:, u, :], start=(u == 0), stop=(u == t))
                mm.then_inc(counted, 1)
                for t in range(TILES):
                    pe.wait_ge(h_done, t // 4 + 1)
                    if t >= 2:
                        pe.wait_ge(added, t - 1)
                    pe.matmul(dp[:, t % 2, 0:DIM], h[:, P * t:P * t + P], wd_sb[:], start=True, stop=True).then_inc(down_done, 1)

            @block.scalar
            def _(act):
                act.wait_ge(routed, 1)
                act.activation(sc[:], lp[:].rearrange("p (t e) -> p t e", e=M_E), ACT.Sigmoid).then_inc(sig_done, 1)
                for c in range(2):
                    act.wait_ge(gate_done, c + 1)
                    act.activation(s_h[:, c, :], gp[:], ACT.Silu).then_inc(silu_done, 1)

            @block.vector
            def _(dve):
                count = [0]

                def chain(ins):
                    count[0] += 1
                    ins.then_inc(step, 1)
                    dve.wait_ge(step, count[0])

                def along(ins):
                    count[0] += 1
                    ins.then_inc(step, 1)

                dve.memset(zeros[:], 0.0)
                dve.memset(zrow[:], 0.0).then_inc(zeroed, 1)
                chain(dve.memset(gs[:], NEG))
                for c in range(2):
                    dve.wait_ge(silu_done, c + 1)
                    dve.wait_ge(up_done, c + 1)
                    dve.tensor_tensor(h[:, 512 * c:512 * c + 512], s_h[:, c, :], up[:], ALU.mult).then_inc(h_done, 1)
                dve.wait_ge(sig_done, 1)
                chain(dve.tensor_tensor(scb[:], sc[:], bias_sb[:].rearrange("p (o e) -> p o e", o=1).to_broadcast([P, TILES, M_E]), ALU.add))
                v8 = scb[:].rearrange("p t (g e) -> p (t g) e", e=GE)
                along(dve.tensor_tensor(hi2[:], v8[:, :, 0:4], v8[:, :, 4:8], ALU.max))
                chain(dve.tensor_tensor(lo2[:], v8[:, :, 0:4], v8[:, :, 4:8], ALU.min))
                for hi, lo, n, hn, ln_, mn, ml in ((hi2[:], lo2[:], 2, hi1[:], lo1[:], mn1[:], ml1[:]),
                                                  (hi1[:], lo1[:], 1, hi0[:].rearrange("p (g o) -> p g o", o=1), lo0[:].rearrange("p (g o) -> p g o", o=1),
                                                   mn0[:].rearrange("p (g o) -> p g o", o=1), ml0[:].rearrange("p (g o) -> p g o", o=1))):
                    along(dve.tensor_tensor(hn, hi[:, :, 0:n], hi[:, :, n:2 * n], ALU.max))
                    along(dve.tensor_tensor(mn, hi[:, :, 0:n], hi[:, :, n:2 * n], ALU.min))
                    chain(dve.tensor_tensor(ml, lo[:, :, 0:n], lo[:, :, n:2 * n], ALU.max))
                    chain(dve.tensor_tensor(ln_, mn, ml, ALU.max))
                chain(dve.tensor_tensor(gs[:, :, 0:G], hi0[:].rearrange("p (t g) -> p t g", g=G), lo0[:].rearrange("p (t g) -> p t g", g=G), ALU.add))
                for t in range(TILES):
                    (along if t < TILES - 1 else chain)(dve.max(g8[:, t, :], gs[:, t, :]))
                chain(dve.memset(g8[:, :, M_KG:8], NEG))
                for t in range(TILES):
                    (along if t < TILES - 1 else chain)(dve.match_replace(gr[:, t, :], g8[:, t, :], gs[:, t, :], NEG))
                chain(dve.tensor_tensor(gm[:], gr[:, :, 0:G], gs[:, :, 0:G], ALU.not_equal))
                chain(dve.tensor_scalar(gpen[:], gm[:], -NEG, NEG, ALU.mult, ALU.add))
                wide = lambda a: a.rearrange("p t (g o) -> p (t g) o", o=1).to_broadcast([P, TILES * G, GE])
                grouped = lambda a: a.rearrange("p t (g e) -> p (t g) e", e=GE)
                chain(dve.tensor_tensor(grouped(cand[:]), grouped(scb[:]), wide(gm[:]), ALU.mult))
                chain(dve.tensor_tensor(grouped(cand2[:]), grouped(cand[:]), wide(gpen[:]), ALU.add))
                for t in range(TILES):
                    (along if t < TILES - 1 else chain)(dve.max(c8[:, t, :], cand2[:, t, :]))
                chain(dve.memset(c8[:, :, M_K:8], NEG))
                for t in range(TILES):
                    (along if t < TILES - 1 else chain)(dve.match_replace(crep[:, t, :], c8[:, t, :], cand2[:, t, :], NEG))
                chain(dve.tensor_tensor(sel[:], crep[:], cand2[:], ALU.not_equal))
                dve.sem_inc(selected, 1)
                chain(dve.tensor_tensor(wsel[:], sc[:], sel[:], ALU.mult))
                chain(dve.tensor_reduce(wsum[:], wsel[:], AX, ALU.add))
                chain(dve.reciprocal(wrec[:], wsum[:]))
                dve.wait_ge(counted, 1)
                dve.wait_ge(iota_done, 1)
                p3 = pp[:].rearrange("p (t e) -> p t e", e=M_E)
                chain(dve.tensor_scalar(fits[:], p3, float(M_CAP), None, ALU.is_lt))
                chain(dve.tensor_tensor(fits[:], fits[:], sel[:], ALU.mult))
                chain(dve.tensor_copy(base[:], base_i[:]))
                chain(dve.tensor_tensor(slot[:], p3, base[:].rearrange("p (o e) -> p o e", o=1).to_broadcast([P, TILES, M_E]), ALU.add))
                chain(dve.tensor_tensor(keyed[:], slot[:], fits[:], ALU.mult))
                chain(dve.tensor_tensor(wfit[:], wsel[:], fits[:], ALU.mult))
                for t in range(TILES):
                    (along if t < TILES - 1 else chain)(dve.max(kf[:, t, :], keyed[:, t, :]))
                chain(dve.tensor_scalar(far[:], kf[:], 0.0, float(M_NONE), ALU.is_equal, ALU.mult))
                chain(dve.tensor_tensor(far[:], far[:], kf[:], ALU.add))
                chain(dve.tensor_copy(idx[:], far[:]))
                dve.sem_inc(keys_done, 1)
                chain(dve.tensor_copy(key[:], kf[:]))
                for t in range(TILES):
                    for k in range(M_K):
                        chain(dve.scalar_tensor_tensor(junk[:], keyed[:, t, :], kf[:, t, k:k + 1], wfit[:, t, :], ALU.is_equal, ALU.mult, accum_out=wkey[:, t, k:k + 1]))
                    chain(dve.tensor_scalar(wkey[:, t, 0:M_K], wkey[:, t, 0:M_K], wrec[:, t:t + 1], M_SCALE, ALU.mult, ALU.mult))
                dve.wait_ge(scattered, 16 * TILES * M_K)
                for t in range(TILES):
                    dve.wait_ge(down_done, t + 1)
                    dve.tensor_tensor(env.x[:, t, :], env.x[:, t, :], dp[:, t % 2, 0:DIM], ALU.add).then_inc(added, 1)

            @block.gpsimd
            def _(pool):
                pool.iota(base_i[:], pattern=[[M_CAP, M_E]], base=1, channel_multiplier=0).then_inc(iota_done, 1)
                pool.wait_ge(zfilled, 32)
                pool.wait_ge(keys_done, 1)
                for t in range(TILES):
                    for k in range(M_K):
                        pool.indirect_dma_start(slot_x[:], bass.IndirectOffsetOnAxis(ap=idx[:, t, k:k + 1], axis=0), env.x[:, t, :], None,
                                                bounds_check=M_SLOTS, oob_is_err=False).then_inc(scattered, 16)
                pool.wait_ge(scattered, 16 * TILES * M_K)


def moe_experts(nc, env, ew, rows, slot_x, out_rows, key, wkey):
    Q, S = M_Q, M_STEPS
    ITER = M_E // (Q * S)
    NQ = Q * M_CAP
    with ExitStack() as ctx:
        sb, ps, sem = tools(nc, ctx, "me")
        xsT = sb("xsT", [P, KC, M_SLOTS])
        act_h, h = sb("act_h", [M_F, 2, NQ]), sb("h", [M_F, 2, NQ])
        o_sb = sb("o", [M_CAP, S, Q, DIM])
        got = sb("got", [P, M_K, DIM])
        tp, hp, op = ps("tp", [P, 2, 512]), ps("hp", [M_F, 2, 512]), ps("op", [M_CAP, 4, 512])
        rows_loaded, turned, xs_copied = [sem(f"rows_loaded{n}") for n in range(4)], sem("turned"), sem("xs_copied")
        hidden, silu_done, h_done, down_done, o_copied, o_copied2 = (sem(n) for n in ("hidden", "silu_done", "h_done", "down_done", "o_copied", "o_copied2"))
        stored = [sem(f"stored{s}") for s in range(S)]
        gathered, summed = [sem(f"gathered{k}") for k in range(M_K)], sem("summed")
        out_view = out_rows[1:1 + M_SLOTS, :].rearrange("(e s) c -> s e c", s=M_CAP)
        with nc.Block() as block:
            @block.sync
            def _(sp):
                view = slot_x[1:1 + M_SLOTS, :].rearrange("(n p) c -> p n c", p=P)
                for n in range(4):
                    sp.dma_start(rows[:, 6 * n:6 * n + 6, :], view[:, 6 * n:6 * n + 6, :]).then_inc(rows_loaded[n], 16)
                with sp.Fori(0, ITER - 1) as i:
                    first = [sp.snap(i * (Q * S) + (S + s) * Q) for s in range(S)]
                    for s in range(S):
                        sp.wait_ge(hidden, done(i, S, s + 1))
                        ew.load_gate_up(sp, s, first[s])
                        if s:
                            sp.wait_ge(down_done, done(i, 2 * S, 2 * s))
                            ew.load_down(sp, s - 1, first[s - 1])
                    sp.wait_ge(down_done, done(i, 2 * S, 2 * S))
                    ew.load_down(sp, S - 1, first[S - 1])

            @block.tensor
            def _(pe):
                credit(pe, hidden, down_done)
                for q in range(12):
                    pe.wait_ge(rows_loaded[q // 3], 16)
                    if q >= 2:
                        pe.wait_ge(xs_copied, q - 1)
                    for j in range(4):
                        mm = pe.transpose(tp[:, q % 2, P * j:P * j + P], rows[:, 2 * q + j % 2, j // 2:DIM:2], env.c("ident"))
                    mm.then_inc(turned, 1)
                pe.wait_ge(xs_copied, 12)

                def hidden_of(i, s):
                    pe.wait_ge(ew.gate_up_loaded[s], i * 32 + 32)
                    pe.wait_ge(h_done, done(i, S, s - 1))
                    for e in range(Q):
                        for w, o in ((ew.wg, 0), (ew.wu, NQ)):
                            for k in range(KC):
                                mm = pe.matmul(hp[:, s % 2, o + M_CAP * e:o + M_CAP * e + M_CAP], w[:, s, e, M_F * k:M_F * k + M_F], xsT[:, k, ds(i * (NQ * S) + (s * NQ + M_CAP * e), M_CAP)], start=(k == 0), stop=(k == KC - 1))
                    mm.then_inc(hidden, 1)

                def down(i, s):
                    pe.wait_ge(h_done, done(i, S, s + 1))
                    pe.wait_ge(ew.down_loaded[s], i * 16 + 16)
                    for e in range(Q):
                        if e % 2 == 0:
                            pe.wait_ge(o_copied if e == 0 else o_copied2, done(i, S, s - 1))
                        mm = pe.matmul(op[:, 2 * (s % 2) + e // 2, DIM * (e % 2):DIM * (e % 2) + DIM], h[:, s % 2, M_CAP * e:M_CAP * e + M_CAP], ew.wd[:, s, e, :], start=True, stop=True)
                        if e % 2:
                            mm.then_inc(down_done, 1)

                with pe.Fori(0, ITER) as i:
                    for s in range(S + 1):
                        if s < S:
                            hidden_of(i, s)
                        if s:
                            down(i, s - 1)

            @block.scalar
            def _(act):
                credit(act, silu_done, o_copied2, *stored)
                with act.Fori(0, ITER) as i:
                    first = act.snap(i * (Q * S))
                    for s in range(S + 1):
                        if s < S:
                            act.wait_ge(hidden, done(i, S, s + 1))
                            act.wait_ge(h_done, done(i, S, s - 1))
                            act.activation(act_h[:, s % 2, :], hp[:, s % 2, 0:NQ], ACT.Silu).then_inc(silu_done, 1)
                        if s:
                            act.wait_ge(stored[s - 1], i * 16 + CREDIT)
                            act.wait_ge(down_done, done(i, 2 * S, 2 * s))
                            act.copy(o_sb[:, s - 1, 2:4, :], op[:, 2 * ((s - 1) % 2) + 1, :].rearrange("p (e c) -> p e c", c=DIM)).then_inc(o_copied2, 1)
                            act.wait_ge(o_copied, done(i, S, s))
                            act.wait_ge(o_copied2, done(i, S, s))
                            act.dma_start(out_view[:, ds(first + (s - 1) * Q, Q), :], o_sb[:, s - 1, :, :]).then_inc(stored[s - 1], 16)

            @block.vector
            def _(dve):
                credit(dve, h_done, o_copied)
                for q in range(12):
                    dve.wait_ge(turned, q + 1)
                    dve.tensor_copy(xsT[:, :, 2 * P * q:2 * P * q + 2 * P], tp[:, q % 2, :].rearrange("p (k n) -> p k n", k=KC)).then_inc(xs_copied, 1)
                with dve.Fori(0, ITER) as i:
                    for s in range(S + 1):
                        if s < S:
                            dve.wait_ge(silu_done, done(i, S, s + 1))
                            dve.wait_ge(down_done, done(i, 2 * S, 2 * (s - 1)))
                            dve.tensor_tensor(h[:, s % 2, :], act_h[:, s % 2, :], hp[:, s % 2, NQ:2 * NQ], ALU.mult).then_inc(h_done, 1)
                        if s:
                            dve.wait_ge(stored[s - 1], i * 16 + CREDIT)
                            dve.wait_ge(down_done, done(i, 2 * S, 2 * s - 1))
                            dve.tensor_copy(o_sb[:, s - 1, 0:2, :], op[:, 2 * ((s - 1) % 2), :].rearrange("p (e c) -> p e c", c=DIM)).then_inc(o_copied, 1)
                for t in range(TILES):
                    for k in range(M_K):
                        dve.wait_ge(gathered[k], 16 * t + 16)
                        if t or k:
                            dve.wait_ge(summed, t * M_K + k)
                        dve.scalar_tensor_tensor(env.x[:, t, :], got[:, k, :], wkey[:, t, k:k + 1], env.x[:, t, :], ALU.mult, ALU.add).then_inc(summed, 1)

            @block.gpsimd
            def _(pool):
                for s in range(S):
                    pool.wait_ge(stored[s], 16 * ITER + CREDIT)
                for t in range(TILES):
                    for k in range(M_K):
                        if t:
                            pool.wait_ge(summed, (t - 1) * M_K + k + 1)
                        pool.indirect_dma_start(got[:, k, :], None, out_rows[:], bass.IndirectOffsetOnAxis(ap=key[:, t, k:k + 1], axis=0),
                                                bounds_check=M_SLOTS, oob_is_err=False).then_inc(gathered[k], 16)


def routed_experts(nc, env, a, slot_x, out_rows):
    with ExitStack() as ctx:
        sb, ps, sem = tools(nc, ctx, "mw")
        ew = ExpertWeights(sb, sem, a)
        rows = sb("rows", [P, M_IN_ROWS, DIM])
        key, wkey = sb("key", [P, TILES, 8], I32), sb("wkey", [P, TILES, 8])
        moe_shared_and_route(nc, env, ew, rows, a["L0_ffn_gate_w"], a["L0_ffn_bias"], a["L0_ffn_ws_gate"], a["L0_ffn_ws_up"], a["L0_ffn_ws_down"], slot_x, out_rows, key, wkey)
        moe_experts(nc, env, ew, rows, slot_x, out_rows, key, wkey)


D_N = D_H * D_V
G_, B_, GAM_, END_ = range(4)


def delta_prepare(nc, env, a, v, gate, par):
    with ExitStack() as ctx:
        sb, ps, sem = tools(nc, ctx, "dp")
        wv, wg = sb("wv", [P, KC, D_N]), sb("wg", [P, KC, D_N])
        wab = sb("wab", [P, KC, 2 * D_H])
        cw = sb("cw", [P, 3, D_CONV])
        dt_b, a_log, a_exp = sb("dt_b", [P, D_H]), sb("a_log", [P, D_H]), sb("a_exp", [P, D_H])
        raw, acc = sb("raw", [P, 3, BATCH, SEQ + 3]), sb("acc", [P, 3, BATCH, SEQ])
        vT = sb("vT", [P, 3, TOKENS])
        z, u, s, s2, poly, up2, sp_ = (sb(n, [P, TILES, D_H]) for n in ("z", "u", "s", "s2", "poly", "up2", "sp"))
        pj, gp, tp, dec, ab = ps("pj", [P, 2, 512]), ps("gp", [P, 2, 512]), ps("tp", [P, 2, 512]), ps("dec", [P, 2, TILES * D_H]), ps("ab", [P, TILES, 2 * D_H])
        loaded, projected, raw_copied, conv_done, silu_done, turned, v_copied = (sem(n) for n in ("loaded", "projected", "raw_copied", "conv_done", "silu_done", "turned", "v_copied"))
        ab_done, gate_done, gate_silu, dec_done, step, exps, z_done, g_done, beta_done, padded, dec_exp = (
            sem(n) for n in ("ab_done", "gate_done", "gate_silu", "dec_done", "step", "exps", "z_done", "g_done", "beta_done", "padded", "dec_exp"))
        NL = 8
        with nc.Block() as block:
            @block.sync
            def _(sp):
                sp.dma_start(wv[:], a["L1_attn_Wv"].rearrange("(k p) n -> p k n", p=P)).then_inc(loaded, 16)
                sp.dma_start(wg[:], a["L1_attn_Wg"].rearrange("(k p) n -> p k n", p=P)).then_inc(loaded, 16)
                sp.dma_start(wab[:, :, 0:D_H], a["L1_attn_Wb"].rearrange("(k p) n -> p k n", p=P)).then_inc(loaded, 16)
                sp.dma_start(wab[:, :, D_H:2 * D_H], a["L1_attn_Wa"].rearrange("(k p) n -> p k n", p=P)).then_inc(loaded, 16)
                sp.dma_start(cw[:], a["L1_attn_conv_wv"].rearrange("(m p) k -> p m k", p=P)).then_inc(loaded, 16)
                sp.dma_start(dt_b[:], a["L1_attn_dt_bias"].rearrange("(o d) -> o d", o=1).to_broadcast([P, D_H])).then_inc(loaded, 16)
                sp.dma_start(a_log[:], a["L1_attn_A_log"].rearrange("(o d) -> o d", o=1).to_broadcast([P, D_H])).then_inc(loaded, 16)

            @block.tensor
            def _(pe):
                pe.wait_ge(loaded, 112)
                for t in range(TILES):
                    for k in range(KC):
                        mm = pe.matmul(ab[:, t, :], env.xT[:, k, P * t:P * t + P], wab[:, k, :], start=(k == 0), stop=(k == KC - 1))
                mm.then_inc(ab_done, 1)
                for n in range(6):
                    m, c = divmod(n, 2)
                    if n >= 2:
                        pe.wait_ge(raw_copied, n - 1)
                    for k in range(KC):
                        mm = pe.matmul(pj[:, n % 2, :], wv[:, k, P * m:P * m + P], env.xT[:, k, 512 * c:512 * c + 512], start=(k == 0), stop=(k == KC - 1))
                    mm.then_inc(projected, 1)
                for t in range(TILES):
                    if t >= 2:
                        pe.wait_ge(gate_silu, t - 1)
                    for k in range(KC):
                        mm = pe.matmul(gp[:, t % 2, 0:D_N], env.xT[:, k, P * t:P * t + P], wg[:, k, :], start=(k == 0), stop=(k == KC - 1))
                    mm.then_inc(gate_done, 1)
                for t in range(TILES):
                    pe.wait_ge(silu_done, 3)
                    if t >= 2:
                        pe.wait_ge(v_copied, t - 1)
                    for m in range(3):
                        mm = pe.transpose(tp[:, t % 2, P * m:P * m + P], vT[:, m, P * t:P * t + P], env.c("ident"))
                    mm.then_inc(turned, 1)
                pe.wait_ge(g_done, 1)
                gsrc = par[:, :, G_, :].rearrange("p h t -> p h t")
                pe.matmul(dec[:, 0, :].rearrange("p (h t) -> p h t", t=TILES), env.c("upto"), gsrc, start=True, stop=True)
                pe.matmul(dec[:, 1, :].rearrange("p (h t) -> p h t", t=TILES), env.c("after"), gsrc, start=True, stop=True).then_inc(dec_done, 1)

            @block.scalar
            def _(act):
                act.wait_ge(loaded, 112)
                act.activation(a_exp[:], a_log[:], ACT.Exp).then_inc(exps, 1)
                act.wait_ge(z_done, 1)
                act.activation(u[:], u[:], ACT.Exp, scale=-1.0).then_inc(exps, 1)
                act.wait_ge(padded, 1)
                for n in range(6):
                    m, c = divmod(n, 2)
                    act.wait_ge(projected, n + 1)
                    act.copy(raw[:, m, 2 * c:2 * c + 2, 3:SEQ + 3], pj[:, n % 2, :].rearrange("p (b t) -> p b t", t=SEQ)).then_inc(raw_copied, 1)
                act.wait_ge(ab_done, 1)
                act.activation(par[:, :, B_, :], ab[:, :, 0:D_H].rearrange("p t h -> p h t"), ACT.Sigmoid).then_inc(beta_done, 1)
                for t in range(TILES):
                    act.wait_ge(gate_done, t + 1)
                    act.activation(gate[:, t, :], gp[:, t % 2, 0:D_N], ACT.Silu).then_inc(gate_silu, 1)
                for m in range(3):
                    act.wait_ge(conv_done, 4 * m + 4)
                    act.activation(vT[:, m, :].rearrange("p (b t) -> p b t", t=SEQ), acc[:, m, :, :], ACT.Silu).then_inc(silu_done, 1)
                act.wait_ge(dec_done, 1)
                act.activation(par[:, :, GAM_, :], dec[:, 0, :].rearrange("p (h t) -> p h t", t=TILES), ACT.Exp)
                act.activation(par[:, :, END_, :], dec[:, 1, :].rearrange("p (h t) -> p h t", t=TILES), ACT.Exp).then_inc(dec_exp, 1)

            @block.vector
            def _(dve):
                dve.memset(raw[:, :, :, 0:3], 0.0).then_inc(padded, 1)
                count = [0]

                def chain(ins):
                    count[0] += 1
                    ins.then_inc(step, 1)
                    dve.wait_ge(step, count[0])

                dve.wait_ge(ab_done, 1)
                dve.wait_ge(loaded, 112)
                chain(dve.tensor_tensor(z[:], ab[:, :, D_H:2 * D_H], dt_b[:].rearrange("p (o h) -> p o h", o=1).to_broadcast([P, TILES, D_H]), ALU.add))
                chain(dve.scalar_tensor_tensor(u[:], z[:], -1.0, z[:], ALU.mult, ALU.max))
                dve.sem_inc(z_done, 1)
                dve.wait_ge(exps, 2)
                chain(dve.tensor_scalar(up2[:], u[:], 2.0, None, ALU.add))
                chain(dve.reciprocal(s[:], up2[:]))
                chain(dve.tensor_tensor(s[:], s[:], u[:], ALU.mult))
                chain(dve.tensor_tensor(s2[:], s[:], s[:], ALU.mult))
                chain(dve.tensor_scalar(poly[:], s2[:], 1.0 / (2 * NL + 1), 1.0 / (2 * NL - 1), ALU.mult, ALU.add))
                for n in range(NL - 2, -1, -1):
                    chain(dve.tensor_tensor(poly[:], poly[:], s2[:], ALU.mult))
                    chain(dve.tensor_scalar(poly[:], poly[:], 1.0 / (2 * n + 1), None, ALU.add))
                chain(dve.tensor_tensor(poly[:], poly[:], s[:], ALU.mult))
                chain(dve.tensor_scalar(sp_[:], z[:], 0.0, None, ALU.max))
                chain(dve.scalar_tensor_tensor(sp_[:], poly[:], 2.0, sp_[:], ALU.mult, ALU.add))
                chain(dve.scalar_tensor_tensor(sp_[:], sp_[:], -1.0, a_exp[:].rearrange("p (o h) -> p o h", o=1).to_broadcast([P, TILES, D_H]), ALU.mult, ALU.mult))
                chain(dve.tensor_copy(par[:, :, G_, :], sp_[:].rearrange("p t h -> p h t")))
                dve.sem_inc(g_done, 1)
                for m in range(3):
                    dve.wait_ge(raw_copied, 2 * m + 2)
                    dve.tensor_scalar(acc[:, m, :, :], raw[:, m, :, 0:SEQ], cw[:, m, 0:1], None, ALU.mult).then_inc(conv_done, 1)
                    for i in range(1, D_CONV):
                        dve.wait_ge(conv_done, 4 * m + i)
                        dve.scalar_tensor_tensor(acc[:, m, :, :], raw[:, m, :, i:i + SEQ], cw[:, m, i:i + 1], acc[:, m, :, :], ALU.mult, ALU.add).then_inc(conv_done, 1)
                for t in range(TILES):
                    dve.wait_ge(turned, t + 1)
                    dve.tensor_copy(v[:, :, t, :], tp[:, t % 2, 0:D_N].rearrange("p (h d) -> p h d", d=D_V)).then_inc(v_copied, 1)


def delta_heads(nc, env, wq, wk, cq, ck, v, par, o):
    NLEV, C = 7, 2
    EPS = 1e-6
    TAPS = D_CONV - 1
    with ExitStack() as ctx:
        sb, ps, sem = tools(nc, ctx, "dh")
        wk_s, wq_s = sb("wk", [P, KC, D_K]), sb("wq", [P, KC, D_K])
        conv_all = sb("conv_all", [P, D_H, 2, D_CONV])
        raw, acc = [sb(f"raw{m}", [P, BATCH, SEQ + 3]) for m in range(2)], [sb(f"acc{m}", [P, BATCH, SEQ]) for m in range(2)]
        th, silu = sb("th", [P, BATCH, SEQ]), sb("silu", [P, 2, TOKENS])
        sq, ss, ssc, rn = sb("sq", [P, 2, 4, P]), sb("ss", [P, 2, TILES]), sb("ssc", [P, 2, TILES]), sb("rn", [P, 2, TILES])
        half = sb("half", [P, TILES])
        both = lambda n, shape: [sb(f"{n}{q}", shape) for q in range(2)]
        conv_w, hp, hv = both("conv_w", [P, 2, D_CONV]), both("hp", [P, 4, TILES]), both("hv", [P, TILES, D_V])
        kq, kqT = both("kq", [P, 2, TILES, P]), both("kqT", [P, TILES, 2, P])
        stream = lambda n: [sb(f"{n}{c}", [P, BATCH, P]) for c in range(C)]
        E, Eb, AT, T, X = (stream(n) for n in ("E", "Eb", "AT", "T", "X"))
        PT, TT = [stream(f"PT{q}_") for q in range(2)], [stream(f"TT{q}_") for q in range(2)]
        OT = [[sb(f"OT{c}{n}", [P, BATCH, P]) for n in range(2)] for c in range(C)]
        R, DL, DE, QS, S = sb("R", [P, BATCH, D_V]), sb("DL", [P, C, BATCH, D_V]), sb("DE", [P, BATCH, D_V]), sb("QS", [P, BATCH, D_V]), sb("S", [P, BATCH, D_V])
        pj, tp = ps("pj", [P, 2, 512]), ps("tp", [P, 2, 512])
        W = [[ps(f"W{c}{n}", [P, 512]) for n in range(2)] for c in range(C)]
        KK = (tp, pj)
        conv_loaded, conv_picked, w_loaded, zeroed = (sem(n) for n in ("conv_loaded", "conv_picked", "w_loaded", "zeroed"))
        projected, turned, returned, seg_done, kk_done = (sem(n) for n in ("projected", "turned", "returned", "seg_done", "kk_done"))
        x_done, tx_done, flip_done = ([sem(f"{n}{c}") for c in range(C)] for n in ("x_done", "tx_done", "flip_done"))
        u_done, o_done, s_done, ks_done = (sem(n) for n in ("u_done", "o_done", "s_done", "ks_done"))
        raw_copied, tap_done, tanh_done, squared, kqT_copied, exp_done = (sem(n) for n in ("raw_copied", "tap_done", "tanh_done", "squared", "kqT_copied", "exp_done"))
        x_copied, flip_copied, ot_done, t_done = ([sem(f"{n}{c}") for c in range(C)] for n in ("x_copied", "flip_copied", "ot_done", "t_done"))
        conv_done, silu_done, sum_done, ssc_done, normed = (sem(n) for n in ("conv_done", "silu_done", "sum_done", "ssc_done", "normed"))
        a_done, p_done, small, o_stored = (sem(n) for n in ("a_done", "p_done", "small", "o_stored"))
        hp_copied, gm_done, em_done, eb_done, pow_done = (sem(n) for n in ("hp_copied", "gm_done", "em_done", "eb_done", "pow_done"))
        SM = 7

        def at(head, per, n):
            i, q = head
            return i * (2 * per) + (CREDIT + q * per + n)

        wide = lambda bank: bank[:].rearrange("p (b i) -> p b i", b=BATCH)
        picked = lambda bank: wide(bank)[:, :, 0:D_V]

        def over_heads(engine, prepare, border, levels):
            prepare((0, 0))
            border(None, (0, 0))
            with engine.Fori(0, D_H // 2 - 1) as i:
                levels((i, 0), (i, 1))
                border((i, 0), (i, 1))
                levels((i, 1), (i, 2))
                border((i, 1), (i, 2))
            i = D_H // 2 - 1
            levels((i, 0), (i, 1))
            border((i, 0), (i, 1))
            levels((i, 1), None)
            border((i, 1), None)

        with nc.Block() as block:
            @block.sync
            def _(sp):
                for m, w in enumerate((ck, cq)):
                    sp.dma_start(conv_all[:, :, m, :], w.rearrange("(h p) k -> p h k", p=D_K)).then_inc(conv_loaded, 16)
                with sp.Fori(0, D_H) as h:
                    head = sp.snap(h * D_K)
                    sp.wait_ge(projected, done(h, 4, 0))
                    sp.dma_start(wk_s[:], wk.rearrange("(k p) n -> p k n", p=P)[:, :, ds(head, D_K)]).then_inc(w_loaded, 16)
                    sp.dma_start(wq_s[:], wq.rearrange("(k p) n -> p k n", p=P)[:, :, ds(head, D_K)]).then_inc(w_loaded, 16)

            @block.tensor
            def _(pe):
                credit(pe, projected, turned, returned, seg_done, kk_done, *x_done, *tx_done, *flip_done, u_done, o_done, s_done, ks_done)
                tiles = lambda c, b: 2 * b + c

                def project(g, n):
                    m, c = divmod(n, 2)
                    if n == 0:
                        pe.wait_ge(w_loaded, g[0] * 64 + (32 * g[1] + 32))
                        pe.wait_ge(p_done, at(g, C, 0))
                    pe.wait_ge(raw_copied, at(g, 4, n - 1))
                    pe.wait_ge(tap_done, at(g, 4, n - 1))
                    for k in range(KC):
                        mm = pe.matmul(pj[:, n % 2, :], (wk_s, wq_s)[m][:, k, :], env.xT[:, k, 512 * c:512 * c + 512], start=(k == 0), stop=(k == KC - 1))
                    mm.then_inc(projected, 1)

                def segment(g, c):
                    pe.wait_ge(gm_done, at(g, C, c + 1))
                    pe.wait_ge(o_stored, at(g, C, -2))
                    for b in range(BATCH):
                        mm = pe.matmul(tp[:, c, P * b:P * b + P], E[c][:, b, :], env.c("upto"), start=True, stop=True)
                    mm.then_inc(seg_done, 1)

                def turn(g, n):
                    m, c = divmod(n, 2)
                    pe.wait_ge(silu_done, at(g, 2, m + 1))
                    if n < 2:
                        pe.wait_ge(exp_done, at(g, C, n + 1))
                    else:
                        pe.wait_ge(normed, at(g, 4, n - 1))
                    for j in range(4):
                        t = 4 * c + j
                        mm = pe.transpose(tp[:, n % 2, P * j:P * j + P], silu[:, m, P * t:P * t + P], env.c("ident"))
                    mm.then_inc(turned, 1)

                def bring_back(g, n):
                    m, c = divmod(n, 2)
                    pe.wait_ge(normed, at(g, 4, n + 1))
                    if n < 2:
                        pe.wait_ge(raw_copied, at(g, 4, 4))
                        pe.wait_ge(tap_done, at(g, 4, 4))
                    else:
                        pe.wait_ge(kqT_copied, at(g, 4, n - 1))
                    for j in range(4):
                        mm = pe.transpose(pj[:, n % 2, P * j:P * j + P], kq[g[1] % 2][:, m, 4 * c + j, :], env.c("ident"))
                    mm.then_inc(returned, 1)

                def k_products(g, c):
                    for b in range(BATCH):
                        if c == 0 and b % 2 == 0:
                            pe.wait_ge(kqT_copied, at(g, 4, 3 + b // 2))
                        kT = kqT[g[1] % 2][:, tiles(c, b), :, :]
                        mm = pe.matmul(KK[c][:, b // 2, SEQ * (b % 2):SEQ * (b % 2) + SEQ], kT[:, 0, :], kT.rearrange("p a n -> p (a n)"), start=True, stop=True)
                    mm.then_inc(kk_done, 1)

                def flip(h, lv, c):
                    pe.wait_ge(t_done[c], at(h, NLEV, lv + 1))
                    src = TT[h[1] % 2][c] if lv == 0 else T[c]
                    for b in range(BATCH):
                        mm = pe.transpose(W[c][1][:, P * b:P * b + P], src[:, b, :], env.c("ident"))
                    mm.then_inc(flip_done[c], 1)

                def x_product(h, lv, c):
                    pe.wait_ge(ot_done[c], at(h, NLEV, lv + 1))
                    pe.wait_ge(flip_copied[c], at(h, NLEV - 1, lv))
                    for b in range(BATCH):
                        mm = pe.matmul(W[c][0][:, P * b:P * b + P], OT[c][lv % 2][:, b, :], T[c][:, b, :], start=True, stop=True)
                    mm.then_inc(x_done[c], 1)

                def tx_product(h, lv, c):
                    pe.wait_ge(x_copied[c], at(h, NLEV - 1, lv))
                    for b in range(BATCH):
                        l, r = (TT[h[1] % 2][c], X[c]) if lv < NLEV - 1 else (X[c], TT[h[1] % 2][c])
                        mm = pe.matmul(W[c][0][:, P * b:P * b + P], l[:, b, :], r[:, b, :], start=True, stop=True)
                    mm.then_inc(tx_done[c], 1)

                def small_products(bank, l, r, s):
                    for b in range(BATCH):
                        col = (P - D_V) * b
                        mm = pe.matmul(bank[:, col:col + P].rearrange("p (b d) -> p b d", d=D_V), l(b), r, start=True, stop=True)
                    mm.then_inc(s, 1)

                def prepare(g):
                    for n in range(4):
                        project(g, n)
                    for c in range(C):
                        segment(g, c)
                    for n in range(4):
                        turn(g, n)
                    for n in range(4):
                        bring_back(g, n)

                def levels(h, g):
                    for lv in range(1, NLEV):
                        if lv > 1:
                            x_product(h, lv, 0)
                            x_product(h, lv, 1)
                        if g and lv <= 3:
                            project(g, (0, 2, 3)[lv - 1])
                        elif g and lv == 5:
                            bring_back(g, 1)
                            turn(g, 2)
                        elif g and lv == 6:
                            bring_back(g, 2)
                        tx_product(h, lv, 0)
                        tx_product(h, lv, 1)
                        if g and lv == 1:
                            project(g, 1)
                        elif g and lv == 2:
                            segment(g, 0)
                        elif g and lv == 3:
                            turn(g, 0)
                        elif g and lv == 6:
                            bring_back(g, 3)
                        if lv < NLEV - 1:
                            flip(h, lv, 0)
                            flip(h, lv, 1)
                        if g and lv == 2:
                            segment(g, 1)
                        elif g and lv == 3:
                            turn(g, 1)
                        elif g and lv == 4:
                            bring_back(g, 0)
                        elif g and lv == 5:
                            turn(g, 3)

                def border(h, g):
                    if g:
                        k_products(g, 0)
                        k_products(g, 1)
                    if h:
                        q = h[1] % 2
                        pe.wait_ge(t_done[0], at(h, NLEV, NLEV))
                        small_products(W[0][0][:], lambda b: TT[q][0][:, b, :], hv[q][:, 0:TILES:2, :], u_done)
                        pe.wait_ge(t_done[1], at(h, NLEV, NLEV))
                        pe.wait_ge(small, at(h, SM, 2))
                        small_products(W[1][0][:], lambda b: kq[q][:, 0, tiles(0, b), :], DE[:], s_done)
                        small_products(W[1][1][:], lambda b: PT[q][0][:, b, :], DL[:, 0, :, :], o_done)
                    if g:
                        flip(g, 0, 0)
                    if h:
                        pe.wait_ge(small, at(h, SM, 3))
                        small_products(W[0][0][:], lambda b: kqT[q][:, tiles(1, b), 0, :], S[:], ks_done)
                        small_products(W[1][0][:], lambda b: kqT[q][:, tiles(1, b), 1, :], S[:], ks_done)
                        pe.wait_ge(o_stored, at(h, C, 1))
                    if g:
                        flip(g, 0, 1)
                    if h:
                        if g:
                            pe.wait_ge(p_done, at(g, C, 1))
                        pe.wait_ge(small, at(h, SM, 5))
                        small_products(tp[:, 0, :], lambda b: TT[q][1][:, b, :], R[:], u_done)
                    if g:
                        x_product(g, 1, 0)
                        if h:
                            pe.wait_ge(small, at(h, SM, 6))
                        x_product(g, 1, 1)
                    if h:
                        pe.wait_ge(small, at(h, SM, 7))
                        small_products(tp[:, 1, :], lambda b: PT[q][1][:, b, :], DL[:, 1, :, :], o_done)

                over_heads(pe, prepare, border, levels)

            @block.scalar
            def _(act):
                credit(act, raw_copied, tap_done, tanh_done, squared, kqT_copied, exp_done, *x_copied, *flip_copied)
                act.wait_ge(zeroed, 1)

                def copy_raw(g, n):
                    m, c = divmod(n, 2)
                    act.wait_ge(conv_picked, at(g, 1, 1))
                    act.wait_ge(conv_done, at(g, 2 * TAPS, TAPS * (m - 1)))
                    act.wait_ge(silu_done, at(g, 2, m - 1))
                    act.wait_ge(projected, at(g, 4, n + 1))
                    src = pj[:, c, :].rearrange("p (b t) -> p b t", t=SEQ)
                    act.copy(raw[m][:, 2 * c:2 * c + 2, TAPS:SEQ + TAPS], src).then_inc(raw_copied, 1)
                    act.activation(acc[m][:, 2 * c:2 * c + 2, :], src, ACT.Copy, scale=conv_w[g[1] % 2][:, m, TAPS:TAPS + 1]).then_inc(tap_done, 1)

                def tanh(g, m):
                    act.wait_ge(conv_done, at(g, 2 * TAPS, TAPS * (m + 1)))
                    act.wait_ge(silu_done, at(g, 2, m))
                    act.activation(th[:], acc[m][:], ACT.Tanh, scale=0.5).then_inc(tanh_done, 1)

                def exp(g, c):
                    act.wait_ge(seg_done, at(g, C, c + 1))
                    act.activation(E[c][:], tp[:, c, :].rearrange("p (b i) -> p b i", b=BATCH), ACT.Exp).then_inc(exp_done, 1)

                def square(g, n):
                    act.wait_ge(turned, at(g, 4, n + 1))
                    act.wait_ge(sum_done, at(g, 4, n - 1))
                    act.activation(sq[:, n % 2, :, :], tp[:, n % 2, :].rearrange("p (j n) -> p j n", n=P), ACT.Square).then_inc(squared, 1)

                def copy_kqT(g, n):
                    m, c = divmod(n, 2)
                    act.wait_ge(returned, at(g, 4, n + 1))
                    act.copy(kqT[g[1] % 2][:, 4 * c:4 * c + 4, m, :], pj[:, n % 2, :].rearrange("p (j n) -> p j n", n=P)).then_inc(kqT_copied, 1)

                def copy_flip(h, lv, c):
                    act.wait_ge(flip_done[c], at(h, NLEV - 1, lv + 1))
                    dst = T[c] if lv == 0 else TT[h[1] % 2][c]
                    act.copy(dst[:], wide(W[c][1])).then_inc(flip_copied[c], 1)

                def copy_x(h, lv, c):
                    act.wait_ge(x_done[c], at(h, NLEV - 1, lv))
                    act.copy(X[c][:], wide(W[c][0])).then_inc(x_copied[c], 1)

                def prepare(g):
                    for n in range(4):
                        copy_raw(g, n)
                    for c in range(C):
                        exp(g, c)
                    for m in range(2):
                        tanh(g, m)
                        square(g, 2 * m)
                        square(g, 2 * m + 1)
                    for n in range(4):
                        copy_kqT(g, n)

                def levels(h, g):
                    for lv in range(1, NLEV):
                        if g and lv == 3:
                            tanh(g, 0)
                        copy_x(h, lv, 0)
                        copy_x(h, lv, 1)
                        if g and lv <= 3:
                            copy_raw(g, (0, 2, 3)[lv - 1])
                        if g and lv == 4:
                            tanh(g, 1)
                        elif g and lv == 5:
                            square(g, 2)
                        elif g and lv == 6:
                            copy_kqT(g, 2)
                            copy_kqT(g, 3)
                        if lv < NLEV - 1:
                            copy_flip(h, lv, 0)
                            copy_flip(h, lv, 1)
                        if g and lv == 1:
                            copy_raw(g, 1)
                        elif g and lv == 2:
                            exp(g, 0)
                            exp(g, 1)
                        elif g and lv == 3:
                            square(g, 0)
                            square(g, 1)
                        elif g and lv == 5:
                            square(g, 3)
                            copy_kqT(g, 0)
                            copy_kqT(g, 1)

                def border(h, g):
                    if g:
                        copy_flip(g, 0, 0)
                        copy_flip(g, 0, 1)

                over_heads(act, prepare, border, levels)

            @block.vector
            def _(dve):
                credit(dve, conv_done, silu_done, sum_done, ssc_done, normed, a_done, p_done, *t_done, small, o_stored)
                for m in range(2):
                    dve.memset(raw[m][:, :, 0:TAPS], 0.0)
                dve.memset(half[:], -0.5).then_inc(zeroed, 1)
                four = lambda h, x, c: hp[h[1] % 2][:, x, c:TILES:2].rearrange("p (b o) -> p b o", o=1).to_broadcast([P, BATCH, D_V])

                def tap(g, m, i):
                    dve.wait_ge(tap_done, at(g, 4, 2 * m + 2))
                    dve.wait_ge(conv_done, at(g, 2 * TAPS, TAPS * m + i))
                    dve.scalar_tensor_tensor(acc[m][:], raw[m][:, :, i:i + SEQ], conv_w[g[1] % 2][:, m, i:i + 1], acc[m][:], ALU.mult, ALU.add).then_inc(conv_done, 1)

                def silu_of(g, m):
                    dve.wait_ge(tanh_done, at(g, 2, m + 1))
                    dve.wait_ge(turned, at(g, 4, 2 * m - 2))
                    dve.scalar_tensor_tensor(silu[:, m, :].rearrange("p (b t) -> p b t", t=SEQ), th[:], 1.0, acc[m][:], ALU.add, ALU.mult).then_inc(silu_done, 1)

                def sums(g, n):
                    m, c = divmod(n, 2)
                    dve.wait_ge(squared, at(g, 4, n + 1))
                    dve.tensor_reduce(ss[:, m, 4 * c:4 * c + 4], sq[:, n % 2, :, :], AX, ALU.add).then_inc(sum_done, 1)
                    dve.wait_ge(sum_done, at(g, 4, n + 1))
                    dve.tensor_scalar(ssc[:, m, 4 * c:4 * c + 4], ss[:, m, 4 * c:4 * c + 4], 4 * EPS, None, ALU.add).then_inc(ssc_done, 1)

                def norm(g, n):
                    m, c = divmod(n, 2)
                    dve.wait_ge(pow_done, at(g, 4, n + 1))
                    dve.tensor_tensor(kq[g[1] % 2][:, m, 4 * c:4 * c + 4, :], tp[:, n % 2, :].rearrange("p (j n) -> p j n", n=P),
                                      rn[:, m, 4 * c:4 * c + 4].rearrange("p (j o) -> p j o", o=1).to_broadcast([P, 4, P]), ALU.mult).then_inc(normed, 1)

                def a_or_p(g, c, a, dst, factor, s):
                    for n in range(2):
                        ins = dve.tensor_tensor(dst[:, 2 * n:2 * n + 2, :], KK[c][:, n, :].rearrange("p (b a i) -> p b a i", b=2, a=2)[:, :, a, :], factor[:, 2 * n:2 * n + 2, :], ALU.mult)
                    ins.then_inc(s, 1)

                def first_level(g, c):
                    dve.wait_ge(ot_done[c], at(g, NLEV, 1))
                    dve.tensor_tensor(TT[g[1] % 2][c][:], env.c("ident").rearrange("p (o i) -> p o i", o=1).to_broadcast([P, BATCH, P]), OT[c][0][:], ALU.subtract).then_inc(t_done[c], 1)

                def subtract(h, lv, c):
                    m = T[c] if lv < NLEV - 1 else TT[h[1] % 2][c]
                    dve.wait_ge(tx_done[c], at(h, NLEV - 1, lv))
                    dve.tensor_tensor(m[:], m[:], wide(W[c][0]), ALU.subtract).then_inc(t_done[c], 1)

                def prepare(g):
                    for i in range(TAPS):
                        tap(g, 0, i)
                    silu_of(g, 0)
                    tap(g, 1, 0)
                    sums(g, 0)
                    sums(g, 1)
                    tap(g, 1, 1)
                    norm(g, 0)
                    norm(g, 1)
                    tap(g, 1, 2)
                    silu_of(g, 1)
                    sums(g, 2)
                    sums(g, 3)
                    norm(g, 2)
                    norm(g, 3)

                def levels(h, g):
                    for lv in range(1, NLEV):
                        if g and lv == 2:
                            tap(g, 0, 0)
                            tap(g, 0, 1)
                        elif g and lv == 3:
                            silu_of(g, 0)
                        elif g and lv == 4:
                            sums(g, 0)
                            sums(g, 1)
                        elif g and lv == 6:
                            norm(g, 3)
                        subtract(h, lv, 0)
                        subtract(h, lv, 1)
                        if g and lv == 2:
                            tap(g, 0, 2)
                        elif g and lv == 3:
                            for i in range(TAPS):
                                tap(g, 1, i)
                        elif g and lv == 4:
                            norm(g, 0)
                            norm(g, 1)
                            silu_of(g, 1)
                        elif g and lv == 5:
                            sums(g, 2)
                            sums(g, 3)
                            norm(g, 2)

                def border(h, g):
                    if g:
                        for c in range(C):
                            dve.wait_ge(kk_done, at(g, C, c + 1))
                            dve.wait_ge(eb_done, at(g, C, c + 1))
                            a_or_p(g, c, 0, AT[c], Eb[c], a_done)
                    if h:
                        q = h[1] % 2
                        dve.wait_ge(u_done, at(h, C, 1))
                        dve.tensor_tensor(DL[:, 0, :, :], picked(W[0][0]), four(h, B_, 0), ALU.mult).then_inc(small, 1)
                        dve.wait_ge(small, at(h, SM, 1))
                        dve.tensor_tensor(DE[:], DL[:, 0, :, :], four(h, END_, 0), ALU.mult).then_inc(small, 1)
                    if g:
                        first_level(g, 0)
                    if h:
                        dve.wait_ge(s_done, at(h, 1, 1))
                        dve.tensor_copy(S[:], picked(W[1][0])).then_inc(small, 1)
                    if g:
                        first_level(g, 1)
                        a_or_p(g, 0, 1, PT[g[1] % 2][0], E[0], p_done)
                    if h:
                        dve.wait_ge(o_done, at(h, C, 1))
                        dve.tensor_copy(o[:, 0:TILES:2, ds(h[0] * (2 * D_V) + h[1] * D_V, D_V)], picked(W[1][1])).then_inc(o_stored, 1)
                    if g:
                        a_or_p(g, 1, 1, PT[g[1] % 2][1], E[1], p_done)
                    if h:
                        dve.wait_ge(ks_done, at(h, 2, 1))
                        dve.tensor_tensor(R[:], picked(W[0][0]), four(h, GAM_, 1), ALU.mult).then_inc(small, 1)
                        dve.wait_ge(small, at(h, SM, 4))
                        dve.tensor_tensor(R[:], hv[q][:, 1:TILES:2, :], R[:], ALU.subtract).then_inc(small, 1)
                        dve.wait_ge(ks_done, at(h, 2, 2))
                        dve.tensor_tensor(QS[:], picked(W[1][0]), four(h, GAM_, 1), ALU.mult).then_inc(small, 1)
                        dve.wait_ge(u_done, at(h, C, 2))
                        dve.tensor_tensor(DL[:, 1, :, :], tp[:, 0, :].rearrange("p (b i) -> p b i", b=BATCH)[:, :, 0:D_V], four(h, B_, 1), ALU.mult).then_inc(small, 1)
                        dve.wait_ge(small, at(h, SM, 6))
                        dve.wait_ge(o_done, at(h, C, 2))
                        dve.tensor_tensor(o[:, 1:TILES:2, ds(h[0] * (2 * D_V) + h[1] * D_V, D_V)], tp[:, 1, :].rearrange("p (b i) -> p b i", b=BATCH)[:, :, 0:D_V], QS[:], ALU.add).then_inc(o_stored, 1)

                over_heads(dve, prepare, border, levels)

            @block.gpsimd
            def _(pool):
                credit(pool, conv_picked, hp_copied, gm_done, em_done, eb_done, pow_done, *ot_done)
                pool.wait_ge(zeroed, 1)
                pool.wait_ge(conv_loaded, 32)
                four = lambda g, x, c: hp[g[1] % 2][:, x, c:TILES:2].rearrange("p (b o) -> p b o", o=1).to_broadcast([P, BATCH, P])
                all4 = lambda n: env.c(n).rearrange("p (o i) -> p o i", o=1).to_broadcast([P, BATCH, P])

                def pick_taps(g):
                    pool.wait_ge(conv_done, at(g, 2 * TAPS, 0))
                    pool.tensor_copy(conv_w[g[1] % 2][:].rearrange("p (o m) k -> p o m k", o=1), conv_all[:, ds(g[0] * 2 + g[1], 1), :, :]).then_inc(conv_picked, 1)

                def pick_head(g):
                    pool.wait_ge(o_stored, at(g, C, -2))
                    pool.tensor_copy(hp[g[1] % 2][:].rearrange("p (o k) t -> p o k t", o=1), par[:, ds(g[0] * 2 + g[1], 1), :, :]).then_inc(hp_copied, 1)
                    pool.tensor_copy(hv[g[1] % 2][:].rearrange("p (o t) d -> p o t d", o=1), v[:, ds(g[0] * 2 + g[1], 1), :, :]).then_inc(hp_copied, 1)

                def mask_g(g):
                    pool.wait_ge(hp_copied, at(g, 2, 2))
                    pool.wait_ge(p_done, at(g, C, 0))
                    for c in range(C):
                        pool.tensor_tensor(E[c][:], all4("after"), four(g, G_, c), ALU.mult).then_inc(gm_done, 1)

                def decays(g, c):
                    pool.wait_ge(exp_done, at(g, C, c + 1))
                    pool.tensor_tensor(E[c][:], E[c][:], all4("upto"), ALU.mult).then_inc(em_done, 1)
                    pool.wait_ge(em_done, at(g, C, c + 1))
                    pool.tensor_tensor(Eb[c][:], E[c][:], four(g, B_, c), ALU.mult).then_inc(eb_done, 1)

                def power(g, n):
                    m, c = divmod(n, 2)
                    pool.wait_ge(ssc_done, at(g, 4, n + 1))
                    pool.tensor_tensor(rn[:, m, 4 * c:4 * c + 4], ssc[:, m, 4 * c:4 * c + 4], half[:, 0:4], ALU.pow).then_inc(pow_done, 1)

                def joins(h, lv, c):
                    if lv == 0:
                        pool.wait_ge(a_done, at(h, C, c + 1))
                    elif lv == 2:
                        pool.wait_ge(t_done[c], at(h, NLEV, 1))
                    if lv >= 3:
                        pool.wait_ge(x_done[c], at(h, NLEV - 1, lv - 2))
                    pool.tensor_tensor(OT[c][lv % 2][:], AT[c][:], all4(f"level{lv}"), ALU.mult).then_inc(ot_done[c], 1)

                def prepare(g):
                    pick_taps(g)
                    pick_head(g)
                    mask_g(g)
                    for c in range(C):
                        decays(g, c)
                    for n in range(4):
                        power(g, n)

                def levels(h, g):
                    for lv in range(1, NLEV):
                        if g and lv == 1:
                            pick_taps(g)
                        if lv < NLEV - 1:
                            joins(h, lv + 1, 0)
                            joins(h, lv + 1, 1)
                        if g and lv == 1:
                            pick_head(g)
                            mask_g(g)
                        elif g and lv == 3:
                            decays(g, 0)
                        elif g and lv == 4:
                            power(g, 0)
                            power(g, 1)
                            decays(g, 1)
                        elif g and lv == 5:
                            power(g, 2)
                            power(g, 3)

                def border(h, g):
                    if g:
                        for lv in range(2):
                            joins(g, lv, 0)
                            joins(g, lv, 1)

                over_heads(pool, prepare, border, levels)


def delta_finish(nc, env, wo, norm_w, o, gate):
    with ExitStack() as ctx:
        sb, ps, sem = tools(nc, ctx, "df")
        wo_s, nw = sb("wo", [P, 3, DIM]), sb("nw", [P, D_V])
        sq, ms, msc, rstd = sb("sq", [P, TILES, D_N]), sb("ms", [P, TILES * D_H]), sb("msc", [P, TILES * D_H]), sb("rstd", [P, TILES * D_H])
        oT = sb("oT", [P, 2, 3, P])
        tp, po = ps("tp", [P, 2, 512]), ps("po", [P, 2, 512])
        loaded, gate_weighted, squared, summed, scaled, inverted, rstd_done, normed, gated, turned, copied, out_done, added = (
            sem(n) for n in ("loaded", "gate_weighted", "squared", "summed", "scaled", "inverted", "rstd_done", "normed", "gated", "turned", "copied", "out_done", "added"))
        by_head = lambda x: x.rearrange("p t (h d) -> p (t h) d", d=D_V)
        with nc.Block() as block:
            @block.sync
            def _(sp):
                sp.dma_start(nw[:], norm_w.rearrange("(o d) -> o d", o=1).to_broadcast([P, D_V])).then_inc(loaded, 16)
                sp.dma_start(wo_s[:], wo.rearrange("(m p) n -> p m n", p=P)).then_inc(loaded, 16)

            @block.scalar
            def _(act):
                for n in range(4):
                    act.activation(sq[:, 2 * n:2 * n + 2, :], o[:, 2 * n:2 * n + 2, :], ACT.Square).then_inc(squared, 1)
                act.wait_ge(inverted, 1)
                act.activation(rstd[:], msc[:], ACT.Sqrt).then_inc(rstd_done, 1)
                for t in range(TILES):
                    act.wait_ge(turned, t + 1)
                    if t >= 2:
                        act.wait_ge(out_done, t - 1)
                    act.copy(oT[:, t % 2, :, :], tp[:, t % 2, 0:D_N].rearrange("p (m n) -> p m n", n=P)).then_inc(copied, 1)

            @block.vector
            def _(dve):
                for n in range(4):
                    dve.wait_ge(squared, n + 1)
                    dve.tensor_reduce(ms[:, 2 * D_H * n:2 * D_H * (n + 1)], by_head(sq[:, 2 * n:2 * n + 2, :]), AX, ALU.add).then_inc(summed, 1)
                dve.wait_ge(summed, 4)
                dve.tensor_scalar(ms[:], ms[:], 1.0 / D_V, 1e-5, ALU.mult, ALU.add).then_inc(scaled, 1)
                dve.wait_ge(scaled, 1)
                dve.reciprocal(msc[:], ms[:]).then_inc(inverted, 1)
                dve.wait_ge(rstd_done, 1)
                for t in range(TILES):
                    r = rstd[:, D_H * t:D_H * t + D_H].rearrange("p (h o) -> p h o", o=1).to_broadcast([P, D_H, D_V])
                    oh = o[:, t, :].rearrange("p (h d) -> p h d", d=D_V)
                    dve.tensor_tensor(oh, oh, r, ALU.mult).then_inc(normed, 1)
                for t in range(TILES):
                    dve.wait_ge(out_done, t + 1)
                    dve.tensor_tensor(env.x[:, t, :], env.x[:, t, :], po[:, t % 2, 0:DIM], ALU.add).then_inc(added, 1)

            @block.gpsimd
            def _(pool):
                pool.wait_ge(loaded, 32)
                for t in range(TILES):
                    gh = gate[:, t, :].rearrange("p (h d) -> p h d", d=D_V)
                    pool.tensor_tensor(gh, gh, nw[:].rearrange("p (o d) -> p o d", o=1).to_broadcast([P, D_H, D_V]), ALU.mult).then_inc(gate_weighted, 1)
                for t in range(TILES):
                    pool.wait_ge(gate_weighted, t + 1)
                    pool.wait_ge(normed, t + 1)
                    pool.tensor_tensor(o[:, t, :], o[:, t, :], gate[:, t, :], ALU.mult).then_inc(gated, 1)

            @block.tensor
            def _(pe):
                pe.wait_ge(loaded, 32)
                for t in range(TILES + 1):
                    if t < TILES:
                        pe.wait_ge(gated, t + 1)
                        if t >= 2:
                            pe.wait_ge(copied, t - 1)
                        for m in range(3):
                            mm = pe.transpose(tp[:, t % 2, P * m:P * m + P], o[:, t, P * m:P * m + P], env.c("ident"))
                        mm.then_inc(turned, 1)
                    if t >= 1:
                        pe.wait_ge(copied, t)
                        if t >= 3:
                            pe.wait_ge(added, t - 2)
                        for m in range(3):
                            mm = pe.matmul(po[:, (t - 1) % 2, 0:DIM], oT[:, (t - 1) % 2, m, :], wo_s[:, m, :], start=(m == 0), stop=(m == 2))
                        mm.then_inc(out_done, 1)


def delta_attention(nc, env, a):
    with ExitStack() as ctx:
        v = ctx.enter_context(nc.sbuf_tensor("d_v", [P, D_H, TILES, D_V], F32))
        gate = ctx.enter_context(nc.sbuf_tensor("d_gate", [P, TILES, D_N], F32))
        par = ctx.enter_context(nc.sbuf_tensor("d_par", [P, D_H, 4, TILES], F32))
        o = ctx.enter_context(nc.sbuf_tensor("d_o", [P, TILES, D_N], F32))
        delta_prepare(nc, env, a, v, gate, par)
        delta_heads(nc, env, a["L1_attn_Wq"], a["L1_attn_Wk"], a["L1_attn_conv_wq"], a["L1_attn_conv_wk"], v, par, o)
        delta_finish(nc, env, a["L1_attn_Wo"], a["L1_attn_norm_w"], o, gate)


def latent_attention(nc, env, ctxT, wq, wkcq, wqrT, wkrT, wkv, woT):
    NH = 2
    ITER = X_H // NH
    CH = TOKENS // 512
    H3 = CTX // 2
    with ExitStack() as ctx:
        sb, ps, sem = tools(nc, ctx, "la")
        kraw, kprod, kcos, kvT, kvt = sb("kraw", [CTX, TOKENS]), sb("kprod", [CTX, BATCH, SEQ]), sb("kcos", [CTX, BATCH, SEQ]), sb("kvT", [P, TOKENS]), sb("kvt", [P, TILES, CTX])
        w_q, w_kcq, w_qr, w_kr, w_kv, w_o = (sb("wq", [X_K, NH, DIM]), sb("wkcq", [X_K, NH, X_CQ]), sb("wqr", [X_R, NH, X_CQ]),
                                             sb("wkr", [X_R, NH, CTX]), sb("wkv", [X_K, NH, CTX]), sb("wo", [X_K, NH, DIM]))
        wabs, mabs, mo = sb("wabs", [P, NH, KC, X_CQ]), sb("mabs", [X_HALF, NH, 2, CTX]), sb("mo", [P, DIM])
        prod, qrot = sb("prod", [X_HALF, 2, 4, 512]), sb("qrot", [X_HALF, 2, 2, 512])
        qc = sb("qc", [P, NH, TOKENS])
        nmax, total, rec = sb("nmax", [P, NH, TILES]), sb("total", [P, NH, TILES]), sb("rec", [P, NH, TILES])
        e, en, eT = sb("e", [P, 2, 2, SEQ]), sb("en", [P, 2, 2, SEQ]), sb("eT", [P, 2, 4, P])
        cxT = sb("cxT", [P, TOKENS])
        qb, qcp, sc, tr, cxp = ps("qb", [P, 2, 512]), ps("qcp", [P, 512]), ps("sc", [P, 2, 2, SEQ]), ps("tr", [P, 512]), ps("cxp", [P, 2, 512])
        flat = sc[:].rearrange("p a n l -> p a (n l)")
        loaded, k_done, k_rot, kt_done, kt_copied = (sem(n) for n in ("loaded", "k_done", "k_rot", "kt_done", "kt_copied"))
        w_loaded, absorbed, mo_done, qb_done, qc_done, sc_done, tr_done, cx_done, po_done = (
            sem(n) for n in ("w_loaded", "absorbed", "mo_done", "qb_done", "qc_done", "sc_done", "tr_done", "cx_done", "po_done"))
        absorbed_copied, qc_copied, exp_done, eT_copied = (sem(n) for n in ("absorbed_copied", "qc_copied", "exp_done", "eT_copied"))
        mo_copied, rope_done, max_done, rec_done, normed, cx_copied, added, rotated, padded = (
            sem(n) for n in ("mo_copied", "rope_done", "max_done", "rec_done", "normed", "cx_copied", "added", "rotated", "padded"))
        ORDER = ("w0 q00 w1 q01 l00 s0 s1 n0 n1 q10 l01 t0 s2 a0 t1 n2 s3 n3 q11 t2 l10 a1 t3 s4 a2 s5 l11 "
                 "n4 t4 a3 n5 s6 t5 s7 n6 a4 a5 t6 n7 o0 t7 a6 a7 o1 o2 o3").split()
        NT = NH * BATCH

        with nc.Block() as block:
            @block.sync
            def _(sp):
                sp.dma_start(kraw[:], ctxT).then_inc(loaded, 16)
                with sp.Fori(0, ITER) as i:
                    head = sp.snap(i * NH)
                    sp.wait_ge(mo_done, done(i, NH, 0))
                    for dst, src in ((w_q, wq.rearrange("(h p) n -> p h n", p=X_K)), (w_kcq, wkcq.rearrange("h p n -> p h n")),
                                     (w_qr, wqrT.rearrange("h p n -> p h n")), (w_kr, wkrT.rearrange("h p n -> p h n")),
                                     (w_kv, wkv.rearrange("h p n -> p h n")), (w_o, woT.rearrange("(h p) n -> p h n", p=X_K))):
                        sp.dma_start(dst[:], src[:, ds(head, NH), :]).then_inc(w_loaded, 16)

            @block.tensor
            def _(pe):
                credit(pe, absorbed, mo_done, qb_done, qc_done, sc_done, tr_done, cx_done, po_done)
                pe.wait_ge(k_rot, 1)
                for t in range(TILES):
                    mm = pe.transpose(qb[:, 0, CTX * t:CTX * t + CTX], kvT[0:CTX, P * t:P * t + P], env.c("ident")[0:CTX, 0:CTX])
                mm.then_inc(kt_done, 1)
                pe.wait_ge(kt_copied, 1)
                pe.wait_ge(padded, 1)
                with pe.Fori(0, ITER) as i:
                    pe.wait_ge(w_loaded, i * 96 + 96)

                    def absorb(a):
                        pe.wait_ge(exp_done, done(i, NT, 0))
                        for k in range(KC):
                            pe.matmul(flat[:, a, X_CQ * k:X_CQ * k + X_CQ], w_q[:, a, P * k:P * k + P], w_kcq[:, a, :], start=True, stop=True)
                        for n in range(2):
                            mm = pe.matmul(flat[0:X_HALF, a, 384 + CTX * n:384 + CTX * n + CTX], w_qr[:, a, X_HALF * n:X_HALF * n + X_HALF], w_kr[:, a, :], start=True, stop=True)
                        mm.then_inc(absorbed, 1)
                        pe.wait_ge(qc_copied, done(i, 2 * NH, 0))
                        pe.wait_ge(mo_copied, done(i, NH, a))
                        pe.matmul(qcp[CTX * a:CTX * a + CTX, 0:DIM], w_kv[:, a, :], w_o[:, a, :], start=True, stop=True).then_inc(mo_done, 1)

                    def queries(a, c):
                        pe.wait_ge(absorbed_copied, done(i, NH, a + 1))
                        pe.wait_ge(rope_done, done(i, 2 * NH, 2 * a + c))
                        pe.wait_ge(added, done(i, BATCH, 0))
                        for n in range(2):
                            for k in range(KC):
                                mm = pe.matmul(qb[0:X_HALF, n, :], wabs[:, a, k, X_HALF * n:X_HALF * n + X_HALF], env.xT[:, k, 512 * c:512 * c + 512], start=(k == 0), stop=(k == KC - 1))
                        mm.then_inc(qb_done, 1)

                    def latent_queries(a, c):
                        pe.wait_ge(rotated, done(i, 4 * NH, 4 * a + 2 * c + 2))
                        pe.wait_ge(qc_copied, done(i, 2 * NH, 2 * a + c))
                        pe.wait_ge(mo_copied, done(i, NH, NH))
                        for n in range(2):
                            mm = pe.matmul(qcp[0:CTX, :], mabs[:, a, n, :], qrot[:, c, n, :], start=(n == 0), stop=(n == 1))
                        mm.then_inc(qc_done, 1)

                    def scores(a, b):
                        u = BATCH * a + b
                        pe.wait_ge(qc_copied, done(i, 2 * NH, 2 * a + b // 2 + 1))
                        pe.wait_ge(exp_done, done(i, NT, u - 1))
                        if u < 2:
                            pe.wait_ge(absorbed_copied, done(i, NH, NH))
                        for n in range(2):
                            t = 2 * b + n
                            mm = pe.matmul(sc[:, u % 2, n, :], qc[:, a, P * t:P * t + P], kvT[:, SEQ * b:SEQ * b + SEQ], start=True, stop=True)
                        mm.then_inc(sc_done, 1)

                    def turn(a, b):
                        u = BATCH * a + b
                        pe.wait_ge(normed, done(i, NT, u + 1))
                        pe.wait_ge(eT_copied, done(i, NT, u))
                        for l in range(2):
                            for n in range(2):
                                mm = pe.transpose(tr[:, P * (2 * l + n):P * (2 * l + n) + P], en[:, u % 2, n, P * l:P * l + P], env.c("ident"))
                        mm.then_inc(tr_done, 1)

                    def attend(a, b):
                        u = BATCH * a + b
                        pe.wait_ge(eT_copied, done(i, NT, u + 1))
                        if u == 0:
                            pe.wait_ge(cx_copied, done(i, 2, 0))
                        for l in range(2):
                            mm = pe.matmul(cxp[CTX * a:CTX * a + CTX, b // 2, SEQ * (b % 2):SEQ * (b % 2) + SEQ], kvt[:, 2 * b + l, :],
                                           eT[:, u % 2, 2 * l:2 * l + 2, :].rearrange("p n q -> p (n q)"), start=(l == 0), stop=(l == 1))
                        mm.then_inc(cx_done, 1)

                    def outputs(b):
                        pe.wait_ge(rope_done, done(i, 2 * NH, 2 * NH))
                        pe.wait_ge(cx_copied, done(i, 2, b // 2 + 1))
                        pe.wait_ge(added, done(i, BATCH, b - 1))
                        for n in range(2):
                            t = 2 * b + n
                            mm = pe.matmul(qb[:, b % 2, DIM * n:DIM * n + DIM], cxT[:, P * t:P * t + P], mo[:], start=True, stop=True)
                        mm.then_inc(po_done, 1)

                    for kind, *at in ORDER:
                        at = [int(x) for x in at]
                        if kind == "q":
                            queries(*at)
                        elif kind == "l":
                            latent_queries(*at)
                        elif kind == "o":
                            outputs(*at)
                        elif kind == "w":
                            absorb(*at)
                        elif kind != "n":
                            {"s": scores, "t": turn, "a": attend}[kind](*divmod(at[0], BATCH))

            @block.scalar
            def _(act):
                credit(act, absorbed_copied, qc_copied, exp_done, eT_copied)
                with act.Fori(0, ITER) as i:
                    def copy_absorbed(a):
                        act.wait_ge(absorbed, done(i, NH, a + 1))
                        act.copy(wabs[:, a, :, :], flat[:, a, 0:2 * X_CQ].rearrange("p (k n) -> p k n", k=KC))
                        act.copy(mabs[:, a, :, :], flat[0:X_HALF, a, 2 * X_CQ:512].rearrange("p (k n) -> p k n", k=2)).then_inc(absorbed_copied, 1)

                    def copy_qc(a, c):
                        act.wait_ge(qc_done, done(i, 2 * NH, 2 * a + c + 1))
                        act.copy(qc[0:CTX, a, 512 * c:512 * c + 512], qcp[0:CTX, :]).then_inc(qc_copied, 1)

                    def exp(u):
                        a, b = divmod(u, BATCH)
                        act.wait_ge(max_done, done(i, NT, u + 1))
                        act.wait_ge(normed, done(i, NT, u - 1))
                        for n in range(2):
                            t = 2 * b + n
                            ins = act.activation(e[:, u % 2, n, :], sc[:, u % 2, n, :], ACT.Exp, bias=nmax[:, a, t:t + 1], accum_out=total[:, a, t:t + 1])
                        ins.then_inc(exp_done, 1)

                    def copy_eT(u):
                        act.wait_ge(tr_done, done(i, NT, u + 1))
                        act.wait_ge(cx_done, done(i, NT, u - 1))
                        act.copy(eT[:, u % 2, :, :], tr[:].rearrange("p (n l) -> p n l", n=4)).then_inc(eT_copied, 1)

                    for kind, *at in ORDER:
                        at = [int(x) for x in at]
                        if kind == "w":
                            copy_absorbed(*at)
                        elif kind == "l":
                            copy_qc(*at)
                        elif kind == "s":
                            exp(*at)
                        elif kind == "t":
                            copy_eT(*at)

            @block.vector
            def _(dve):
                credit(dve, mo_copied, rope_done, max_done, rec_done, normed, cx_copied, added)
                dve.memset(kvT[CTX:P, :], 0.0)
                dve.memset(qc[CTX:P, :, :], 0.0).then_inc(padded, 1)
                dve.wait_ge(loaded, 16)
                per_batch = lambda x: x.rearrange("p (o t) -> p o t", o=1).to_broadcast([H3, BATCH, SEQ])
                kr = kraw[:].rearrange("p (b t) -> p b t", t=SEQ)
                for lo in (0, H3):
                    dve.tensor_tensor(kcos[lo:lo + H3, :, :], kr[lo:lo + H3, :, :], per_batch(env.c("k_cos")[lo:lo + H3, :]), ALU.mult)
                    dve.tensor_tensor(kprod[H3 - lo:2 * H3 - lo, :, :], kr[lo:lo + H3, :, :], per_batch(env.c("k_sin")[lo:lo + H3, :]), ALU.mult).then_inc(k_done, 1)
                dve.wait_ge(k_done, 2)
                dve.tensor_tensor(kvT[0:CTX, :].rearrange("p (b t) -> p b t", t=SEQ), kcos[:], kprod[:], ALU.add).then_inc(k_rot, 1)
                dve.wait_ge(kt_done, 1)
                dve.tensor_copy(kvt[:], qb[:, 0, :].rearrange("p (t d) -> p t d", d=CTX)).then_inc(kt_copied, 1)
                with dve.Fori(0, ITER) as i:
                    def copy_mo(a):
                        dve.wait_ge(mo_done, done(i, NH, a + 1))
                        if a == 0:
                            dve.wait_ge(po_done, done(i, BATCH, 0))
                        dve.tensor_copy(mo[CTX * a:CTX * a + CTX, :], qcp[CTX * a:CTX * a + CTX, 0:DIM]).then_inc(mo_copied, 1)

                    def rope(a, c):
                        dve.wait_ge(qb_done, done(i, 2 * NH, 2 * a + c + 1))
                        dve.wait_ge(rotated, done(i, 4 * NH, 2 * (2 * a + c - 1)))
                        for j, (n, tab) in enumerate(((0, "x_cos0"), (1, "x_sin0"), (1, "x_cos1"), (0, "x_sin1"))):
                            ins = dve.tensor_tensor(prod[:, c, j, :], qb[0:X_HALF, n, :], env.c(tab)[0:X_HALF, :], ALU.mult)
                        ins.then_inc(rope_done, 1)

                    def maximum(u):
                        a, b = divmod(u, BATCH)
                        dve.wait_ge(sc_done, done(i, NT, u + 1))
                        dve.tensor_reduce(nmax[:, a, 2 * b:2 * b + 2], sc[:, u % 2, :, :], AX, ALU.max, negate=True).then_inc(max_done, 1)

                    def norm(u):
                        a, b = divmod(u, BATCH)
                        dve.wait_ge(exp_done, done(i, NT, u + 1))
                        dve.reciprocal(rec[:, a, 2 * b:2 * b + 2], total[:, a, 2 * b:2 * b + 2]).then_inc(rec_done, 1)
                        dve.wait_ge(rec_done, done(i, NT, u + 1))
                        dve.wait_ge(tr_done, done(i, NT, u - 1))
                        for n in range(2):
                            ins = dve.tensor_scalar(en[:, u % 2, n, :], e[:, u % 2, n, :], rec[:, a, 2 * b + n:2 * b + n + 1], None, ALU.mult)
                        ins.then_inc(normed, 1)

                    def copy_cx(g):
                        dve.wait_ge(cx_done, done(i, NT, BATCH + 2 * g + 2))
                        dve.tensor_copy(cxT[:, 512 * g:512 * g + 512], cxp[:, g, :]).then_inc(cx_copied, 1)

                    def add(b):
                        dve.wait_ge(po_done, done(i, BATCH, b + 1))
                        dve.tensor_tensor(env.x[:, 2 * b:2 * b + 2, :], env.x[:, 2 * b:2 * b + 2, :], qb[:, b % 2, :].rearrange("p (n c) -> p n c", n=2), ALU.add).then_inc(added, 1)

                    for kind, *at in ORDER:
                        at = [int(x) for x in at]
                        if kind == "w":
                            copy_mo(*at)
                        elif kind == "q":
                            rope(*at)
                        elif kind == "s":
                            maximum(*at)
                        elif kind == "n":
                            norm(*at)
                        elif kind == "a" and at[0] in (BATCH + 1, BATCH + 3):
                            copy_cx((at[0] - BATCH) // 2)
                        elif kind == "o":
                            add(*at)

            @block.gpsimd
            def _(pool):
                credit(pool, rotated)
                with pool.Fori(0, ITER) as i:
                    for a in range(NH):
                        for c in range(CH):
                            pool.wait_ge(rope_done, done(i, 2 * NH, 2 * a + c + 1))
                            pool.wait_ge(qc_done, done(i, 2 * NH, 2 * a + c - 1))
                            for n in range(2):
                                pool.tensor_tensor(qrot[:, c, n, :], prod[:, c, 2 * n, :], prod[:, c, 2 * n + 1, :], ALU.add).then_inc(rotated, 1)


def gate_projections(nc, env, sim, gates, w_table, wT):
    MIN, OFF = 2, 1e9
    with ExitStack() as ctx:
        sb, ps, sem = tools(nc, ctx, "fg")
        sim_s, sim2, thr_in, thr = sb("sim", [P, KC, F_E]), sb("sim2", [P, KC, F_E]), sb("thr_in", [P, F_E]), sb("thr", [P, F_E])
        xsq, xss = sb("xsq", [P, 2, DIM]), sb("xss", [P, TILES])
        norms, half, inv = sb("norms", [P, TILES + F_E]), sb("half", [P, TILES + F_E]), sb("inv", [P, TILES + F_E])
        lg, lpad, l8, lrep, fb = sb("lg", [P, TILES, F_E]), sb("lpad", [P, TILES, F_E + 8]), sb("l8", [P, TILES, 8]), sb("lrep", [P, TILES, F_E + 8]), sb("fb", [P, TILES, F_E])
        gated, on, cnt, idle, m, off = (sb("gated", [P, TILES, F_E]), sb("on", [P, TILES, F_E]), sb("cnt", [P, TILES]), sb("idle", [P, TILES]), sb("m", [P, TILES, F_E]), sb("off", [P, TILES, F_E]))
        mx, ex, tot, w = sb("mx", [P, TILES]), sb("ex", [P, TILES, F_E]), sb("tot", [P, TILES]), sb("w", [P, TILES, F_E])
        rp, tp = ps("rp", [P, TILES + 1, F_E]), ps("tp", [F_E, 2, 512])
        loaded, sim_sq, raw_done, sq_done, sig_done, pow_done, exp_done, turned, wT_copied, stored, norms_done, sub_done, w_done, step = (
            sem(n) for n in ("loaded", "sim_sq", "raw_done", "sq_done", "sig_done", "pow_done", "exp_done", "turned", "wT_copied", "stored", "norms_done", "sub_done", "w_done", "step"))
        with nc.Block() as block:
            @block.sync
            def _(sp):
                sp.dma_start(sim_s[:], sim.rearrange("(k p) n -> p k n", p=P)).then_inc(loaded, 16)
                sp.dma_start(thr_in[:], gates.rearrange("(o d) -> o d", o=1).to_broadcast([P, F_E])).then_inc(loaded, 16)
                sp.wait_ge(wT_copied, 2)
                sp.dma_start(w_table, wT[:]).then_inc(stored, 16)
                sp.wait_ge(stored, 16)

            @block.tensor
            def _(pe):
                pe.wait_ge(loaded, 32)
                for t in range(TILES):
                    for k in range(KC):
                        pe.matmul(rp[:, t, :], env.xT[:, k, P * t:P * t + P], sim_s[:, k, :], start=(k == 0), stop=(k == KC - 1))
                pe.wait_ge(sim_sq, 1)
                for k in range(KC):
                    mm = pe.matmul(rp[:, TILES, :], env.c("ones"), sim2[:, k, :], start=(k == 0), stop=(k == KC - 1))
                mm.then_inc(raw_done, 1)
                pe.wait_ge(w_done, 1)
                for t in range(TILES):
                    mm = pe.transpose(tp[:, t // 4, P * (t % 4):P * (t % 4) + P], w[:, t, :], env.c("ident"))
                    if t % 4 == 3:
                        mm.then_inc(turned, 1)

            @block.scalar
            def _(act):
                act.wait_ge(loaded, 32)
                act.activation(thr[:], thr_in[:], ACT.Sigmoid).then_inc(sig_done, 1)
                for t in range(TILES):
                    if t >= 2:
                        act.wait_ge(sq_done, t - 1)
                    act.activation(xsq[:, t % 2, :], env.x[:, t, :], ACT.Square, accum_out=xss[:, t:t + 1]).then_inc(sq_done, 1)
                act.wait_ge(sub_done, 1)
                act.activation(ex[:], ex[:], ACT.Exp).then_inc(exp_done, 1)

            @block.gpsimd
            def _(pool):
                pool.wait_ge(norms_done, 1)
                pool.tensor_tensor(inv[:], norms[:], half[:], ALU.pow).then_inc(pow_done, 1)

            @block.vector
            def _(dve):
                count = [0]

                def chain(ins):
                    count[0] += 1
                    ins.then_inc(step, 1)
                    dve.wait_ge(step, count[0])

                experts = lambda a: a.rearrange("p (t o) -> p t o", o=1).to_broadcast([P, TILES, F_E])
                rows = lambda a: a.rearrange("p (o e) -> p o e", o=1).to_broadcast([P, TILES, F_E])
                dve.memset(half[:], -0.5)
                dve.memset(lpad[:], NEG)
                dve.wait_ge(loaded, 32)
                dve.tensor_tensor(sim2[:], sim_s[:], sim_s[:], ALU.mult).then_inc(sim_sq, 1)
                dve.wait_ge(raw_done, 1)
                dve.wait_ge(sq_done, TILES)
                dve.tensor_scalar(norms[:, 0:TILES], xss[:], 1e-24, None, ALU.max)
                chain(dve.tensor_scalar(norms[:, TILES:], rp[:, TILES, :], 1e-24, None, ALU.max))
                dve.sem_inc(norms_done, 1)
                dve.wait_ge(pow_done, 1)
                chain(dve.tensor_tensor(lg[:], rp[:, 0:TILES, :], experts(inv[:, 0:TILES]), ALU.mult))
                chain(dve.tensor_tensor(lg[:], lg[:], rows(inv[:, TILES:]), ALU.mult))
                dve.wait_ge(sig_done, 1)
                chain(dve.tensor_tensor(lpad[:, :, 0:F_E], lg[:], rows(thr[:]), ALU.subtract))
                l = lpad[:, :, 0:F_E]
                for t in range(TILES):
                    chain(dve.max(l8[:, t, :], lpad[:, t, :]))
                chain(dve.memset(l8[:, :, MIN:8], NEG))
                for t in range(TILES):
                    chain(dve.match_replace(lrep[:, t, :], l8[:, t, :], lpad[:, t, :], NEG))
                chain(dve.tensor_tensor(fb[:], lrep[:, :, 0:F_E], l, ALU.not_equal))
                chain(dve.tensor_scalar(gated[:], l, 0.0, None, ALU.max))
                chain(dve.tensor_scalar(on[:], gated[:], 0.0, None, ALU.is_gt))
                chain(dve.tensor_reduce(cnt[:], on[:], AX, ALU.add))
                chain(dve.tensor_scalar(idle[:], cnt[:], 0.0, None, ALU.is_equal))
                chain(dve.tensor_tensor(m[:], fb[:], experts(idle[:]), ALU.mult))
                chain(dve.tensor_tensor(m[:], m[:], on[:], ALU.max))
                chain(dve.tensor_scalar(off[:], m[:], OFF, -OFF, ALU.mult, ALU.add))
                chain(dve.tensor_tensor(gated[:], gated[:], m[:], ALU.mult))
                chain(dve.tensor_tensor(gated[:], gated[:], off[:], ALU.add))
                chain(dve.tensor_reduce(mx[:], gated[:], AX, ALU.max))
                chain(dve.tensor_tensor(ex[:], gated[:], experts(mx[:]), ALU.subtract))
                dve.sem_inc(sub_done, 1)
                dve.wait_ge(exp_done, 1)
                chain(dve.tensor_reduce(tot[:], ex[:], AX, ALU.add))
                chain(dve.reciprocal(tot[:], tot[:]))
                chain(dve.tensor_tensor(w[:], ex[:], experts(tot[:]), ALU.mult))
                chain(dve.tensor_tensor(w[:], w[:], m[:], ALU.mult))
                dve.sem_inc(w_done, 1)
                for n in range(2):
                    dve.wait_ge(turned, n + 1)
                    dve.tensor_copy(wT[:, 512 * n:512 * n + 512], tp[:, n, :]).then_inc(wT_copied, 1)


def mixed_attention(nc, env, w_table, wq, wk, wv, wo):
    SCALE = float(F_H) ** -0.5
    with ExitStack() as ctx:
        sb, ps, sem = tools(nc, ctx, "fa")
        wb = sb("wb", [P, F_E, TOKENS])
        qkv, vt, aT = sb("qkv", [P, 3, TOKENS]), sb("vt", [P, TILES, F_H]), sb("aT", [P, TOKENS])
        wb_loaded = [sem(f"wb_loaded{n}") for n in range(3)]
        with ExitStack() as inner:
            sb, ps, sem = tools(nc, inner, "fp")
            w_s, xe = sb("w", [P, 2, 3, KC, F_H]), sb("xe", [P, 2, KC, TOKENS])
            acc = ps("acc", [P, 3, 2, 512])
            w_loaded, scaled, projected, copied = [sem("w_loaded0"), sem("w_loaded1")], sem("scaled"), sem("projected"), sem("copied")
            PAIRS = F_E // 2
            with nc.Block() as block:
                @block.gpsimd
                def _(pool):
                    for first, count, s in ((0, 1, 0), (1, 1, 0), (2, 2, 1), (4, 4, 2), (8, 4, 2), (12, 4, 2)):
                        pool.dma_start(wb[:, first:first + count, :], w_table[first:first + count, :].rearrange("(o e) t -> o e t", o=1).to_broadcast([P, count, TOKENS])).then_inc(wb_loaded[s], 16)
                    pool.wait_ge(wb_loaded[2], 48)

                @block.sync
                def _(sp):
                    with sp.Fori(0, PAIRS) as i:
                        pair = sp.snap(i * 2)
                        for s in range(2):
                            sp.wait_ge(projected, done(i, 2, s - 1))
                            for m, w in enumerate((wq, wk, wv)):
                                sp.dma_start(w_s[:, s, m, :, :], w.rearrange("e (k p) h -> p e k h", p=P)[:, ds(pair + s, 1), :, :].rearrange("p e k h -> p (e k) h")).then_inc(w_loaded[s], 16)

                @block.vector
                def _(dve):
                    credit(dve, scaled)

                    def scale_pair(i):
                        for s in range(2):
                            dve.wait_ge(projected, done(i, 2, s - 1))
                            dve.tensor_tensor(xe[:, s, :, :], env.xT[:], wb[:, ds(i * 2 + s, 1), :].to_broadcast([P, KC, TOKENS]), ALU.mult).then_inc(scaled, 1)

                    dve.wait_ge(wb_loaded[0], 32)
                    scale_pair(0)
                    dve.wait_ge(wb_loaded[1], 16)
                    scale_pair(1)
                    dve.wait_ge(wb_loaded[2], 48)
                    with dve.Fori(2, PAIRS) as i:
                        scale_pair(i)
                    for n in range(6):
                        dve.wait_ge(projected, CREDIT + F_E)
                        dve.tensor_copy(qkv[:, n // 2, 512 * (n % 2):512 * (n % 2) + 512], acc[:, n // 2, n % 2, :]).then_inc(copied, 1)

                @block.tensor
                def _(pe):
                    credit(pe, projected)

                    def expert(i, s, first, last):
                        pe.wait_ge(w_loaded[s], i * 48 + 48)
                        pe.wait_ge(scaled, done(i, 2, s + 1))
                        for m in range(3):
                            for k in range(KC):
                                for c in range(2):
                                    mm = pe.matmul(acc[:, m, c, :], w_s[:, s, m, k, :], xe[:, s, k, 512 * c:512 * c + 512], start=first and k == 0, stop=last and k == KC - 1)
                        mm.then_inc(projected, 1)

                    expert(0, 0, True, False)
                    expert(0, 1, False, False)
                    with pe.Fori(1, PAIRS - 1) as i:
                        expert(i, 0, False, False)
                        expert(i, 1, False, False)
                    expert(PAIRS - 1, 0, False, False)
                    expert(PAIRS - 1, 1, False, True)
        with ExitStack() as inner:
            sb, ps, sem = tools(nc, inner, "fc")
            sm, mx, e, tot, rec, pn, pT = (sb("sm", [P, 2, 2, SEQ]), sb("mx", [P, TILES]), sb("e", [P, 2, 2, SEQ]), sb("tot", [P, TILES]),
                                           sb("rec", [P, TILES]), sb("pn", [P, 2, 2, SEQ]), sb("pT", [P, 2, 4, P]))
            nmx = sb("nmx", [P, TILES])
            tv, sc, tr, ap_ = ps("tv", [P, 2, 512]), ps("sc", [P, 2, 2, SEQ]), ps("tr", [P, 2, 512]), ps("ap", [P, 2, 512])
            v_turned, v_copied, sc_done, masked, max_done, scaled, exp_done, rec_done, normed, turned, copied, a_done, a_copied = (
                sem(n) for n in ("v_turned", "v_copied", "sc_done", "masked", "max_done", "scaled", "exp_done", "rec_done", "normed", "turned", "copied", "a_done", "a_copied"))
            q, k, v = qkv[:, 0, :], qkv[:, 1, :], qkv[:, 2, :]
            with nc.Block() as block:
                @block.tensor
                def _(pe):
                    for n in range(2):
                        for j in range(4):
                            t = 4 * n + j
                            mm = pe.transpose(tv[:, n, P * j:P * j + P], v[:, P * t:P * t + P], env.c("ident"))
                        mm.then_inc(v_turned, 1)
                    for u in range(BATCH + 2):
                        if u < BATCH:
                            if u >= 2:
                                pe.wait_ge(masked, 2 * (u - 1))
                            for n in range(2):
                                t = 2 * u + n
                                mm = pe.matmul(sc[:, u % 2, n, :], q[:, P * t:P * t + P], k[:, SEQ * u:SEQ * u + SEQ], start=True, stop=True)
                            mm.then_inc(sc_done, 1)
                        if 1 <= u <= BATCH:
                            w = u - 1
                            pe.wait_ge(normed, 2 * w + 2)
                            if w >= 2:
                                pe.wait_ge(copied, w - 1)
                            for n in range(2):
                                for l in range(2):
                                    mm = pe.transpose(tr[:, w % 2, P * (2 * l + n):P * (2 * l + n) + P], pn[:, w % 2, n, P * l:P * l + P], env.c("ident"))
                            mm.then_inc(turned, 1)
                        if u >= 2:
                            w = u - 2
                            pe.wait_ge(copied, w + 1)
                            pe.wait_ge(v_copied, 2)
                            if w >= 2:
                                pe.wait_ge(a_copied, w - 1)
                            for l in range(2):
                                mm = pe.matmul(ap_[:, w % 2, 0:SEQ], vt[:, 2 * w + l, :], pT[:, w % 2, 2 * l:2 * l + 2, :].rearrange("p n q -> p (n q)"), start=(l == 0), stop=(l == 1))
                            mm.then_inc(a_done, 1)

                @block.scalar
                def _(act):
                    for u in range(BATCH + 1):
                        if u < BATCH:
                            act.wait_ge(scaled, u + 1)
                            if u >= 2:
                                act.wait_ge(normed, 2 * (u - 1))
                            for n in range(2):
                                t = 2 * u + n
                                ins = act.activation(e[:, u % 2, n, :], sm[:, u % 2, n, :], ACT.Exp, bias=nmx[:, t:t + 1], scale=SCALE, accum_out=tot[:, t:t + 1])
                            ins.then_inc(exp_done, 1)
                        if u >= 1:
                            w = u - 1
                            act.wait_ge(turned, w + 1)
                            if w >= 2:
                                act.wait_ge(a_done, w - 1)
                            act.copy(pT[:, w % 2, :, :], tr[:, w % 2, :].rearrange("p (n l) -> p n l", n=4)).then_inc(copied, 1)

                @block.vector
                def _(dve):
                    for n in range(2):
                        dve.wait_ge(v_turned, n + 1)
                        dve.tensor_copy(vt[:, 4 * n:4 * n + 4, :], tv[:, n, :].rearrange("p (j h) -> p j h", j=4)).then_inc(v_copied, 1)
                    mask = env.c("f_mask")
                    for u in range(BATCH + 1):
                        if u < BATCH:
                            dve.wait_ge(sc_done, u + 1)
                            if u >= 2:
                                dve.wait_ge(exp_done, u - 1)
                            for n in range(2):
                                for l in range(2):
                                    src = mask[:, P:SEQ] if l == n else mask[:, 0:P]
                                    if n == 0 and l == 1:
                                        ins = dve.tensor_scalar(sm[:, u % 2, n, P:SEQ], sc[:, u % 2, n, P:SEQ], 0.0, NEG, ALU.mult, ALU.add)
                                    else:
                                        ins = dve.tensor_tensor(sm[:, u % 2, n, P * l:P * l + P], sc[:, u % 2, n, P * l:P * l + P], src, ALU.add)
                                ins.then_inc(masked, 1)
                            dve.wait_ge(masked, 2 * u + 2)
                            dve.tensor_reduce(mx[:, 2 * u:2 * u + 2], sm[:, u % 2, :, :], AX, ALU.max, negate=True).then_inc(max_done, 1)
                            dve.wait_ge(max_done, u + 1)
                            dve.tensor_scalar(nmx[:, 2 * u:2 * u + 2], mx[:, 2 * u:2 * u + 2], SCALE, None, ALU.mult).then_inc(scaled, 1)
                        if u >= 1:
                            w = u - 1
                            dve.wait_ge(exp_done, w + 1)
                            dve.reciprocal(rec[:, 2 * w:2 * w + 2], tot[:, 2 * w:2 * w + 2]).then_inc(rec_done, 1)
                            dve.wait_ge(rec_done, w + 1)
                            if w >= 2:
                                dve.wait_ge(turned, w - 1)
                            for n in range(2):
                                t = 2 * w + n
                                dve.tensor_scalar(pn[:, w % 2, n, :], e[:, w % 2, n, :], rec[:, t:t + 1], None, ALU.mult).then_inc(normed, 1)
                    for u in range(BATCH):
                        dve.wait_ge(a_done, u + 1)
                        dve.tensor_copy(aT[:, SEQ * u:SEQ * u + SEQ], ap_[:, u % 2, 0:SEQ]).then_inc(a_copied, 1)
        with ExitStack() as inner:
            sb, ps, sem = tools(nc, inner, "fo")
            w_s, ae = sb("w", [P, 2, DIM]), sb("ae", [P, 2, TOKENS])
            acc = ps("acc", [P, TILES, 512])
            w_loaded, scaled, out_done, added = [sem("w_loaded0"), sem("w_loaded1")], sem("scaled"), sem("out_done"), sem("added")
            PAIRS = F_E // 2
            with nc.Block() as block:
                @block.sync
                def _(sp):
                    with sp.Fori(0, PAIRS) as i:
                        pair = sp.snap(i * 2)
                        for s in range(2):
                            sp.wait_ge(out_done, done(i, 2, s - 1))
                            sp.dma_start(w_s[:, s, :].rearrange("p (o n) -> p o n", o=1), wo.rearrange("e p n -> p e n")[:, ds(pair + s, 1), :]).then_inc(w_loaded[s], 16)

                @block.vector
                def _(dve):
                    credit(dve, scaled)
                    with dve.Fori(0, PAIRS) as i:
                        for s in range(2):
                            dve.wait_ge(out_done, done(i, 2, s - 1))
                            dve.tensor_tensor(ae[:, s, :].rearrange("p (o t) -> p o t", o=1), aT[:].rearrange("p (o t) -> p o t", o=1), wb[:, ds(i * 2 + s, 1), :], ALU.mult).then_inc(scaled, 1)
                    dve.wait_ge(out_done, CREDIT + F_E)
                    for t in range(TILES):
                        dve.tensor_tensor(env.x[:, t, :], env.x[:, t, :], acc[:, t, 0:DIM], ALU.add).then_inc(added, 1)

                @block.tensor
                def _(pe):
                    credit(pe, out_done)

                    def expert(i, s, first, last):
                        pe.wait_ge(w_loaded[s], i * 16 + 16)
                        pe.wait_ge(scaled, done(i, 2, s + 1))
                        for t in range(TILES):
                            mm = pe.matmul(acc[:, t, 0:DIM], ae[:, s, P * t:P * t + P], w_s[:, s, :], start=first, stop=last)
                        mm.then_inc(out_done, 1)

                    expert(0, 0, True, False)
                    expert(0, 1, False, False)
                    with pe.Fori(1, PAIRS - 1) as i:
                        expert(i, 0, False, False)
                        expert(i, 1, False, False)
                    expert(PAIRS - 1, 0, False, False)
                    expert(PAIRS - 1, 1, False, True)


def mixture_attention(nc, env, a, w_table):
    with ExitStack() as ctx:
        wT = ctx.enter_context(nc.sbuf_tensor("f_wT", [F_E, TOKENS], F32))
        gate_projections(nc, env, a["L1_ffn_sim_matrix"], a["L1_ffn_gates"], w_table, wT)
        mixed_attention(nc, env, w_table, a["L1_ffn_q_proj"], a["L1_ffn_k_proj"], a["L1_ffn_v_proj"], a["L1_ffn_o_proj"])


def build(nc, a, const_at, out):
    slot_x = nc.dram_tensor("slot_x", [1 + M_SLOTS, DIM], F32).ap()
    out_rows = nc.dram_tensor("out_rows", [1 + M_SLOTS, DIM], F32).ap()
    w_table = nc.dram_tensor("w_table", [F_E, TOKENS], F32).ap()
    with ExitStack() as ctx:
        env = Env(nc, ctx, const_at)
        load_inputs(nc, env, a["x"], a["const"])
        window_attention(nc, env, a["L0_attn_q_kernel"], a["L0_attn_k_kernel"], a["L0_attn_v_kernel"], a["L0_attn_out_kernel"])
        normalize(nc, env, "n0")
        softmax_cross(nc, env, a["ctxT"], a["L0_xattn_W_kT"], a["L0_xattn_b_k"], a["L0_xattn_ln_gamma"], a["L0_xattn_ln_beta"])
        normalize(nc, env, "n1")
        routed_experts(nc, env, a, slot_x, out_rows)
        normalize(nc, env, "n2")
        delta_attention(nc, env, a)
        normalize(nc, env, "n3")
        latent_attention(nc, env, a["ctxT"], a["L1_xattn_Wq"], a["L1_xattn_w_kc_q"], a["L1_xattn_W_qrT"], a["L1_xattn_W_krT"], a["L1_xattn_w_kc_kv"], a["L1_xattn_WoT"])
        normalize(nc, env, "n4")
        mixture_attention(nc, env, a, w_table)
        normalize(nc, env, "n5", out)


def kernel(**inputs):
    import concourse.bacc as bacc
    from concourse.bass_utils import run_bass_kernel_spmd

    given = {k: np.asarray(v) for k, v in inputs.items()}
    turned = {
        "ctxT": given.pop("ctx_512").reshape(TOKENS, CTX).T,
        "L0_xattn_W_kT": given.pop("L0_xattn_W_k").T,
        "L1_xattn_W_qrT": given.pop("L1_xattn_W_qr").transpose(0, 2, 1),
        "L1_xattn_W_krT": given.pop("L1_xattn_W_kr").transpose(0, 2, 1),
        "L1_xattn_WoT": given.pop("L1_xattn_Wo").T,
    }
    const, const_at = constants()
    arrays = {k: np.ascontiguousarray(v) for k, v in {**given, **turned, "const": const}.items()}
    nc = bacc.Bacc("TRN2", target_bir_lowering=False, num_devices=1)
    a = {k: nc.dram_tensor(f"in_{k}", v.shape, mybir.dt.from_np(v.dtype), kind="ExternalInput").ap() for k, v in arrays.items()}
    out = nc.dram_tensor("out_x", [BATCH, SEQ, DIM], F32, kind="ExternalOutput").ap()
    build(nc, a, const_at, out)
    r = run_bass_kernel_spmd(nc, [{f"in_{k}": v for k, v in arrays.items()}], core_ids=[0])
    return r.results[0]["out_x"]
```
